# Optimizing a Trainium2 kernel written in Bass

```python
import numpy as np
import jax
import jax.numpy as jnp

def _softmax(x, axis=-1):
    return jax.nn.softmax(x, axis=axis)

def _gelu(x):
    return jax.nn.gelu(x, approximate=True)

def _silu(x):
    return jax.nn.silu(x)

def _sigmoid(x):
    return jax.nn.sigmoid(x)

def _layernorm(x, axis=-1, eps=1e-05):
    m = jnp.mean(x, axis=axis, keepdims=True)
    v = jnp.var(x, axis=axis, keepdims=True)
    return (x - m) / jnp.sqrt(v + eps)

def _scatter_add(tgt, idx, src, axis=0):
    return tgt.at[idx].add(src)

def _segment_sum(src, seg, n):
    return jax.ops.segment_sum(src, seg, n)
kernel_name = 'mk_hybrid_d1_jaxref_r8_0c2336'

def setup_inputs(seed: int=0):
    np.random.seed(seed)
    _w = jnp.asarray

    def _L0_attn_a_setup():
        import jax, jax.numpy as jnp
        import numpy as np
        B, T, HID = (1, 128, 256)
        H, DK, DV, M, KW = (16, 128, 128, 128, 4)
        SCALE = DK ** (-0.5)
        EPS = 1e-05

        def short_conv(x, w):
            K = w.shape[1]
            xp = jnp.pad(x, ((0, 0), (K - 1, 0), (0, 0)))
            t = x.shape[1]
            y = sum((xp[:, i:i + t] * w[:, i] for i in range(K)))
            return jax.nn.silu(y)

        def l2norm(x):
            return x * jax.lax.rsqrt(jnp.sum(x * x, axis=-1, keepdims=True) + 1e-06)

        def gsa2_scan(q, k, v, w, g, beta):
            b = q.shape[0]
            tm = lambda x: jnp.moveaxis(x, 1, 0)
            Sk0 = jnp.zeros((b, H, DK, M), q.dtype)
            Sv0 = jnp.zeros((b, H, M, DV), q.dtype)

            def step(carry, xs):
                Sk, Sv = carry
                q_t, k_t, v_t, w_t, g_t, b_t = xs
                gt = jnp.exp(g_t)
                bw = b_t[:, :, None] * w_t
                Sk = Sk * gt[:, :, None, :] + k_t[..., :, None] * bw[:, :, None, :]
                Sv = Sv * gt[..., None] + bw[..., None] * v_t[:, :, None, :]
                s = jnp.einsum('bhd,bhdm->bhm', q_t, Sk) * SCALE
                a = jax.nn.softmax(s, axis=-1)
                o_t = jnp.einsum('bhm,bhmd->bhd', a, Sv)
                return ((Sk, Sv), o_t)
            (_, _), o = jax.lax.scan(step, (Sk0, Sv0), (tm(q), tm(k), tm(v), tm(w), tm(g), tm(beta)))
            return jnp.moveaxis(o, 0, 1)
        key = jax.random.key(seed)
        ks = jax.random.split(key, 16)
        s = 0.02
        return {'hidden_states': jax.random.normal(ks[0], (B, T, HID), jnp.float32), 'Wq': jax.random.normal(ks[1], (HID, H * DK), jnp.float32) * s, 'Wk': jax.random.normal(ks[2], (HID, H * DK), jnp.float32) * s, 'Wv': jax.random.normal(ks[3], (HID, H * DV), jnp.float32) * s, 'Ww': jax.random.normal(ks[4], (HID, H * M), jnp.float32) * s, 'cq': jax.random.normal(ks[5], (H * DK, KW), jnp.float32) * 0.2, 'ck': jax.random.normal(ks[6], (H * DK, KW), jnp.float32) * 0.2, 'cv': jax.random.normal(ks[7], (H * DV, KW), jnp.float32) * 0.2, 'Wf1': jax.random.normal(ks[8], (HID, DV), jnp.float32) * s, 'Wf2': jax.random.normal(ks[9], (DV, H * M), jnp.float32) * s, 'Wb': jax.random.normal(ks[10], (HID, H), jnp.float32) * s, 'Wg1': jax.random.normal(ks[11], (HID, DV), jnp.float32) * s, 'Wg2': jax.random.normal(ks[12], (DV, H * DV), jnp.float32) * s, 'bg2': jnp.zeros((H * DV,), jnp.float32), 'norm_w': jnp.ones((DV,), jnp.float32), 'Wo': jax.random.normal(ks[13], (H * DV, HID), jnp.float32) * s}
    _L0_attn_a_in = _L0_attn_a_setup()

    def _L0_attn_b_setup():
        import jax, jax.numpy as jnp
        import numpy as np
        EMBED_DIM = 256
        NUM_HEADS = 16
        HEAD_DIM = EMBED_DIM // NUM_HEADS
        BASE = 10000.0

        def rotate_half(x):
            half = x.shape[-1] // 2
            x1, x2 = (x[..., :half], x[..., half:])
            return jnp.concatenate([-x2, x1], axis=-1)

        def apply_rope(x, base=BASE):
            S, Dh = (x.shape[-2], x.shape[-1])
            inv_freq = 1.0 / base ** (jnp.arange(0, Dh, 2, dtype=jnp.float32) / Dh)
            t = jnp.arange(S, dtype=jnp.float32)
            freqs = jnp.einsum('i,j->ij', t, inv_freq)
            emb = jnp.concatenate([freqs, freqs], axis=-1)
            return x * jnp.cos(emb) + rotate_half(x) * jnp.sin(emb)
        key = jax.random.key(seed)
        ks = jax.random.split(key, 9)
        B, S, D = (2, 256, EMBED_DIM)
        xavier = lambda k, shape: jax.random.uniform(k, shape, jnp.float32, -1.0, 1.0) * float(np.sqrt(6.0 / (shape[0] + shape[1])))
        return {'x': jax.random.normal(ks[0], (B, S, D), jnp.float32), 'q_w': xavier(ks[1], (D, D)), 'k_w': xavier(ks[2], (D, D)), 'v_w': xavier(ks[3], (D, D)), 'q_b': jnp.zeros((D,), jnp.float32), 'k_b': jnp.zeros((D,), jnp.float32), 'v_b': jnp.zeros((D,), jnp.float32), 'out_w': xavier(ks[4], (D, D)), 'out_b': jnp.zeros((D,), jnp.float32)}
    _L0_attn_b_in = _L0_attn_b_setup()

    def _L0_ffn_setup():
        import jax, jax.numpy as jnp
        import numpy as np
        import math
        B, S, D = (2, 256, 256)
        H, HD = (16, 128)
        E, I = (4, 256)
        TOP_K = 2
        ROPE_THETA = 10000.0

        def _layernorm(x, w, b):
            mu = jnp.mean(x, axis=-1, keepdims=True)
            var = jnp.mean(jnp.square(x - mu), axis=-1, keepdims=True)
            return (x - mu) * jax.lax.rsqrt(var + 1e-05) * w + b

        def _rotate_half(x):
            x1, x2 = jnp.split(x, 2, axis=-1)
            return jnp.concatenate((-x2, x1), axis=-1)

        def _attention(h, wq, bq, wk, bk, wv, bv, wo, bo):
            b, s, _ = h.shape
            q = (h @ wq + bq).reshape(b, s, H, HD).transpose(0, 2, 1, 3)
            k = (h @ wk + bk).reshape(b, s, H, HD).transpose(0, 2, 1, 3)
            v = (h @ wv + bv).reshape(b, s, H, HD).transpose(0, 2, 1, 3)
            inv_freq = 1.0 / ROPE_THETA ** (jnp.arange(0, HD, 2, dtype=jnp.float32) / HD)
            freqs = jnp.arange(s, dtype=jnp.float32)[:, None] * inv_freq[None, :]
            emb = jnp.concatenate((freqs, freqs), axis=-1)
            cos = jnp.cos(emb)[None, None]
            sin = jnp.sin(emb)[None, None]
            q = q * cos + _rotate_half(q) * sin
            k = k * cos + _rotate_half(k) * sin
            scores = jnp.einsum('bhqd,bhkd->bhqk', q, k) / math.sqrt(HD)
            causal = jnp.tril(jnp.ones((s, s), bool))
            scores = jnp.where(causal[None, None], scores, jnp.finfo(jnp.float32).min)
            probs = jax.nn.softmax(scores.astype(jnp.float32), axis=-1).astype(q.dtype)
            out = jnp.einsum('bhqk,bhkd->bhqd', probs, v)
            out = out.transpose(0, 2, 1, 3).reshape(b, s, H * HD)
            return out @ wo + bo

        def _moe(h, w_gate, we1, be1, we2, be2):
            b, s, d = h.shape
            x = h.reshape(-1, d)
            t = x.shape[0]
            raw = jax.nn.softmax(x @ w_gate, axis=-1)
            top_vals, top_idx = jax.lax.top_k(raw, TOP_K)
            w = jax.nn.softmax(top_vals, axis=-1)
            comb = jnp.zeros((t, E), x.dtype).at[jnp.arange(t)[:, None], top_idx].add(w)
            hmid = jax.nn.gelu(jnp.einsum('td,edi->tei', x, we1) + be1[None], approximate=False)
            eout = jnp.einsum('tei,eid->ted', hmid, we2) + be2[None]
            out = jnp.einsum('te,ted->td', comb, eout)
            return out.reshape(b, s, d)
        key = jax.random.key(seed)
        ks = jax.random.split(key, 20)
        s = 0.02
        p = {'hidden_states': jax.random.normal(ks[0], (B, S, D), jnp.float32), 'wq': jax.random.normal(ks[1], (D, H * HD), jnp.float32) * s, 'bq': jnp.zeros((H * HD,), jnp.float32), 'wk': jax.random.normal(ks[2], (D, H * HD), jnp.float32) * s, 'bk': jnp.zeros((H * HD,), jnp.float32), 'wv': jax.random.normal(ks[3], (D, H * HD), jnp.float32) * s, 'bv': jnp.zeros((H * HD,), jnp.float32), 'wo': jax.random.normal(ks[4], (H * HD, D), jnp.float32) * s, 'bo': jnp.zeros((D,), jnp.float32), 'ln1_w': jnp.ones((D,), jnp.float32), 'ln1_b': jnp.zeros((D,), jnp.float32), 'ln2_w': jnp.ones((D,), jnp.float32), 'ln2_b': jnp.zeros((D,), jnp.float32), 'w_gate': jax.random.normal(ks[5], (D, E), jnp.float32) * s, 'we1': jax.random.normal(ks[6], (E, D, I), jnp.float32) * s, 'be1': jnp.zeros((E, I), jnp.float32), 'we2': jax.random.normal(ks[7], (E, I, D), jnp.float32) * s, 'be2': jnp.zeros((E, D), jnp.float32)}
        return p
    _L0_ffn_in = _L0_ffn_setup()
    _d = {'L0_attn_a_hidden_states': _L0_attn_a_in['hidden_states'], 'L0_attn_a_Wq': _L0_attn_a_in['Wq'], 'L0_attn_a_Wk': _L0_attn_a_in['Wk'], 'L0_attn_a_Wv': _L0_attn_a_in['Wv'], 'L0_attn_a_Ww': _L0_attn_a_in['Ww'], 'L0_attn_a_cq': _L0_attn_a_in['cq'], 'L0_attn_a_ck': _L0_attn_a_in['ck'], 'L0_attn_a_cv': _L0_attn_a_in['cv'], 'L0_attn_a_Wf1': _L0_attn_a_in['Wf1'], 'L0_attn_a_Wf2': _L0_attn_a_in['Wf2'], 'L0_attn_a_Wb': _L0_attn_a_in['Wb'], 'L0_attn_a_Wg1': _L0_attn_a_in['Wg1'], 'L0_attn_a_Wg2': _L0_attn_a_in['Wg2'], 'L0_attn_a_bg2': _L0_attn_a_in['bg2'], 'L0_attn_a_norm_w': _L0_attn_a_in['norm_w'], 'L0_attn_a_Wo': _L0_attn_a_in['Wo'], 'L0_attn_b_q_w': _L0_attn_b_in['q_w'], 'L0_attn_b_k_w': _L0_attn_b_in['k_w'], 'L0_attn_b_v_w': _L0_attn_b_in['v_w'], 'L0_attn_b_q_b': _L0_attn_b_in['q_b'], 'L0_attn_b_k_b': _L0_attn_b_in['k_b'], 'L0_attn_b_v_b': _L0_attn_b_in['v_b'], 'L0_attn_b_out_w': _L0_attn_b_in['out_w'], 'L0_attn_b_out_b': _L0_attn_b_in['out_b'], 'L0_ffn_wq': _L0_ffn_in['wq'], 'L0_ffn_bq': _L0_ffn_in['bq'], 'L0_ffn_wk': _L0_ffn_in['wk'], 'L0_ffn_bk': _L0_ffn_in['bk'], 'L0_ffn_wv': _L0_ffn_in['wv'], 'L0_ffn_bv': _L0_ffn_in['bv'], 'L0_ffn_wo': _L0_ffn_in['wo'], 'L0_ffn_bo': _L0_ffn_in['bo'], 'L0_ffn_ln1_w': _L0_ffn_in['ln1_w'], 'L0_ffn_ln1_b': _L0_ffn_in['ln1_b'], 'L0_ffn_ln2_w': _L0_ffn_in['ln2_w'], 'L0_ffn_ln2_b': _L0_ffn_in['ln2_b'], 'L0_ffn_w_gate': _L0_ffn_in['w_gate'], 'L0_ffn_we1': _L0_ffn_in['we1'], 'L0_ffn_be1': _L0_ffn_in['be1'], 'L0_ffn_we2': _L0_ffn_in['we2'], 'L0_ffn_be2': _L0_ffn_in['be2']}
    _x0 = _d['L0_attn_a_hidden_states']
    _d['L0_attn_a_hidden_states'] = jax.random.normal(jax.random.fold_in(jax.random.key(seed), 1), (2, 512, 256), dtype=_x0.dtype)
    del _x0
    return _d

def reference(L0_attn_a_hidden_states, L0_attn_a_Wq, L0_attn_a_Wk, L0_attn_a_Wv, L0_attn_a_Ww, L0_attn_a_cq, L0_attn_a_ck, L0_attn_a_cv, L0_attn_a_Wf1, L0_attn_a_Wf2, L0_attn_a_Wb, L0_attn_a_Wg1, L0_attn_a_Wg2, L0_attn_a_bg2, L0_attn_a_norm_w, L0_attn_a_Wo, L0_attn_b_q_w, L0_attn_b_k_w, L0_attn_b_v_w, L0_attn_b_q_b, L0_attn_b_k_b, L0_attn_b_v_b, L0_attn_b_out_w, L0_attn_b_out_b, L0_ffn_wq, L0_ffn_bq, L0_ffn_wk, L0_ffn_bk, L0_ffn_wv, L0_ffn_bv, L0_ffn_wo, L0_ffn_bo, L0_ffn_ln1_w, L0_ffn_ln1_b, L0_ffn_ln2_w, L0_ffn_ln2_b, L0_ffn_w_gate, L0_ffn_we1, L0_ffn_be1, L0_ffn_we2, L0_ffn_be2):

    def _L0_attn_a_ref(hidden_states, Wq, Wk, Wv, Ww, cq, ck, cv, Wf1, Wf2, Wb, Wg1, Wg2, bg2, norm_w, Wo):
        import jax, jax.numpy as jnp
        import numpy as np
        B, T, HID = (1, 128, 256)
        H, DK, DV, M, KW = (16, 128, 128, 128, 4)
        SCALE = DK ** (-0.5)
        EPS = 1e-05

        def short_conv(x, w):
            K = w.shape[1]
            xp = jnp.pad(x, ((0, 0), (K - 1, 0), (0, 0)))
            t = x.shape[1]
            y = sum((xp[:, i:i + t] * w[:, i] for i in range(K)))
            return jax.nn.silu(y)

        def l2norm(x):
            return x * jax.lax.rsqrt(jnp.sum(x * x, axis=-1, keepdims=True) + 1e-06)

        def gsa2_scan(q, k, v, w, g, beta):
            b = q.shape[0]
            tm = lambda x: jnp.moveaxis(x, 1, 0)
            Sk0 = jnp.zeros((b, H, DK, M), q.dtype)
            Sv0 = jnp.zeros((b, H, M, DV), q.dtype)

            def step(carry, xs):
                Sk, Sv = carry
                q_t, k_t, v_t, w_t, g_t, b_t = xs
                gt = jnp.exp(g_t)
                bw = b_t[:, :, None] * w_t
                Sk = Sk * gt[:, :, None, :] + k_t[..., :, None] * bw[:, :, None, :]
                Sv = Sv * gt[..., None] + bw[..., None] * v_t[:, :, None, :]
                s = jnp.einsum('bhd,bhdm->bhm', q_t, Sk) * SCALE
                a = jax.nn.softmax(s, axis=-1)
                o_t = jnp.einsum('bhm,bhmd->bhd', a, Sv)
                return ((Sk, Sv), o_t)
            (_, _), o = jax.lax.scan(step, (Sk0, Sv0), (tm(q), tm(k), tm(v), tm(w), tm(g), tm(beta)))
            return jnp.moveaxis(o, 0, 1)
        h = hidden_states
        q = short_conv(h @ Wq, cq)
        k = short_conv(h @ Wk, ck)
        v = short_conv(h @ Wv, cv)
        w = short_conv(h @ Ww, cv)
        g = jax.nn.log_sigmoid(h @ Wf1 @ Wf2)
        beta = jax.nn.sigmoid(h @ Wb)
        rs = lambda x, d: x.reshape(x.shape[0], x.shape[1], -1, d)
        q, k = (rs(q, DK), rs(k, DK))
        v = rs(v, DV)
        w = l2norm(rs(w, M))
        g = rs(g, M)
        o = gsa2_scan(q, k, v, w, g, beta)
        gate = rs(h @ Wg1 @ Wg2 + bg2, DV)
        o = o * jax.lax.rsqrt(jnp.mean(o * o, axis=-1, keepdims=True) + EPS)
        o = o * norm_w * jax.nn.sigmoid(gate)
        o = o.reshape(o.shape[0], o.shape[1], -1)
        return o @ Wo

    def _L0_attn_b_ref(x, q_w, k_w, v_w, q_b, k_b, v_b, out_w, out_b):
        import jax, jax.numpy as jnp
        import numpy as np
        EMBED_DIM = 256
        NUM_HEADS = 16
        HEAD_DIM = EMBED_DIM // NUM_HEADS
        BASE = 10000.0

        def rotate_half(x):
            half = x.shape[-1] // 2
            x1, x2 = (x[..., :half], x[..., half:])
            return jnp.concatenate([-x2, x1], axis=-1)

        def apply_rope(x, base=BASE):
            S, Dh = (x.shape[-2], x.shape[-1])
            inv_freq = 1.0 / base ** (jnp.arange(0, Dh, 2, dtype=jnp.float32) / Dh)
            t = jnp.arange(S, dtype=jnp.float32)
            freqs = jnp.einsum('i,j->ij', t, inv_freq)
            emb = jnp.concatenate([freqs, freqs], axis=-1)
            return x * jnp.cos(emb) + rotate_half(x) * jnp.sin(emb)
        B, S, D = x.shape
        H, Dh = (NUM_HEADS, HEAD_DIM)
        scaling = Dh ** (-0.5)
        q = (x @ q_w.T + q_b).reshape(B, S, H, Dh).transpose(0, 2, 1, 3)
        k = (x @ k_w.T + k_b).reshape(B, S, H, Dh).transpose(0, 2, 1, 3)
        v = (x @ v_w.T + v_b).reshape(B, S, H, Dh).transpose(0, 2, 1, 3)
        q = apply_rope(q)
        k = apply_rope(k)
        attn = jnp.einsum('bhqd,bhkd->bhqk', q, k) * scaling
        probs = jax.nn.softmax(attn, axis=-1)
        out = jnp.einsum('bhqk,bhkd->bhqd', probs, v)
        out = out.transpose(0, 2, 1, 3).reshape(B, S, D)
        return out @ out_w.T + out_b

    def _L0_ffn_ref(hidden_states, wq, bq, wk, bk, wv, bv, wo, bo, ln1_w, ln1_b, ln2_w, ln2_b, w_gate, we1, be1, we2, be2):
        import jax, jax.numpy as jnp
        import numpy as np
        import math
        B, S, D = (2, 256, 256)
        H, HD = (16, 128)
        E, I = (4, 256)
        TOP_K = 2
        ROPE_THETA = 10000.0

        def _layernorm(x, w, b):
            mu = jnp.mean(x, axis=-1, keepdims=True)
            var = jnp.mean(jnp.square(x - mu), axis=-1, keepdims=True)
            return (x - mu) * jax.lax.rsqrt(var + 1e-05) * w + b

        def _rotate_half(x):
            x1, x2 = jnp.split(x, 2, axis=-1)
            return jnp.concatenate((-x2, x1), axis=-1)

        def _attention(h, wq, bq, wk, bk, wv, bv, wo, bo):
            b, s, _ = h.shape
            q = (h @ wq + bq).reshape(b, s, H, HD).transpose(0, 2, 1, 3)
            k = (h @ wk + bk).reshape(b, s, H, HD).transpose(0, 2, 1, 3)
            v = (h @ wv + bv).reshape(b, s, H, HD).transpose(0, 2, 1, 3)
            inv_freq = 1.0 / ROPE_THETA ** (jnp.arange(0, HD, 2, dtype=jnp.float32) / HD)
            freqs = jnp.arange(s, dtype=jnp.float32)[:, None] * inv_freq[None, :]
            emb = jnp.concatenate((freqs, freqs), axis=-1)
            cos = jnp.cos(emb)[None, None]
            sin = jnp.sin(emb)[None, None]
            q = q * cos + _rotate_half(q) * sin
            k = k * cos + _rotate_half(k) * sin
            scores = jnp.einsum('bhqd,bhkd->bhqk', q, k) / math.sqrt(HD)
            causal = jnp.tril(jnp.ones((s, s), bool))
            scores = jnp.where(causal[None, None], scores, jnp.finfo(jnp.float32).min)
            probs = jax.nn.softmax(scores.astype(jnp.float32), axis=-1).astype(q.dtype)
            out = jnp.einsum('bhqk,bhkd->bhqd', probs, v)
            out = out.transpose(0, 2, 1, 3).reshape(b, s, H * HD)
            return out @ wo + bo

        def _moe(h, w_gate, we1, be1, we2, be2):
            b, s, d = h.shape
            x = h.reshape(-1, d)
            t = x.shape[0]
            raw = jax.nn.softmax(x @ w_gate, axis=-1)
            top_vals, top_idx = jax.lax.top_k(raw, TOP_K)
            w = jax.nn.softmax(top_vals, axis=-1)
            comb = jnp.zeros((t, E), x.dtype).at[jnp.arange(t)[:, None], top_idx].add(w)
            hmid = jax.nn.gelu(jnp.einsum('td,edi->tei', x, we1) + be1[None], approximate=False)
            eout = jnp.einsum('tei,eid->ted', hmid, we2) + be2[None]
            out = jnp.einsum('te,ted->td', comb, eout)
            return out.reshape(b, s, d)
        a = _attention(_layernorm(hidden_states, ln1_w, ln1_b), wq, bq, wk, bk, wv, bv, wo, bo)
        h = hidden_states + a
        m = _moe(_layernorm(h, ln2_w, ln2_b), w_gate, we1, be1, we2, be2)
        return h + m
    x = L0_attn_a_hidden_states
    x = x + _L0_attn_a_ref(_layernorm(x, axis=-1), L0_attn_a_Wq, L0_attn_a_Wk, L0_attn_a_Wv, L0_attn_a_Ww, L0_attn_a_cq, L0_attn_a_ck, L0_attn_a_cv, L0_attn_a_Wf1, L0_attn_a_Wf2, L0_attn_a_Wb, L0_attn_a_Wg1, L0_attn_a_Wg2, L0_attn_a_bg2, L0_attn_a_norm_w, L0_attn_a_Wo)
    x = x + _L0_ffn_ref(_layernorm(x, axis=-1), L0_ffn_wq, L0_ffn_bq, L0_ffn_wk, L0_ffn_bk, L0_ffn_wv, L0_ffn_bv, L0_ffn_wo, L0_ffn_bo, L0_ffn_ln1_w, L0_ffn_ln1_b, L0_ffn_ln2_w, L0_ffn_ln2_b, L0_ffn_w_gate, L0_ffn_we1, L0_ffn_be1, L0_ffn_we2, L0_ffn_be2)
    x = x + _L0_attn_b_ref(_layernorm(x, axis=-1), L0_attn_b_q_w, L0_attn_b_k_w, L0_attn_b_v_w, L0_attn_b_q_b, L0_attn_b_k_b, L0_attn_b_v_b, L0_attn_b_out_w, L0_attn_b_out_b)
    x = x + _L0_ffn_ref(_layernorm(x, axis=-1), L0_ffn_wq, L0_ffn_bq, L0_ffn_wk, L0_ffn_bk, L0_ffn_wv, L0_ffn_bv, L0_ffn_wo, L0_ffn_bo, L0_ffn_ln1_w, L0_ffn_ln1_b, L0_ffn_ln2_w, L0_ffn_ln2_b, L0_ffn_w_gate, L0_ffn_we1, L0_ffn_be1, L0_ffn_we2, L0_ffn_be2)
    return x

_drawn_inputs = setup_inputs


def setup_inputs(seed=0):
    import zlib

    import numpy as np

    out = dict(_drawn_inputs(seed))
    spreads = {'L0_attn_a_bg2': (0.0, 0.8),
     'L0_attn_a_norm_w': (1.0, 0.6),
     'L0_attn_b_q_b': (0.0, 0.8),
     'L0_attn_b_k_b': (0.0, 0.8),
     'L0_attn_b_v_b': (0.0, 0.1),
     'L0_attn_b_out_b': (0.0, 0.1),
     'L0_ffn_bq': (0.0, 0.8),
     'L0_ffn_bk': (0.0, 0.8),
     'L0_ffn_bv': (0.0, 0.1),
     'L0_ffn_bo': (0.0, 0.1),
     'L0_ffn_ln1_w': (1.0, 0.6),
     'L0_ffn_ln1_b': (0.0, 0.301),
     'L0_ffn_ln2_w': (1.0, 0.6),
     'L0_ffn_ln2_b': (0.0, 0.539),
     'L0_ffn_be1': (0.0, 0.742),
     'L0_ffn_be2': (0.0, 0.1)}
    factors = {'L0_attn_a_Wq': 8.0,
     'L0_attn_a_Wk': 8.0,
     'L0_attn_a_cq': 8.0,
     'L0_attn_a_ck': 8.0,
     'L0_attn_a_Wf1': 8.0,
     'L0_attn_a_Wf2': 8.0,
     'L0_attn_a_Wb': 6.714,
     'L0_attn_a_Wg1': 8.0,
     'L0_attn_a_Wg2': 8.0,
     'L0_ffn_wq': 8.0,
     'L0_ffn_wk': 8.0}
    for name, (base, spread) in spreads.items():
        noise = np.random.default_rng([zlib.crc32(name.encode()), seed]).standard_normal(out[name].shape)
        drawn = base * np.exp(spread * noise) if base else spread * noise
        out[name] = jnp.asarray(drawn.astype(out[name].dtype))
    for name, factor in factors.items():
        out[name] = (out[name] * factor).astype(out[name].dtype)
    return out
```

```python
from contextlib import ExitStack

import numpy as np

import concourse.bass as bass
from concourse import mybir

F32 = mybir.dt.float32
U32 = mybir.dt.uint32
BF16 = mybir.dt.bfloat16
ALU = mybir.AluOpType
ACT = mybir.ActivationFunctionType
AX = mybir.AxisListType

P = 128
B, T, D = 2, 512, 256
NT = B * T // P
CH = T // P
DC = D // P
EPS = 1e-5

H = 16
HG = 4
NG = H // HG
LEVELS = 7
SLOT_SCALE = float(P) ** -0.5

FH = 16
E, I, TOPK = 4, 256, 2
BH, BD = 16, 16
BT = 4
B_SCALE = float(BD) ** -0.5


def rope(heads_dim, length):
    inv = (1.0 / np.float32(10000.0) ** (np.arange(0, heads_dim, 2, dtype=np.float32) / np.float32(heads_dim))).astype(np.float32)
    freqs = np.arange(length, dtype=np.float32)[:, None] * inv[None, :]
    emb = np.concatenate([freqs, freqs], axis=-1)
    return np.cos(emb).astype(np.float32).T, np.sin(emb).astype(np.float32).T


def constants():
    eye = np.eye(P, dtype=np.float32)
    i, t = np.arange(P)[:, None], np.arange(P)[None, :]
    masks = []
    for l in range(LEVELS):
        right = [c for c in range(P) if (c >> l) & 1]
        masks.append(((i >> l) + 1 == (t >> l)).astype(np.float32)[:, right])
    cos, sin = rope(P, T)
    swap = np.concatenate([sin[P // 2:], -sin[:P // 2]])
    scale = np.float32(P ** -0.5)
    fold = np.stack([cos * scale, swap * scale, cos, swap])
    bcos, bsin = rope(BD, T)
    pcos, psin = np.zeros((P, T), np.float32), np.zeros((P, T), np.float32)
    turn = np.zeros((P, P), np.float32)
    for g in range(4):
        pcos[32 * g:32 * g + BD], psin[32 * g:32 * g + BD] = bcos, bsin
        for d in range(BD // 2):
            turn[32 * g + d + BD // 2, 32 * g + d] = -1.0
            turn[32 * g + d, 32 * g + d + BD // 2] = 1.0
    causal = np.where(t <= i, 0.0, -3.3e38).astype(np.float32)
    return {
        "c_eye": eye,
        "c_masks": np.ascontiguousarray(np.concatenate(masks, axis=1)),
        "c_rope": np.ascontiguousarray(fold.transpose(1, 0, 2)),
        "c_brope": np.ascontiguousarray(np.stack([pcos, psin], axis=1)),
        "c_turn": turn,
        "c_causal": causal,
    }


class Chain:

    def __init__(self, eng, sem, at, total):
        self.eng, self.sem, self.base, self.total, self.n = eng, sem, at * total, total, 0

    def then(self, ins):
        self.n += 1
        ins.then_inc(self.sem, 1)
        self.eng.wait_ge(self.sem, self.base + self.n)

    def end(self):
        assert self.n == self.total, f"{self.sem.name}: {self.n} signals, {self.total} stated"


class Core:

    def __init__(self, nc, ctx, d):
        self.nc, self.ctx, self.d = nc, ctx, d
        self.bank = [ctx.enter_context(nc.psum_tensor(f"bank{n}", [P, 512], F32)) for n in range(8)]
        self.x = self.sb("x", [P, NT, D])
        self.xT = self.sb("xT", [P, DC, B * T])
        self.eye = self.sb("eye", [P, P])
        self.io_in = self.sem("io_in")
        self.stats = self.sb("stats", [P, NT, 6])
        self.mean_var = self.sb("mean_var", [P, NT, 2])
        self.rstd = self.sb("rstd", [P, NT])
        self.norm_chain = self.sem("norm_chain")
        self.norm_var = self.sem("norm_var")
        self.norm_root = self.sem("norm_root")
        self.norm_tile = self.sem("norm_tile")
        self.norm_turned = self.sem("norm_turned")
        self.norm_stored = self.sem("norm_stored")
        self.norms = 0
        self.norms_turned = 0
        self.norm_chains = 0

    def sb(self, name, shape, dt=F32, ctx=None):
        return (ctx or self.ctx).enter_context(self.nc.sbuf_tensor(name, shape, dt))

    def sem(self, name, ctx=None):
        return self.ctx.enter_context(self.nc.semaphore(name))


def layer_norm(k, src, dst, turned, weight=None, bias=None):
    nc = k.nc
    n = k.norms
    k.norms += 1
    before = k.norms_turned
    k.norms_turned += 2 * DC if turned else 0
    with nc.Block() as block:
        @block.vector
        def _(dve):
            chain = [k.norm_chains]

            def then(ins):
                chain[0] += 1
                ins.then_inc(k.norm_chain, 1)
                dve.wait_ge(k.norm_chain, chain[0])

            for t in range(NT):
                last = nc.vector.bn_stats(k.stats[:, t, :], src[:, t, :])
            then(last)
            for t in range(NT):
                last = nc.vector.bn_aggr(k.mean_var[:, t, :], k.stats[:, t, :])
            then(last)
            nc.vector.tensor_scalar(k.rstd[:], k.mean_var[:, :, 1], EPS, None, ALU.add).then_inc(k.norm_var, 1)
            dve.wait_ge(k.norm_root, n + 1)
            then(nc.vector.reciprocal(k.rstd[:], k.rstd[:]))
            for t in range(NT):
                nc.vector.tensor_scalar(dst[:, t, :], src[:, t, :], k.mean_var[:, t, 0:1], k.rstd[:, t:t + 1],
                                        ALU.subtract, ALU.mult).then_inc(k.norm_tile, 1)
            k.norm_chains = chain[0]

        @block.scalar
        def _(act):
            act.wait_ge(k.norm_var, n + 1)
            nc.scalar.activation(k.rstd[:], k.rstd[:], ACT.Sqrt).then_inc(k.norm_root, 1)
            if turned:
                for g in range(2 * DC):
                    c, half = g % DC, g // DC
                    act.wait_ge(k.norm_turned, before + g + 1)
                    out = k.xT[:, c, half * 512:half * 512 + 512]
                    if weight is None:
                        ins = nc.scalar.activation(out, k.bank[g][:], ACT.Copy)
                    else:
                        ins = nc.scalar.activation(out, k.bank[g][:], ACT.Identity, bias=bias[:, c:c + 1],
                                                   scale=weight[:, c:c + 1])
                    ins.then_inc(k.norm_stored, 1)

        if turned:
            @block.tensor
            def _(pe):
                for g in range(2 * DC):
                    c, half = g % DC, g // DC
                    pe.wait_ge(k.norm_tile, n * NT + 4 * half + 4)
                    for t in range(4):
                        last = nc.tensor.transpose(k.bank[g][:, t * P:(t + 1) * P],
                                                   dst[:, 4 * half + t, c * P:(c + 1) * P], k.eye[:])
                    last.then_inc(k.norm_turned, 1)


def lay_out(a):
    a = dict(a)
    wide = np.zeros((D, BT, 4, 32), np.float32)
    for name in ("b_q_w", "b_k_w"):
        w = wide.copy()
        w[:, :, :, :BD] = np.asarray(a[name]).T.reshape(D, BT, 4, BD)
        a[name] = np.ascontiguousarray(w.reshape(D, BT * P))
    for name in ("b_q_b", "b_k_b"):
        w = np.zeros((BT, 4, 32), np.float32)
        w[:, :, :BD] = np.asarray(a[name]).reshape(BT, 4, BD)
        a[name] = w.reshape(-1)
    for name in ("b_v_w", "b_out_w"):
        a[name] = np.ascontiguousarray(np.asarray(a[name]).T)
    return a


KINDS = ("w", "k", "v", "q")
UNITS = [(kind, b, h) for kind in KINDS for b in range(B) for h in range(HG)]
NU, NTURN = len(UNITS), 3 * B * HG

TURNS = [(c, what) for c in range(CH)
         for what in [("decayed", l) for l in range(1, LEVELS)] + [("decayed", LEVELS)] * (c < CH - 1)
         + ["scores", "slots"] + ["keys"] * (c < CH - 1)]
PRODUCTS = [(c, what) for c in range(CH)
            for what in ["own score"] + [("score", l) for l in range(LEVELS)] + ["state score"] * (c > 0)
            + ["own pair"] + [("pair", l) for l in range(LEVELS)]
            + ["state 0", "state 1"] * (c < CH - 1)]
CHAIN_W = [(c, y, l) for c in range(CH) for y in range(2)
           for l in range(LEVELS - (1 if (c == CH - 1 or y) else 0))]
CHAIN_S = [(c, y, l) for c in range(CH) for y in range(2)
           for l in ([-1] if y else []) + list(range(LEVELS - (c == 0)))]


def order(events, at, c, *what):
    key = (c, *what)
    return at * len(events) + events.index(key) + 1


def halves(ap, l):
    return ap.rearrange("p h (b s n) -> p h b s n", s=2, n=1 << l)


def packed(ap, l):
    return ap.rearrange("p h (b n) -> p h b n", n=1 << l)


def slot_attention(k):
    nc, d = k.nc, k.d
    with ExitStack() as ctx:
        def sb(name, shape, dt=F32):
            return k.sb(name, shape, dt, ctx)

        sem = k.sem
        masks = sb("masks", [P, LEVELS * 64])
        low_f, low_g = sb("low_f", [P, B * T]), sb("low_g", [P, B * T])
        beta = sb("beta", [P, NT, H])
        taps = sb("taps", [P, 3, H, 4])
        beta_g, taps_g = sb("beta_g", [P, NT, HG]), sb("taps_g", [P, 3, HG, 4])
        nw = sb("nw", [P, 1])
        wring = [sb(f"wring{n}", [P, DC, HG * P]) for n in range(2)]
        wf2, wg2 = sb("wf2", [P, HG * P]), sb("wg2", [P, HG * P])
        bg2 = sb("bg2", [P, HG * P])
        wo = sb("wo_a", [P, HG, D])
        qT, kT, wT, gT = (sb(n, [P, B, HG, T]) for n in ("qT", "kT", "wT", "gT"))
        kv = sb("kv", [P, B, CH, HG, 2 * P])
        bw = sb("bw", [P, B, CH, HG, P])
        ss_w, rt_w = sb("ss_w", [P, NT, HG]), sb("rt_w", [P, NT, HG])
        ss_o, rt_o = sb("ss_o", [P, NT, HG]), sb("rt_o", [P, NT, HG])
        sums, nmax = sb("sums", [P, B, HG]), sb("nmax", [P, B, HG])

        work = sb("work", [P, WORK_WORDS])
        a_const = sem("a_const")
        low_made, low_kept = sem("low_made"), sem("low_kept")
        layer_norm(k, k.x, qT[:, 0].rearrange("p h t -> p (h t)").rearrange("p (t n) -> p t n", n=D), True)
        wlow = work[:, 0:2 * DC * P].rearrange("p (m c n) -> p m c n", m=2, c=DC)
        wb = work[:, 2 * DC * P:2 * DC * P + DC * H].rearrange("p (c n) -> p c n", c=DC)
        with nc.Block() as block:
            @block.sync
            def _(sp):
                sp.dma_start(wlow[:, 0], d["Wf1"].rearrange("(c p) n -> p c n", p=P)).then_inc(a_const, 16)
                sp.dma_start(wlow[:, 1], d["Wg1"].rearrange("(c p) n -> p c n", p=P)).then_inc(a_const, 16)
                sp.dma_start(wb, d["Wb"].rearrange("(c p) n -> p c n", p=P)).then_inc(a_const, 16)
                sp.dma_start(masks[:], d["c_masks"]).then_inc(a_const, 16)
                for n, name in enumerate(("cq", "ck", "cv")):
                    sp.dma_start(taps[:, n], d[name].rearrange("(h p) j -> p h j", p=P)).then_inc(a_const, 16)
                sp.dma_start(nw[:], d["norm_w"].rearrange("(p a) -> p a", a=1)).then_inc(a_const, 16)

            @block.tensor
            def _(pe):
                pe.wait_ge(a_const, 8 * 16)
                for m in range(2):
                    for half in range(2):
                        for c in range(DC):
                            last = nc.tensor.matmul(k.bank[2 * m + half][:], wlow[:, m, c, :],
                                                    k.xT[:, c, half * 512:half * 512 + 512],
                                                    start=(c == 0), stop=(c == DC - 1))
                        last.then_inc(low_made, 1)
                for t in range(NT):
                    for c in range(DC):
                        last = nc.tensor.matmul(k.bank[4][:, t * H:(t + 1) * H], k.xT[:, c, t * P:(t + 1) * P],
                                                wb[:, c, :], start=(c == 0), stop=(c == DC - 1))
                last.then_inc(low_made, 1)

            @block.scalar
            def _(act):
                for m, low in enumerate((low_f, low_g)):
                    for half in range(2):
                        act.wait_ge(low_made, 2 * m + half + 1)
                        nc.scalar.activation(low[:, half * 512:half * 512 + 512], k.bank[2 * m + half][:],
                                             ACT.Copy).then_inc(low_kept, 1)
                act.wait_ge(low_made, 5)
                nc.scalar.activation(beta[:].rearrange("p t h -> p (t h)"), k.bank[4][:, 0:NT * H],
                                     ACT.Sigmoid).then_inc(low_kept, 1)

        w_in = [sem(f"w_in{n}") for n in range(2)]
        rest_in = sem("rest_in")
        taps_ready = sem("taps_ready")
        projected, tapped, conved, silued = sem("projected"), sem("tapped"), sem("conved"), sem("silued")
        conv_chain = sem("conv_chain")
        turned1, kept1 = sem("turned1"), sem("kept1")
        gated = sem("gated")
        squared, w_sums, w_root, w_scale, w_scaled = (sem(n) for n in ("squared", "w_sums", "w_root", "w_scale", "w_scaled"))
        turned = [sem(f"turned_{b}") for b in range(B)]
        kept = [sem(f"kept_{b}") for b in range(B)]
        made = [sem(f"made_{b}") for b in range(B)]
        used = [sem(f"used_{b}") for b in range(B)]
        paired = [sem(f"paired_{b}") for b in range(B)]
        masked = [sem(f"masked_{b}") for b in range(B)]
        out_kept = [sem(f"out_kept_{b}") for b in range(B)]
        chain_w = [sem(f"chain_w_{b}") for b in range(B)]
        chain_s = [sem(f"chain_s_{b}") for b in range(B)]
        chain_e = sem("chain_e")
        scored = [sem(f"scored_{b}") for b in range(B)]
        maxed = [sem(f"maxed_{b}") for b in range(B)]
        normed = [sem(f"normed_{b}") for b in range(B)]
        dve_chain = sem("dve_chain")
        out_copied = sem("out_copied")
        o_var, o_root, o_rstd = sem("o_var"), sem("o_root"), sem("o_rstd")
        gate_made, gate_biased, gate_done = sem("gate_made"), sem("gate_biased"), sem("gate_done")
        y_ready, y_turned, y_kept, y_out, x_added = (sem(n) for n in ("y_ready", "y_turned", "y_kept", "y_out", "x_added"))

        at = [0]

        def part(words):
            at[0] += words
            assert at[0] <= WORK_WORDS
            return work[:, at[0] - words:at[0]]

        hv = "p (h n) -> p h n"
        at[0] = 0
        cbuf = [part(512) for _ in range(4)]
        vtmp = [part(512) for _ in range(2)]
        sq = part(CH * HG * P).rearrange("p (c h n) -> p c h n", c=CH, h=HG)
        at[0] = 0
        U = [part(512).rearrange(hv, h=HG) for _ in range(B)]
        UT = [[part(512).rearrange(hv, h=HG) for _ in range(2)] for _ in range(B)]
        S = [part(512).rearrange(hv, h=HG) for _ in range(B)]
        acc = [part(512).rearrange(hv, h=HG) for _ in range(B)]
        EE = [part(512).rearrange(hv, h=HG) for _ in range(B)]
        PT = [part(512).rearrange(hv, h=HG) for _ in range(B)]
        AM = [[part(256).rearrange(hv, h=HG) for _ in range(2)] for _ in range(B)]
        KV = [part(1024).rearrange(hv, h=HG) for _ in range(B)]
        SK = [part(512).rearrange(hv, h=HG) for _ in range(B)]
        tmp = part(512).rearrange(hv, h=HG)
        at[0] = 0
        gt = [part(512) for _ in range(2)]
        y = [part(512).rearrange(hv, h=HG) for _ in range(2)]
        yT = [part(512).rearrange(hv, h=HG) for _ in range(2)]

        def blocks(b, l, c):
            if l == 0:
                return gT[:, b, :, c * P:(c + 1) * P]
            o = P - (P >> (l - 1))
            return EE[b][:, :, o:o + (P >> l)]

        def decay(b, l, c, half):
            e = blocks(b, l, c).rearrange("p h (b s) -> p h b s", s=2)[:, :, :, half:half + 1]
            return e.broadcast_to([P, HG, 64 >> l, 1 << l])

        def chunk(ap, b, c):
            return ap[:, b, :, c * P:(c + 1) * P]

        def rbank(b, c, *what):
            return k.bank[4 * b + 1 + PRODUCTS.index((c, *what)) % 2]

        b3 = lambda n: n[:].rearrange("p (h n) -> p h n", h=HG)

        def mask(l):
            m = masks[:, 64 * l:64 * l + 64].rearrange("p (b n) -> p b n", n=1 << l)
            return m.unsqueeze(1).broadcast_to([P, HG, 64 >> l, 1 << l])

        eyes = k.eye[:].unsqueeze(1).broadcast_to([P, HG, P])

        with nc.Block() as block:
            @block.sync
            def _(sp):
                src = {"w": "Ww", "k": "Wk", "v": "Wv", "q": "Wq"}

                def load(kind, g):
                    n = KINDS.index(kind) % 2
                    w = d[src[kind]].rearrange("(c p) (g n) -> g p c n", p=P, n=HG * P)
                    sp.dma_start(wring[n][:], w[bass.ds(g, 1)].rearrange("g p c n -> (g p) c n")).then_inc(w_in[n], 16)

                def rest(g):
                    sp.dma_start(wf2[:], d["Wf2"].rearrange("p (g n) -> p g n", n=HG * P)[:, bass.ds(g, 1)]
                                 .rearrange("p g n -> p (g n)")).then_inc(rest_in, 16)
                    sp.dma_start(wg2[:], d["Wg2"].rearrange("p (g n) -> p g n", n=HG * P)[:, bass.ds(g, 1)]
                                 .rearrange("p g n -> p (g n)")).then_inc(rest_in, 16)
                    sp.dma_start(bg2[:], d["bg2"].rearrange("(g n) -> g n", n=HG * P)[bass.ds(g, 1)]
                                 .broadcast_to([P, HG * P])).then_inc(rest_in, 16)
                    sp.dma_start(wo[:], d["Wo"].rearrange("(g h p) n -> g p h n", p=P, h=HG)[bass.ds(g, 1)]
                                 .rearrange("g p h n -> (g p) h n")).then_inc(rest_in, 16)

                def group(g, last):
                    sp.wait_ge(x_added, g * NT + 1)
                    rest(g)
                    for n, kind in enumerate(("v", "q")):
                        sp.wait_ge(projected, g * (NU + 8) + 8 * n + 8)
                        load(kind, g)
                    if not last:
                        for n, kind in enumerate(("w", "k")):
                            sp.wait_ge(projected, g * (NU + 8) + 8 * n + 24)
                            load(kind, g + 1)

                load("w", 0)
                load("k", 0)
                with sp.Fori(0, NG - 1) as g:
                    group(g, False)
                group(NG - 1, True)

            @block.tensor
            def _(pe):
                with pe.Fori(0, NG) as g:
                    pe.wait_ge(x_added, g * NT + 1)

                    def turn_unit(i):
                        kind, b, h = UNITS[i]
                        src = {"w": wT[:, b, h], "k": kT[:, b, h], "v": vtmp[i % 2]}[kind]
                        pe.wait_ge(silued, g * NU + i + 1)
                        if i >= 2:
                            pe.wait_ge(kept1, g * 32 + i - 1)
                        for c in range(CH):
                            last = nc.tensor.transpose(k.bank[4 + i % 2][:, c * P:(c + 1) * P],
                                                       src[:, c * P:(c + 1) * P], k.eye[:])
                        last.then_inc(turned1, 1)

                    for i, (kind, b, h) in enumerate(UNITS):
                        n = KINDS.index(kind)
                        if i % 8 == 0:
                            pe.wait_ge(w_in[n % 2], g * 32 + 16 * (n // 2) + 16)
                        if i >= 4:
                            pe.wait_ge(conved, g * NU + i - 3)
                        for c in range(DC):
                            last = nc.tensor.matmul(k.bank[i % 4][:], wring[n % 2][:, c, h * P:(h + 1) * P],
                                                    k.xT[:, c, b * T:(b + 1) * T], start=(c == 0), stop=(c == DC - 1))
                        last.then_inc(projected, 1)
                        if 2 <= i < NTURN + 2:
                            turn_unit(i - 2)
                    pe.wait_ge(rest_in, g * 64 + 64)
                    for i in range(8):
                        b, h = i // HG, i % HG
                        if i < 4:
                            pe.wait_ge(conved, g * NU + NU - 3 + i)
                        else:
                            pe.wait_ge(gated, g * 8 + i - 3)
                        nc.tensor.matmul(k.bank[i % 4][:], wf2[:, h * P:(h + 1) * P], low_f[:, b * T:(b + 1) * T],
                                         start=True, stop=True).then_inc(projected, 1)
                    for i in range(8):
                        b, h = i // HG, i % HG
                        if i % HG == 0:
                            pe.wait_ge(w_scaled, g * 2 + b + 1)
                        pe.wait_ge(kept1, g * 32 + NTURN + i - 1)
                        for c in range(CH):
                            last = nc.tensor.transpose(k.bank[4 + i % 2][:, c * P:(c + 1) * P], bw[:, b, c, h, :], k.eye[:])
                        last.then_inc(turned1, 1)

                    pe.wait_ge(kept1, g * 32 + 32)
                    pe.wait_ge(gated, g * 8 + 8)

                    def product(b, c, what, pairs):
                        i = PRODUCTS.index((c, what))
                        if i >= 2:
                            pe.wait_ge(used[b], g * len(PRODUCTS) + i - 1)
                        out = b3(rbank(b, c, what))
                        for h in range(HG):
                            lhsT, rhs = pairs(h)
                            last = nc.tensor.matmul(out[:, h], lhsT, rhs, start=True, stop=True)
                        last.then_inc(made[b], 1)

                    def turn(b, c, what, src):
                        i = TURNS.index((c, what))
                        if i >= 1:
                            pe.wait_ge(kept[b], g * len(TURNS) + i)
                        for h in range(HG):
                            last = nc.tensor.transpose(k.bank[4 * b][:, h * P:(h + 1) * P], src(h), k.eye[:])
                        last.then_inc(turned[b], 1)

                    for c in range(CH):
                        for b in range(B):
                            if c:
                                pe.wait_ge(out_kept[b], g * CH + c)
                            for h in range(HG):
                                last = nc.tensor.matmul(b3(k.bank[4 * b + 3])[:, h], chunk(kT, b, c)[:, h], chunk(qT, b, c)[:, h],
                                                        start=True, stop=True)
                            last.then_inc(paired[b], 1)
                        for b in range(B):
                            pe.wait_ge(masked[b], g * CH * 8 + c * 8 + 1)
                            product(b, c, "own score", lambda h: (bw[:, b, c, h], PT[b][:, h]))
                        for l in range(LEVELS):
                            for b in range(B):
                                pe.wait_ge(masked[b], g * CH * 8 + c * 8 + 2 + l)
                                if l:
                                    pe.wait_ge(kept[b], order(TURNS, g, c, ("decayed", l)))
                                product(b, c, ("score", l),
                                        lambda h: (UT[b][l % 2][:, h] if l else bw[:, b, c, h],
                                                   AM[b][l % 2][:, h].unsqueeze(1).broadcast_to([P, 2, 64])))
                            for b in range(B):
                                if (c, ("decayed", l + 1)) in TURNS:
                                    pe.wait_ge(chain_w[b], order(CHAIN_W, g, c, 0, l))
                                    turn(b, c, ("decayed", l + 1), lambda h: U[b][:, h])
                        if c:
                            for b in range(B):
                                pe.wait_ge(kept[b], order(TURNS, g, c - 1, "keys"))
                                product(b, c, "state score", lambda h: (SK[b][:, h], chunk(qT, b, c)[:, h]))
                        for b in range(B):
                            pe.wait_ge(scored[b], g * CH + c + 1)
                            turn(b, c, "scores", lambda h: acc[b][:, h])
                        for b in range(B):
                            pe.wait_ge(normed[b], g * CH + c + 1)
                            turn(b, c, "slots", lambda h: acc[b][:, h])
                        for b in range(B):
                            pe.wait_ge(kept[b], order(TURNS, g, c, "slots"))
                            product(b, c, "own pair", lambda h: (chunk(wT, b, c)[:, h], S[b][:, h]))
                        for l in range(LEVELS):
                            for b in range(B):
                                if l:
                                    pe.wait_ge(chain_w[b], order(CHAIN_W, g, c, 1, l - 1))
                                pe.wait_ge(chain_s[b], order(CHAIN_S, g, c, 1, l - 1))
                                product(b, c, ("pair", l),
                                        lambda h: (U[b][:, h] if l else chunk(wT, b, c)[:, h],
                                                   S[b][:, h]))
                        for b in range(B):
                            pe.wait_ge(used[b], order(PRODUCTS, g, c, ("pair", LEVELS - 1)))
                            if c:
                                pe.wait_ge(chain_s[b], order(CHAIN_S, g, c, 1, LEVELS - 1))
                            for h in range(HG):
                                out = b3(k.bank[4 * b + 3])[:, h]
                                if c:
                                    nc.tensor.matmul(out, S[b][:, h], KV[b][:, h, P:], start=True, stop=False)
                                last = nc.tensor.matmul(out, PT[b][:, h], kv[:, b, c, h, P:], start=(c == 0), stop=True)
                            last.then_inc(paired[b], 1)
                        if c < CH - 1:
                            for b in range(B):
                                for n in range(2):
                                    what = f"state {n}"
                                    i = PRODUCTS.index((c, what))
                                    pe.wait_ge(used[b], g * len(PRODUCTS) + i - 1)
                                    for h in (2 * n, 2 * n + 1):
                                        last = nc.tensor.matmul(rbank(b, c, what)[:, (h % 2) * 256:(h % 2) * 256 + 256],
                                                                UT[b][LEVELS % 2][:, h], kv[:, b, c, h, :], start=True, stop=True)
                                    last.then_inc(made[b], 1)
                            for b in range(B):
                                pe.wait_ge(used[b], order(PRODUCTS, g, c, "state 1"))
                                turn(b, c, "keys", lambda h: KV[b][:, h, 0:P])

                    def gate(t):
                        if t >= 2:
                            pe.wait_ge(gate_biased, g * NT + t - 1)
                        nc.tensor.matmul(k.bank[t % 2][:], low_g[:, t * P:(t + 1) * P], wg2[:], start=True, stop=True)\
                            .then_inc(gate_made, 1)

                    for b in range(B):
                        pe.wait_ge(out_kept[b], g * CH + CH)
                    gate(0)
                    for t in range(NT):
                        if t + 1 < NT:
                            gate(t + 1)
                        pe.wait_ge(y_ready, g * NT + t + 1)
                        if t >= 2:
                            pe.wait_ge(y_kept, g * NT + t - 1)
                        for h in range(HG):
                            last = nc.tensor.transpose(k.bank[2 + t % 2][:, h * P:(h + 1) * P], y[t % 2][:, h], k.eye[:])
                        last.then_inc(y_turned, 1)
                        pe.wait_ge(y_kept, g * NT + t + 1)
                        if t >= 2:
                            pe.wait_ge(x_added, g * NT + t)
                        for h in range(HG):
                            last = nc.tensor.matmul(k.bank[4 + t % 2][:, 0:D], yT[t % 2][:, h], wo[:, h], start=(h == 0), stop=(h == HG - 1))
                        last.then_inc(y_out, 1)

            @block.scalar
            def _(act):
                with act.Fori(0, NG) as g:
                    dest = {"w": wT, "k": kT, "q": qT}

                    def keep_turned(i):
                        kind, b, h = UNITS[i]
                        act.wait_ge(turned1, g * 32 + i + 1)
                        out = {"w": bw[:, b, :, h, :], "k": kv[:, b, :, h, 0:P], "v": kv[:, b, :, h, P:]}[kind]
                        nc.scalar.activation(out, k.bank[4 + i % 2][:].rearrange("p (c n) -> p c n", c=CH), ACT.Copy).then_inc(kept1, 1)

                    act.wait_ge(taps_ready, g + 1)
                    for i in range(NU + 2):
                        if i < NU:
                            kind, b, h = UNITS[i]
                            act.wait_ge(projected, g * (NU + 8) + i + 1)
                            if i >= 4:
                                act.wait_ge(silued, g * NU + i - 3)
                            nc.scalar.activation(cbuf[i % 4], k.bank[i % 4][:], ACT.Copy,
                                                 scale=taps_g[:, {"q": 0, "k": 1}.get(kind, 2), h, 3:4]).then_inc(tapped, 1)
                        if 1 <= i <= NU:
                            kind, b, h = UNITS[i - 1]
                            act.wait_ge(conved, g * NU + i)
                            if kind == "v" and i - 1 >= 18:
                                act.wait_ge(turned1, g * 32 + i - 2)
                            out = vtmp[(i - 1) % 2] if kind == "v" else dest[kind][:, b, h]
                            nc.scalar.activation(out, cbuf[(i - 1) % 4], ACT.Silu).then_inc(silued, 1)
                        if 3 <= i < NTURN + 3:
                            keep_turned(i - 3)
                    act.wait_ge(w_sums, g * 3 + 3)
                    nc.scalar.activation(rt_w[:], ss_w[:], ACT.Sqrt).then_inc(w_root, 1)
                    for i in range(8):
                        act.wait_ge(projected, g * (NU + 8) + NU + i + 1)
                        nc.scalar.activation(gT[:, i // HG, i % HG], k.bank[i % 4][:], ACT.Sigmoid).then_inc(gated, 1)
                    for i in range(8):
                        act.wait_ge(turned1, g * 32 + NTURN + i + 1)
                        nc.scalar.activation(wT[:, i // HG, i % HG], k.bank[4 + i % 2][:], ACT.Copy).then_inc(kept1, 1)

                    def keep(b, c, what, out):
                        act.wait_ge(turned[b], order(TURNS, g, c, what))
                        nc.scalar.activation(out, b3(k.bank[4 * b]), ACT.Copy).then_inc(kept[b], 1)

                    for c in range(CH):
                        for l in range(1, LEVELS + 1):
                            for b in range(B):
                                if (c, ("decayed", l)) in TURNS:
                                    keep(b, c, ("decayed", l), UT[b][l % 2])
                        for b in range(B):
                            act.wait_ge(turned[b], order(TURNS, g, c, "scores"))
                            act.wait_ge(maxed[b], g * CH + c + 1)
                            for h in range(HG):
                                last = nc.scalar.activation(acc[b][:, h], b3(k.bank[4 * b])[:, h], ACT.Exp, bias=nmax[:, b, h:h + 1],
                                                            scale=SLOT_SCALE, accum_out=sums[:, b, h:h + 1])
                            last.then_inc(kept[b], 1)
                        for b in range(B):
                            keep(b, c, "slots", S[b])
                        for b in range(B):
                            act.wait_ge(paired[b], g * 2 * CH + 2 * c + 2)
                            out = b3(k.bank[4 * b + 3])
                            nc.scalar.activation(chunk(qT, b, c), out, ACT.Copy).then_inc(out_copied, 1)
                            act.wait_ge(out_copied, g * CH * B + c * B + b + 1)
                            for h in range(HG):
                                last = nc.scalar.activation(out[:, h], out[:, h], ACT.Square, accum_out=ss_o[:, b * CH + c, h:h + 1])
                            last.then_inc(out_kept[b], 1)
                        if c < CH - 1:
                            for b in range(B):
                                keep(b, c, "keys", SK[b])

                    act.wait_ge(o_var, g + 1)
                    nc.scalar.activation(rt_o[:], rt_o[:], ACT.Sqrt).then_inc(o_root, 1)

                    def gate(t):
                        act.wait_ge(gate_biased, g * NT + t + 1)
                        nc.scalar.activation(gt[t % 2], gt[t % 2], ACT.Sigmoid).then_inc(gate_done, 1)

                    gate(0)
                    for t in range(NT):
                        if t + 1 < NT:
                            gate(t + 1)
                        act.wait_ge(y_turned, g * NT + t + 1)
                        if t >= 2:
                            act.wait_ge(y_out, g * NT + t - 1)
                        nc.scalar.activation(yT[t % 2], b3(k.bank[2 + t % 2]), ACT.Copy, scale=nw[:]).then_inc(y_kept, 1)

            @block.gpsimd
            def _(pool):
                with pool.Fori(0, NG) as g:
                    pool.wait_ge(kept1, g * 32 + 8)
                    for b in range(B):
                        if b:
                            pool.wait_ge(w_sums, g * 3 + 1)
                        nc.gpsimd.tensor_tensor(sq, bw[:, b], bw[:, b], ALU.mult).then_inc(squared, 1)
                    pool.wait_ge(gated, g * 8 + 8)
                    pool.wait_ge(kept1, g * 32 + 32)
                    e = Chain(pool, chain_e, g, B * CH * (LEVELS + 0))

                    for c in range(CH):
                        def weights(b, yy, l):
                            src = chunk(wT, b, c) if l == 0 else U[b]
                            nc.gpsimd.tensor_tensor(halves(U[b], l)[:, :, :, 0], halves(src, l)[:, :, :, 0], decay(b, l, c, 1), ALU.mult)\
                                .then_inc(chain_w[b], 1)
                            pool.wait_ge(chain_w[b], order(CHAIN_W, g, c, yy, l))

                        for l in range(LEVELS):
                            for b in range(B):
                                if l == 0:
                                    if c:
                                        pool.wait_ge(paired[b], g * 2 * CH + 2 * c)
                                        pool.wait_ge(used[b], order(PRODUCTS, g, c - 1, "state 1"))
                                eb = blocks(b, l, c).rearrange("p h (b s) -> p h b s", s=2)
                                ins = nc.gpsimd.tensor_tensor(blocks(b, l + 1, c), eb[:, :, :, 0], eb[:, :, :, 1], ALU.mult)
                                if l == 0:
                                    nc.gpsimd.tensor_copy(halves(U[b], 0)[:, :, :, 1], halves(chunk(wT, b, c), 0)[:, :, :, 1])
                                    nc.gpsimd.tensor_copy(halves(S[b], 0)[:, :, :, 0], halves(chunk(gT, b, c), 0)[:, :, :, 0])
                                e.then(ins)
                                if (c, 0, l) in CHAIN_W:
                                    if l:
                                        pool.wait_ge(turned[b], order(TURNS, g, c, ("decayed", l)))
                                    weights(b, 0, l)
                                if (c, 0, l) in CHAIN_S:
                                    if l:
                                        pool.wait_ge(used[b], order(PRODUCTS, g, c, ("score", l)))
                                    src = S[b] if l else chunk(gT, b, c)
                                    nc.gpsimd.tensor_tensor(halves(S[b], l)[:, :, :, 1], halves(src, l)[:, :, :, 1], decay(b, l, c, 0), ALU.mult)\
                                        .then_inc(chain_s[b], 1)
                                    pool.wait_ge(chain_s[b], order(CHAIN_S, g, c, 0, l))
                        for b in range(B):
                            last_turn = ("decayed", LEVELS if c < CH - 1 else LEVELS - 1)
                            pool.wait_ge(turned[b], order(TURNS, g, c, last_turn))
                            nc.gpsimd.tensor_tensor(halves(U[b], 0)[:, :, :, 0], halves(chunk(wT, b, c), 0)[:, :, :, 0], decay(b, 0, c, 1), ALU.mult)
                            nc.gpsimd.tensor_copy(halves(U[b], 0)[:, :, :, 1], halves(chunk(wT, b, c), 0)[:, :, :, 1]).then_inc(chain_w[b], 1)
                            pool.wait_ge(chain_w[b], order(CHAIN_W, g, c, 1, 0))
                        for b in range(B):
                            pool.wait_ge(made[b], order(PRODUCTS, g, c, "own pair"))
                            nc.gpsimd.tensor_tensor(S[b], S[b], chunk(gT, b, c), ALU.mult).then_inc(chain_s[b], 1)
                            pool.wait_ge(chain_s[b], order(CHAIN_S, g, c, 1, -1))
                        for l in range(LEVELS):
                            for b in range(B):
                                if (c, 1, l) not in CHAIN_W and (c, 1, l) not in CHAIN_S:
                                    continue
                                pool.wait_ge(made[b], order(PRODUCTS, g, c, ("pair", l)))
                                if l and (c, 1, l) in CHAIN_W:
                                    weights(b, 1, l)
                                if (c, 1, l) in CHAIN_S:
                                    nc.gpsimd.tensor_tensor(halves(S[b], l)[:, :, :, 1], halves(S[b], l)[:, :, :, 1], decay(b, l, c, 0), ALU.mult)\
                                        .then_inc(chain_s[b], 1)
                                    pool.wait_ge(chain_s[b], order(CHAIN_S, g, c, 1, l))
                    e.end()

            @block.vector
            def _(dve):
                dve.sem_inc(x_added, 1)
                with dve.Fori(0, NG) as g:
                    nc.vector.tensor_copy(beta_g[:], beta[:, :, bass.ds(g * HG, HG)])
                    nc.vector.tensor_copy(taps_g[:], taps[:, :, bass.ds(g * HG, HG), :]).then_inc(taps_ready, 1)
                    ch = Chain(dve, conv_chain, g, 2 * NU)
                    for i, (kind, b, h) in enumerate(UNITS):
                        dve.wait_ge(tapped, g * NU + i + 1)
                        for j in (2, 1, 0):
                            s = 3 - j
                            ins = nc.vector.scalar_tensor_tensor(out=cbuf[i % 4][:, s:], in0=k.bank[i % 4][:, 0:T - s],
                                                                 scalar=taps_g[:, {"q": 0, "k": 1}.get(kind, 2), h, j:j + 1],
                                                                 in1=cbuf[i % 4][:, s:], op0=ALU.mult, op1=ALU.add)
                            if j:
                                ch.then(ins)
                            else:
                                ins.then_inc(conved, 1)
                        if i == 20 or i == 26:
                            b = (i - 20) // 6
                            dve.wait_ge(squared, g * 2 + b + 1)
                            nc.vector.tensor_reduce(ss_w[:, b * CH:(b + 1) * CH], sq, AX.X, ALU.add).then_inc(w_sums, 1)
                    ch.end()
                    dve.wait_ge(w_sums, g * 3 + 2)
                    nc.vector.tensor_scalar(ss_w[:], ss_w[:], 1e-6, None, ALU.add).then_inc(w_sums, 1)
                    dve.wait_ge(w_root, g + 1)
                    nc.vector.reciprocal(rt_w[:], rt_w[:]).then_inc(w_scale, 1)
                    dve.wait_ge(w_scale, g * 2 + 1)
                    nc.vector.tensor_tensor(rt_w[:], rt_w[:], beta_g[:], ALU.mult).then_inc(w_scale, 1)
                    dve.wait_ge(w_scale, g * 2 + 2)
                    for b in range(B):
                        sc = rt_w[:, b * CH:(b + 1) * CH].unsqueeze(3).broadcast_to([P, CH, HG, P])
                        nc.vector.tensor_tensor(bw[:, b], bw[:, b], sc, ALU.mult).then_inc(w_scaled, 1)

                    ch = Chain(dve, dve_chain, g, DVE_CHAIN)
                    for c in range(CH):
                        def mask_level(b, l):
                            if l >= 2:
                                dve.wait_ge(made[b], order(PRODUCTS, g, c, ("score", l - 2)))
                            src = halves(b3(k.bank[4 * b + 3]), l)[:, :, :, 1]
                            nc.vector.tensor_tensor(packed(AM[b][l % 2], l), src, mask(l), ALU.mult).then_inc(masked[b], 1)

                        def take(b, what):
                            dve.wait_ge(made[b], order(PRODUCTS, g, c, what))
                            return b3(rbank(b, c, what))

                        for b in range(B):
                            dve.wait_ge(paired[b], g * 2 * CH + 2 * c + 1)
                            nc.vector.tensor_tensor(PT[b], b3(k.bank[4 * b + 3]), eyes, ALU.mult).then_inc(masked[b], 1)
                            mask_level(b, 0)
                            mask_level(b, 1)
                        for b in range(B):
                            nc.vector.tensor_copy(acc[b], take(b, "own score")).then_inc(used[b], 1)
                            dve.wait_ge(used[b], order(PRODUCTS, g, c, "own score"))
                        for l in range(LEVELS):
                            for b in range(B):
                                src = packed(take(b, ("score", l))[:, :, 0:64], l)
                                if l:
                                    dve.wait_ge(chain_s[b], order(CHAIN_S, g, c, 0, l - 1))
                                reach = S[b] if l else chunk(gT, b, c)
                                if l == 0:
                                    dve.wait_ge(gated, g * 8 + 8)
                                nc.vector.tensor_tensor(packed(tmp[:, :, 0:64], l), src, halves(reach, l)[:, :, :, 1], ALU.mult).then_inc(used[b], 1)
                                dve.wait_ge(used[b], order(PRODUCTS, g, c, ("score", l)))
                                a = halves(acc[b], l)[:, :, :, 1]
                                ins = nc.vector.tensor_tensor(a, a, packed(tmp[:, :, 0:64], l), ALU.add)
                                if l == LEVELS - 1 and c == 0:
                                    ins.then_inc(scored[b], 1)
                                    dve.wait_ge(scored[b], g * CH + c + 1)
                                else:
                                    ch.then(ins)
                                if l + 2 < LEVELS:
                                    mask_level(b, l + 2)
                        if c:
                            for b in range(B):
                                src = take(b, "state score")
                                dve.wait_ge(chain_s[b], order(CHAIN_S, g, c, 0, LEVELS - 1))
                                nc.vector.tensor_tensor(tmp, src, S[b], ALU.mult).then_inc(used[b], 1)
                                dve.wait_ge(used[b], order(PRODUCTS, g, c, "state score"))
                                nc.vector.tensor_tensor(acc[b], acc[b], tmp, ALU.add).then_inc(scored[b], 1)
                                dve.wait_ge(scored[b], g * CH + c + 1)
                        for b in range(B):
                            dve.wait_ge(turned[b], order(TURNS, g, c, "scores"))
                            ch.then(nc.vector.tensor_reduce(nmax[:, b], b3(k.bank[4 * b]), AX.X, ALU.max, negate=True))
                            nc.vector.tensor_scalar(nmax[:, b], nmax[:, b], SLOT_SCALE, None, ALU.mult).then_inc(maxed[b], 1)
                        for b in range(B):
                            dve.wait_ge(kept[b], order(TURNS, g, c, "scores"))
                            ch.then(nc.vector.reciprocal(sums[:, b], sums[:, b]))
                            r = sums[:, b].unsqueeze(2).broadcast_to([P, HG, P])
                            nc.vector.tensor_tensor(acc[b], acc[b], r, ALU.mult).then_inc(normed[b], 1)
                        for b in range(B):
                            nc.vector.tensor_tensor(PT[b], take(b, "own pair"), eyes, ALU.mult).then_inc(used[b], 1)
                        for l in range(LEVELS):
                            for b in range(B):
                                there = dve.to_reg(order(PRODUCTS, g, c, ("pair", l)))
                                before = dve.to_reg(g * len(PRODUCTS) + PRODUCTS.index((c, ("pair", l))))
                                dve.wait_ge(a_const, 8 * 16)
                                dve.wait_ge(made[b], there)
                                dve.wait_ge(used[b], before)
                                src = halves(b3(rbank(b, c, ("pair", l))), l)[:, :, :, 1]
                                nc.vector.copy_predicated(halves(PT[b], l)[:, :, :, 1], mask(l).bitcast(U32), src).then_inc(used[b], 1)
                        if c < CH - 1:
                            for b in range(B):
                                dve.wait_ge(paired[b], g * 2 * CH + 2 * c + 2)
                                for n in range(2):
                                    dve.wait_ge(made[b], order(PRODUCTS, g, c, f"state {n}"))
                                    src = rbank(b, c, f"state {n}")[:].rearrange("p (h n) -> p h n", h=2)
                                    for h in (2 * n, 2 * n + 1):
                                        if c:
                                            ins = nc.vector.scalar_tensor_tensor(out=KV[b][:, h], in0=KV[b][:, h], scalar=blocks(b, LEVELS, c)[:, h],
                                                                                 in1=src[:, h % 2], op0=ALU.mult, op1=ALU.add)
                                        else:
                                            ins = nc.vector.tensor_copy(KV[b][:, h], src[:, h % 2])
                                    ins.then_inc(used[b], 1)
                    ch.end()

                    for b in range(B):
                        dve.wait_ge(out_kept[b], g * CH + CH)
                    nc.vector.tensor_scalar(rt_o[:], ss_o[:], 1.0 / P, EPS, ALU.mult, ALU.add).then_inc(o_var, 1)
                    dve.wait_ge(o_root, g + 1)
                    nc.vector.reciprocal(rt_o[:], rt_o[:]).then_inc(o_rstd, 1)
                    dve.wait_ge(o_rstd, g + 1)

                    def bias(t):
                        dve.wait_ge(gate_made, g * NT + t + 1)
                        if t == 0:
                            dve.wait_ge(rest_in, g * 64 + 64)
                        nc.vector.tensor_tensor(gt[t % 2], k.bank[t % 2][:], bg2[:], ALU.add).then_inc(gate_biased, 1)

                    def add(t):
                        dve.wait_ge(y_out, g * NT + t + 1)
                        nc.vector.tensor_tensor(k.x[:, t], k.x[:, t], k.bank[4 + t % 2][:, 0:D], ALU.add).then_inc(x_added, 1)

                    bias(0)
                    for t in range(NT):
                        dve.wait_ge(gate_done, g * NT + t + 1)
                        if t >= 2:
                            dve.wait_ge(y_turned, g * NT + t - 1)
                        for h in range(HG):
                            o = qT[:, t // CH, h, (t % CH) * P:(t % CH + 1) * P]
                            last = nc.vector.scalar_tensor_tensor(out=y[t % 2][:, h], in0=o, scalar=rt_o[:, t, h:h + 1],
                                                                  in1=gt[t % 2][:, h * P:(h + 1) * P], op0=ALU.mult, op1=ALU.mult)
                        last.then_inc(y_ready, 1)
                        if t + 1 < NT:
                            bias(t + 1)
                        if t:
                            add(t - 1)
                    add(NT - 1)


WORK_WORDS = 11776
DVE_CHAIN = B * (CH * LEVELS - 1) + 2 * B * CH


def expert_block(k, rep):
    nc, d = k.nc, k.d
    r = f"_{rep}"
    with ExitStack() as ctx:
        def sb(name, shape, dt=F32):
            return k.sb(name + r, shape, dt, ctx)

        def sem(name):
            return k.sem(name + r)

        hid = sb("hid", [P, NT, D])
        nrm = sb("nrm", [P, NT, D])
        ln = sb("ln", [P, 4, DC])
        ropes = sb("ropes", [P, 4, T])
        causal = sb("causal", [P, P])
        bqkv = sb("bqkv", [P, 3, FH + 1])
        bo = sb("bo", [P, D])
        wqkv = [sb(f"wqkv{n}", [P, 3, DC, P]) for n in range(2)]
        wo = sb("wo", [P, FH, D])
        oT = sb("oT", [P, FH, B * T])

        f_const, wo_in = sem("f_const"), sem("wo_in")
        with nc.Block() as block:
            @block.sync
            def _(sp):
                for n, name in enumerate(("ln1_w", "ln1_b", "ln2_w", "ln2_b")):
                    sp.dma_start(ln[:, n], d["f_" + name].rearrange("(c p) -> p c", p=P),
                                 allow_slow_non_contiguous=True).then_inc(f_const, 16)
                sp.dma_start(ropes[:], d["c_rope"]).then_inc(f_const, 16)
                sp.dma_start(causal[:], d["c_causal"]).then_inc(f_const, 16)
                for n, name in enumerate(("bq", "bk", "bv")):
                    sp.dma_start(bqkv[:, n, 0:FH], d["f_" + name].rearrange("(h p) -> p h", p=P),
                                 allow_slow_non_contiguous=True).then_inc(f_const, 16)
                sp.dma_start(bo[:], d["f_bo"].rearrange("(a n) -> a n", a=1).broadcast_to([P, D])).then_inc(f_const, 16)
                sp.wait_ge(f_const, 160)
                sp.dma_start(wo[:], d["f_wo"].rearrange("(h p) n -> p h n", p=P)).then_inc(wo_in, 16)
        layer_norm(k, k.x, hid, False)
        layer_norm(k, hid, nrm, True, ln[:, 0], ln[:, 1])

        PAIR = 2
        BODY = PAIR * B
        q_in = [sem(f"q_in{n}") for n in range(PAIR)]
        made_p, roped = sem("made_p"), sem("roped")
        halves_done = sem("halves_done")
        v_made, v_kept = sem("v_made"), sem("v_kept")
        s_made, s_max, s_exp = sem("s_made"), sem("s_max"), sem("s_exp")
        s_recip, p_ready = sem("s_recip"), sem("p_ready")
        p_turned, p_kept = sem("p_turned"), sem("p_kept")
        o_made, o_kept = sem("o_made"), sem("o_kept")
        masks_in = sem("masks_in")
        with ExitStack() as inner:
            def tb(name, shape):
                return k.sb(name + r, shape, F32, inner)

            rot = [[tb(f"rot{n}_{m}", [P, T]) for m in range(2)] for n in range(2)]
            part = [tb(f"rpart{n}", [P, T]) for n in range(2)]
            vv = [tb(f"vv{n}", [P, CH, P]) for n in range(2)]
            pr = [tb(f"pr{n}", [P, T]) for n in range(2)]
            pT = [tb(f"pT{n}", [P, CH, T]) for n in range(2)]
            nmax = tb("nmaxf", [P, 2])
            rs = tb("rs", [P, 2])
            eye_b = k.sb("eye_b" + r, [P, P], BF16, inner)
            causal_b = k.sb("causal_b" + r, [P, P], BF16, inner)

            def keep_o(act, u, g):
                n, b = u // B, u % B
                act.wait_ge(f_const, 160)
                act.wait_ge(o_made, g * BODY + u + 1)
                out = oT[:, bass.ds(g * PAIR + n, 1), b * T:(b + 1) * T].rearrange("p h t -> p (h t)")
                nc.scalar.activation(out, k.bank[6][:], ACT.Identity, bias=bqkv[:, 2, bass.ds(g * PAIR + n, 1)]).then_inc(o_kept, 1)
            with nc.Block() as block:
                @block.sync
                def _(sp):
                    def load(head, n):
                        for m, name in enumerate(("f_wq", "f_wk", "f_wv")):
                            w = d[name].rearrange("(c p) (h n) -> h p c n", p=P, n=P)[bass.ds(head, 1)]
                            sp.dma_start(wqkv[n][:, m], w.rearrange("h p c n -> (h p) c n")).then_inc(q_in[n], 16)

                    for n in range(PAIR):
                        load(n, n)
                    with sp.Fori(0, FH // PAIR - 1) as g:
                        for n in range(PAIR):
                            sp.wait_ge(v_made, g * BODY + n * B + B)
                            load(g * PAIR + PAIR + n, n)
                    sp.wait_ge(v_made, FH * B - B)
                    load(0, 0)

                @block.tensor
                def _(pe):
                    def project(g, u, m):
                        n, b = u // B % PAIR, u % B
                        if m == 0 and b == 0:
                            pe.wait_ge(q_in[n], (g + u // BODY) * 48 + 48)
                        if u or m:
                            pe.wait_ge(roped, (g * BODY + u) * 2 + m)
                        for c in range(DC):
                            last = nc.tensor.matmul(k.bank[0][:], wqkv[n][:, m, c, :], k.xT[:, c, b * T:(b + 1) * T],
                                                    start=(c == 0), stop=(c == DC - 1))
                        last.then_inc(made_p, 1)

                    def values(g, u):
                        n, b = u // B % PAIR, u % B
                        if u:
                            pe.wait_ge(v_kept, g * BODY + u)
                        for t in range(CH):
                            for c in range(DC):
                                last = nc.tensor.matmul(k.bank[1][:, t * P:(t + 1) * P], k.xT[:, c, b * T + t * P:b * T + (t + 1) * P],
                                                        wqkv[n][:, 2, c, :], start=(c == 0), stop=(c == DC - 1))
                        last.then_inc(v_made, 1)

                    pe.wait_ge(masks_in, 2)
                    project(0, 0, 0)
                    project(0, 0, 1)
                    values(0, 0)
                    with pe.Fori(0, FH // PAIR) as g:
                        def scores(u, qt):
                            i = u * CH + qt
                            if qt == 0:
                                pe.wait_ge(roped, (g * BODY + u) * 2 + 2)
                            q, kk = rot[u % 2]
                            if i >= 2:
                                pe.wait_ge(s_exp, g * BODY * CH + i - 1)
                            nc.tensor.matmul(k.bank[2 + i % 2][:, 0:(qt + 1) * P], q[:, qt * P:(qt + 1) * P],
                                             kk[:, 0:(qt + 1) * P], start=True, stop=False)
                            nc.tensor.matmul(k.bank[2 + i % 2][:, qt * P:(qt + 1) * P], eye_b[:], causal_b[:],
                                             start=False, stop=True).then_inc(s_made, 1)

                        def turn(u, qt):
                            i = u * CH + qt
                            pe.wait_ge(p_ready, g * BODY * CH + i + 1)
                            if i >= 2:
                                pe.wait_ge(p_kept, g * BODY * CH + i - 1)
                            for t in range(qt + 1):
                                last = nc.tensor.transpose(k.bank[4 + i % 2][:, t * P:(t + 1) * P],
                                                           pr[i % 2][:, t * P:(t + 1) * P], k.eye[:])
                            last.then_inc(p_turned, 1)

                        def outputs(u):
                            pe.wait_ge(p_kept, (g * BODY + u + 1) * CH)
                            pe.wait_ge(v_kept, g * BODY + u + 1)
                            if u >= 1:
                                pe.wait_ge(o_kept, g * BODY + u + 1)
                            for t in range(CH):
                                last = nc.tensor.matmul(k.bank[6][:, t * P:], vv[u % 2][:, t, :], pT[u % 2][:, t, t * P:],
                                                        start=(t == 0), stop=(t == CH - 1))
                            last.then_inc(o_made, 1)

                        pe.wait_ge(o_kept, g * BODY + 1)
                        for u in range(BODY):
                            scores(u, 0)
                            scores(u, 1)
                            if u:
                                outputs(u - 1)
                            project(g, u + 1, 0)
                            turn(u, 0)
                            scores(u, 2)
                            project(g, u + 1, 1)
                            turn(u, 1)
                            scores(u, 3)
                            values(g, u + 1)
                            turn(u, 2)
                            turn(u, 3)
                        outputs(BODY - 1)

                @block.vector
                def _(dve):
                    def rope(g, u, m):
                        n = u // B
                        i = u * 2 + m
                        dve.wait_ge(made_p, g * BODY * 2 + i + 1)
                        if m == 0 and u >= 2:
                            dve.wait_ge(s_made, g * BODY * CH + (u - 1) * CH)
                        src, out, half = k.bank[0], rot[u % 2][m], P // 2
                        bias = bqkv[:, m, bass.ds(g * PAIR + n, 1)]
                        nc.vector.scalar_tensor_tensor(out=out[:], in0=src[:], scalar=bias, in1=ropes[:, 2 * m],
                                                       op0=ALU.add, op1=ALU.mult)
                        for lo in (0, half):
                            last = nc.vector.scalar_tensor_tensor(
                                out=part[m][half - lo:P - lo, :], in0=src[lo:lo + half, :],
                                scalar=bqkv[lo:lo + half, m, bass.ds(g * PAIR + n, 1)],
                                in1=ropes[lo:lo + half, 2 * m + 1], op0=ALU.add, op1=ALU.mult)
                        last.then_inc(halves_done, 1)

                    nc.vector.tensor_copy(eye_b[:], k.eye[:]).then_inc(masks_in, 1)
                    nc.vector.tensor_copy(causal_b[:], causal[:]).then_inc(masks_in, 1)
                    nc.vector.memset(bqkv[:, :, FH:FH + 1], 0.0).then_inc(masks_in, 1)
                    dve.wait_ge(f_const, 160)
                    dve.wait_ge(masks_in, 3)

                    def turned_unit(g, u, m):
                        rope(g, u, m)
                        i = u * 2 + m
                        dve.wait_ge(halves_done, g * BODY * 2 + i + 1)
                        out = rot[u % 2][m]
                        nc.vector.tensor_tensor(out[:], out[:], part[m][:], ALU.add).then_inc(roped, 1)
                        dve.wait_ge(roped, g * BODY * 2 + i + 1)

                    turned_unit(0, 0, 0)
                    turned_unit(0, 0, 1)
                    with dve.Fori(0, FH // PAIR) as g:
                        def maximum(u, qt):
                            i = u * CH + qt
                            dve.wait_ge(s_made, g * BODY * CH + i + 1)
                            if i >= 2:
                                dve.wait_ge(s_exp, g * BODY * CH + i - 1)
                            nc.vector.tensor_reduce(nmax[:, i % 2:i % 2 + 1], k.bank[2 + i % 2][:, 0:(qt + 1) * P], AX.X, ALU.max,
                                                    negate=True).then_inc(s_max, 1)

                        def normalise(u, qt):
                            i = u * CH + qt
                            dve.wait_ge(s_exp, g * BODY * CH + i + 1)
                            nc.vector.reciprocal(rs[:, i % 2:i % 2 + 1], rs[:, i % 2:i % 2 + 1]).then_inc(s_recip, 1)
                            dve.wait_ge(s_recip, g * BODY * CH + i + 1)
                            nc.vector.tensor_scalar(pr[i % 2][:, 0:(qt + 1) * P], pr[i % 2][:, 0:(qt + 1) * P], rs[:, i % 2:i % 2 + 1],
                                                    None, ALU.mult).then_inc(p_ready, 1)

                        for u in range(BODY):
                            maximum(u, 0)
                            maximum(u, 1)
                            normalise(u, 0)
                            turned_unit(g, u + 1, 0)
                            maximum(u, 2)
                            normalise(u, 1)
                            turned_unit(g, u + 1, 1)
                            maximum(u, 3)
                            normalise(u, 2)
                            normalise(u, 3)

                @block.scalar
                def _(act):
                    def keep_v(g, u):
                        act.wait_ge(v_made, g * BODY + u + 1)
                        if u >= 2:
                            act.wait_ge(o_made, g * BODY + u - 1)
                        nc.scalar.activation(vv[u % 2][:].rearrange("p t n -> p (t n)"), k.bank[1][:], ACT.Copy).then_inc(v_kept, 1)

                    act.sem_inc(o_kept, 1)
                    keep_v(0, 0)
                    with act.Fori(0, FH // PAIR) as g:
                        def exps(u, qt):
                            i = u * CH + qt
                            act.wait_ge(s_max, g * BODY * CH + i + 1)
                            if i >= 2:
                                act.wait_ge(p_turned, g * BODY * CH + i - 1)
                            nc.scalar.activation(pr[i % 2][:, 0:(qt + 1) * P], k.bank[2 + i % 2][:, 0:(qt + 1) * P], ACT.Exp,
                                                 bias=nmax[:, i % 2:i % 2 + 1], accum_out=rs[:, i % 2:i % 2 + 1]).then_inc(s_exp, 1)

                        def keep_p(u, qt):
                            i = u * CH + qt
                            act.wait_ge(p_turned, g * BODY * CH + i + 1)
                            nc.scalar.activation(pT[u % 2][:, 0:qt + 1, qt * P:(qt + 1) * P],
                                                 k.bank[4 + i % 2][:, 0:(qt + 1) * P].rearrange("p (t n) -> p t n", n=P),
                                                 ACT.Copy).then_inc(p_kept, 1)

                        for u in range(BODY):
                            exps(u, 0)
                            exps(u, 1)
                            if u:
                                keep_o(act, u - 1, g)
                            keep_p(u, 0)
                            exps(u, 2)
                            keep_p(u, 1)
                            exps(u, 3)
                            keep_v(g, u + 1)
                            keep_p(u, 2)
                            keep_p(u, 3)
                        keep_o(act, BODY - 1, g)

        out_made, h_added = sem("out_made"), sem("h_added")
        hid_biased = sem("hid_biased")
        with nc.Block() as block:
            @block.tensor
            def _(pe):
                pe.wait_ge(wo_in, 16)
                for t in range(NT):
                    if t >= 4:
                        pe.wait_ge(h_added, t - 3)
                    for h in range(FH):
                        last = nc.tensor.matmul(k.bank[t % 4][:, 0:D], oT[:, h, t * P:(t + 1) * P], wo[:, h, :],
                                                start=(h == 0), stop=(h == FH - 1))
                    last.then_inc(out_made, 1)

            @block.vector
            def _(dve):
                nc.vector.tensor_tensor(hid[:], hid[:], bo[:].unsqueeze(1).broadcast_to([P, NT, D]), ALU.add).then_inc(hid_biased, 1)
                dve.wait_ge(hid_biased, 1)
                for t in range(NT):
                    dve.wait_ge(out_made, t + 1)
                    nc.vector.tensor_tensor(hid[:, t], hid[:, t], k.bank[t % 4][:, 0:D], ALU.add).then_inc(h_added, 1)
                dve.wait_ge(h_added, NT)
                nc.vector.tensor_tensor(k.x[:], k.x[:], hid[:], ALU.add)

        layer_norm(k, hid, nrm, True, ln[:, 2], ln[:, 3])
        with ExitStack() as inner:
            def tb(name, shape):
                return k.sb(name + r, shape, F32, inner)

            we1, we2 = tb("we1", [P, E, DC, I]), tb("we2", [P, E, I // P, D])
            wg, be1, be2 = tb("wg", [P, DC, E]), tb("be1", [P, E, I // P]), tb("be2", [E, D])
            raw, gap, comb = tb("raw", [P, NT, E]), tb("gap", [P, NT, E]), tb("comb", [P, NT, E])
            gap2 = tb("gap2", [P, NT, E])
            top, tot = tb("top", [P, NT]), tb("tot", [P, NT])
            beat = tb("beat", [P, NT, E, E])
            combT = tb("combT", [E, B * T])
            hm = [tb(f"hm{n}", [P, I // P, B * T]) for n in range(2)]
            m_in = sem("m_in")
            logits, chain_m, exped, combed, comb_turned, comb_kept = (sem(n) for n in ("logits", "chain_m", "exped", "combed", "comb_turned", "comb_kept"))
            h_made, h_kept, y_made, y_used = (sem(n) for n in ("h_made", "h_kept", "y_made", "y_used"))
            IC = I // P
            with nc.Block() as block:
                @block.sync
                def _(sp):
                    sp.dma_start(wg[:], d["f_w_gate"].rearrange("(c p) e -> p c e", p=P)).then_inc(m_in, 16)
                    sp.dma_start(we1[:], d["f_we1"].rearrange("e (c p) n -> p e c n", p=P)).then_inc(m_in, 16)
                    sp.dma_start(be1[:], d["f_be1"].rearrange("e (c p) -> p e c", p=P), allow_slow_non_contiguous=True).then_inc(m_in, 16)
                    sp.dma_start(be2[:], d["f_be2"]).then_inc(m_in, 16)
                    sp.dma_start(we2[:], d["f_we2"].rearrange("e (c p) n -> p e c n", p=P)).then_inc(m_in, 16)

                @block.tensor
                def _(pe):
                    pe.wait_ge(m_in, 80)
                    for t in range(NT):
                        for c in range(DC):
                            last = nc.tensor.matmul(k.bank[0][:, t * E:(t + 1) * E], k.xT[:, c, t * P:(t + 1) * P], wg[:, c, :],
                                                    start=(c == 0), stop=(c == DC - 1))
                    last.then_inc(logits, 1)

                    def hidden(e):
                        for i in range(2 * IC):
                            ic, half = i // 2, i % 2
                            n = e * 2 * IC + i
                            if n >= 2:
                                pe.wait_ge(h_kept, n - 1)
                            for c in range(DC):
                                last = nc.tensor.matmul(k.bank[4 + n % 2][:], we1[:, e, c, ic * P:(ic + 1) * P],
                                                        k.xT[:, c, half * 512:half * 512 + 512], start=(c == 0), stop=(c == DC - 1))
                            last.then_inc(h_made, 1)

                    def result(n, pairs):
                        if n >= 2:
                            pe.wait_ge(y_used, n - 1)
                        for i, (lhsT, rhs) in enumerate(pairs):
                            last = nc.tensor.matmul(k.bank[6 + n % 2][:, 0:D], lhsT, rhs, start=(i == 0), stop=(i == len(pairs) - 1))
                        last.then_inc(y_made, 1)

                    hidden(0)
                    hidden(1)
                    pe.wait_ge(combed, 1)
                    for t in range(NT):
                        last = nc.tensor.transpose(k.bank[1 + t // 4][0:E, (t % 4) * P:(t % 4 + 1) * P], comb[:, t, :], k.eye[:])
                    last.then_inc(comb_turned, 1)
                    pe.wait_ge(comb_kept, 1)
                    for t in range(NT):
                        result(t, [(combT[:, t * P:(t + 1) * P], be2[:])])
                    for e in range(E):
                        pe.wait_ge(h_kept, (e + 1) * 2 * IC)
                        for t in range(NT):
                            result((e + 1) * NT + t, [(hm[e % 2][:, ic, t * P:(t + 1) * P], we2[:, e, ic, :]) for ic in range(IC)])
                        if e + 2 < E:
                            hidden(e + 2)

                @block.scalar
                def _(act):
                    act.wait_ge(exped, 1)
                    nc.scalar.activation(raw[:], gap[:], ACT.Exp).then_inc(exped, 1)
                    act.wait_ge(exped, 3)
                    nc.scalar.activation(comb[:], gap[:], ACT.Exp).then_inc(exped, 1)
                    for e in range(E):
                        if e == 2:
                            act.wait_ge(comb_turned, 1)
                            for n in range(2):
                                last = nc.scalar.activation(combT[:, n * 512:n * 512 + 512], k.bank[1 + n][0:E, :], ACT.Copy)
                            last.then_inc(comb_kept, 1)
                        for i in range(2 * IC):
                            ic, half = i // 2, i % 2
                            n = e * 2 * IC + i
                            act.wait_ge(h_made, n + 1)
                            if e >= 2:
                                act.wait_ge(y_made, e * NT)
                            nc.scalar.activation(hm[e % 2][:, ic, half * 512:half * 512 + 512], k.bank[4 + n % 2][:], ACT.Gelu,
                                                 bias=be1[:, e, ic:ic + 1]).then_inc(h_kept, 1)

                @block.vector
                def _(dve):
                    count = [0]

                    def then(ins):
                        count[0] += 1
                        ins.then_inc(chain_m, 1)
                        dve.wait_ge(chain_m, count[0])

                    def wide(ap):
                        return ap.unsqueeze(2).broadcast_to([P, NT, E])

                    dve.wait_ge(logits, 1)
                    lg = k.bank[0][:, 0:NT * E].rearrange("p (t e) -> p t e", e=E)
                    then(nc.vector.tensor_reduce(top[:], lg, AX.X, ALU.max))
                    nc.vector.tensor_tensor(gap[:], lg, wide(top[:]), ALU.subtract).then_inc(exped, 1)
                    dve.wait_ge(exped, 2)
                    then(nc.vector.tensor_reduce(tot[:], raw[:], AX.X, ALU.add))
                    then(nc.vector.reciprocal(tot[:], tot[:]))
                    then(nc.vector.tensor_tensor(raw[:], raw[:], wide(tot[:]), ALU.mult))
                    then(nc.vector.tensor_reduce(top[:], raw[:], AX.X, ALU.max))
                    nc.vector.tensor_tensor(gap[:], raw[:], wide(top[:]), ALU.subtract).then_inc(exped, 1)
                    then(nc.vector.memset(beat[:], 0.0))
                    for e in range(E):
                        if e:
                            last = nc.vector.tensor_tensor(beat[:, :, e, 0:e], raw[:, :, 0:e], raw[:, :, e:e + 1].broadcast_to([P, NT, e]), ALU.is_ge)
                        if e < E - 1:
                            last = nc.vector.tensor_tensor(beat[:, :, e, e + 1:E], raw[:, :, e + 1:E], raw[:, :, e:e + 1].broadcast_to([P, NT, E - 1 - e]), ALU.is_gt)
                    then(last)
                    then(nc.vector.tensor_reduce(gap2[:], beat[:], AX.X, ALU.add))
                    then(nc.vector.tensor_scalar(gap2[:], gap2[:], TOPK - 0.5, None, ALU.is_lt))
                    dve.wait_ge(exped, 4)
                    then(nc.vector.tensor_tensor(comb[:], comb[:], gap2[:], ALU.mult))
                    then(nc.vector.tensor_reduce(tot[:], comb[:], AX.X, ALU.add))
                    then(nc.vector.reciprocal(tot[:], tot[:]))
                    nc.vector.tensor_tensor(comb[:], comb[:], wide(tot[:]), ALU.mult).then_inc(combed, 1)
                    dve.wait_ge(combed, 1)
                    for n in range((E + 1) * NT):
                        t = n % NT
                        dve.wait_ge(y_made, n + 1)
                        if n >= NT:
                            dve.wait_ge(y_used, n - NT + 1)
                            nc.vector.scalar_tensor_tensor(out=k.x[:, t], in0=k.bank[6 + n % 2][:, 0:D], scalar=comb[:, t, n // NT - 1:n // NT],
                                                           in1=k.x[:, t], op0=ALU.mult, op1=ALU.add).then_inc(y_used, 1)
                        else:
                            nc.vector.tensor_tensor(k.x[:, t], k.x[:, t], k.bank[6 + n % 2][:, 0:D], ALU.add).then_inc(y_used, 1)


def full_attention(k):
    nc, d = k.nc, k.d
    with ExitStack() as ctx:
        def sb(name, shape, dt=F32):
            return k.sb(name, shape, dt, ctx)

        sem = k.sem
        nrm = sb("c_nrm", [P, NT, D])
        brope, turn_m = sb("brope", [P, 2, T]), sb("turn_m", [P, P])
        wq, wk = sb("c_wq", [P, DC, BT * P]), sb("c_wk", [P, DC, BT * P])
        wv, wout = sb("c_wv", [P, DC, D]), sb("c_wout", [P, DC, D])
        bqk = sb("c_bqk", [P, 2, BT])
        bv, bout = sb("c_bv", [P, D]), sb("c_bout", [P, D])
        q, kk = sb("c_q", [P, BT, B * T]), sb("c_k", [P, BT, B * T])
        v = sb("c_v", [P, NT, D])
        c_in = sem("c_in")
        with nc.Block() as block:
            @block.sync
            def _(sp):
                for dst, src in ((wq, "b_q_w"), (wk, "b_k_w"), (wv, "b_v_w"), (wout, "b_out_w")):
                    sp.dma_start(dst[:], d[src].rearrange("(c p) n -> p c n", p=P)).then_inc(c_in, 16)
                for n, name in enumerate(("b_q_b", "b_k_b")):
                    sp.dma_start(bqk[:, n], d[name].rearrange("(j p) -> p j", p=P), allow_slow_non_contiguous=True).then_inc(c_in, 16)
                for dst, name in ((bv, "b_v_b"), (bout, "b_out_b")):
                    sp.dma_start(dst[:], d[name].rearrange("(a n) -> a n", a=1).broadcast_to([P, D])).then_inc(c_in, 16)
                sp.dma_start(brope[:], d["c_brope"]).then_inc(c_in, 16)
                sp.dma_start(turn_m[:], d["c_turn"]).then_inc(c_in, 16)
        layer_norm(k, k.x, nrm, True)

        flat, biased = [sb(f"c_flat{n}", [P, T]) for n in range(2)], sem("c_biased")
        sn = [sb(f"c_sn{n}", [P, T]) for n in range(2)]
        c_proj, c_turned, c_roped, c_sin, c_vmade, c_vkept = (sem(n) for n in ("c_proj", "c_turned", "c_roped", "c_sin", "c_vmade", "c_vkept"))
        parts = [(m, j, b) for m in range(2) for j in range(BT) for b in range(B)]
        with nc.Block() as block:
            @block.tensor
            def _(pe):
                pe.wait_ge(c_in, 160)

                def project(i):
                    m, j, b = parts[i]
                    if i >= 2:
                        pe.wait_ge(biased, i - 1)
                    for c in range(DC):
                        last = nc.tensor.matmul(k.bank[i % 2][:], (wq, wk)[m][:, c, j * P:(j + 1) * P], k.xT[:, c, b * T:(b + 1) * T],
                                                start=(c == 0), stop=(c == DC - 1))
                    last.then_inc(c_proj, 1)

                project(0)
                for i in range(len(parts)):
                    if i + 1 < len(parts):
                        project(i + 1)
                    pe.wait_ge(biased, i + 1)
                    if i >= 2:
                        pe.wait_ge(c_sin, i - 1)
                    nc.tensor.matmul(k.bank[2 + i % 2][:], turn_m[:], flat[i % 2][:], start=True, stop=True).then_inc(c_turned, 1)
                for t in range(NT):
                    if t >= 2:
                        pe.wait_ge(c_vkept, t - 1)
                    for c in range(DC):
                        last = nc.tensor.matmul(k.bank[4 + t % 2][:, 0:D], k.xT[:, c, t * P:(t + 1) * P], wv[:, c, :],
                                                start=(c == 0), stop=(c == DC - 1))
                    last.then_inc(c_vmade, 1)

            @block.scalar
            def _(act):
                for i, (m, j, b) in enumerate(parts):
                    act.wait_ge(c_proj, i + 1)
                    if i >= 2:
                        act.wait_ge(c_roped, i - 1)
                    nc.scalar.activation(flat[i % 2][:], k.bank[i % 2][:], ACT.Identity, bias=bqk[:, m, j:j + 1]).then_inc(biased, 1)

            @block.vector
            def _(dve):
                for i, (m, j, b) in enumerate(parts):
                    out = (q, kk)[m][:, j, b * T:(b + 1) * T]
                    dve.wait_ge(c_turned, i + 1)
                    nc.vector.tensor_tensor(out, flat[i % 2][:], brope[:, 0], ALU.mult)
                    nc.vector.tensor_tensor(sn[i % 2][:], k.bank[2 + i % 2][:], brope[:, 1], ALU.mult).then_inc(c_sin, 1)
                    dve.wait_ge(c_sin, i + 1)
                    nc.vector.tensor_tensor(out, out, sn[i % 2][:], ALU.add).then_inc(c_roped, 1)
                    dve.wait_ge(c_roped, i + 1)
                for t in range(NT):
                    dve.wait_ge(c_vmade, t + 1)
                    nc.vector.tensor_tensor(v[:, t], k.bank[4 + t % 2][:, 0:D], bv[:], ALU.add).then_inc(c_vkept, 1)

        qc = [sb(f"c_qc{n}", [P, BT, P]) for n in range(B)]
        pr = [sb(f"c_pr{n}", [P, T]) for n in range(2)]
        pT = [sb(f"c_pT{n}", [P, CH, P]) for n in range(2)]
        nmax, rs = sb("c_nmax", [P, 2]), sb("c_rs", [P, B, BH])
        on = [sb(f"c_on{n}", [P, D]) for n in range(B)]
        oT = [sb(f"c_oT{n}", [P, DC, P]) for n in range(B)]
        names = ("c_q_in", "c_made", "c_max", "c_exp", "c_pturned", "c_pkept", "c_out", "c_recip", "c_norm", "c_oturned", "c_okept", "c_done", "c_added")
        q_in, made, maxed, exped, pturned, pkept, out_made, recip, normed, oturned, okept, done, added = (sem(n) for n in names)
        sums_added, nm_made = sem("c_chain"), sem("c_nm_made")
        N = B * BH
        with nc.Block() as block:
            @block.tensor
            def _(pe):
                with pe.Fori(0, CH) as g:
                    def scores(i):
                        b, h = i // BH, i % BH
                        if h == 0:
                            pe.wait_ge(q_in, g * B + b + 1)
                        p0 = 32 * (h % 4)
                        pe.wait_ge(exped, g * N + i - 1) if i >= 2 else None
                        nc.tensor.matmul(k.bank[i % 2][:], qc[b][p0:p0 + BD, h // 4, :], kk[p0:p0 + BD, h // 4, b * T:(b + 1) * T],
                                         start=True, stop=True).then_inc(made, 1)

                    def turn(i):
                        pe.wait_ge(exped, g * N + i + 1)
                        if i >= 2:
                            pe.wait_ge(pkept, g * N + i - 1)
                        for t in range(CH):
                            last = nc.tensor.transpose(k.bank[2 + i % 2][:, t * P:(t + 1) * P], pr[i % 2][:, t * P:(t + 1) * P], k.eye[:])
                        last.then_inc(pturned, 1)

                    def outputs(i):
                        b, h = i // BH, i % BH
                        pe.wait_ge(pkept, g * N + i + 1)
                        for t in range(CH):
                            last = nc.tensor.matmul(k.bank[4 + b][:, h * BD:(h + 1) * BD], pT[i % 2][:, t, :],
                                                    v[:, b * CH + t, h * BD:(h + 1) * BD], start=(t == 0), stop=(t == CH - 1))
                        last.then_inc(out_made, 1)

                    def finish(b):
                        pe.wait_ge(normed, g * B + b + 1)
                        for c in range(DC):
                            last = nc.tensor.transpose(k.bank[6][:, c * P:(c + 1) * P], on[b][:, c * P:(c + 1) * P], k.eye[:])
                        last.then_inc(oturned, 1)

                    def project(b):
                        pe.wait_ge(okept, g * B + b + 1)
                        for c in range(DC):
                            last = nc.tensor.matmul(k.bank[7][:, 0:D], oT[b][:, c, :], wout[:, c, :], start=(c == 0), stop=(c == DC - 1))
                        last.then_inc(done, 1)

                    pe.wait_ge(added, g * B + 1)
                    for i in range(N + 2):
                        if i < N:
                            scores(i)
                        if 1 <= i <= N:
                            turn(i - 1)
                        if i >= 2:
                            outputs(i - 2)
                        if i == BH + 4:
                            finish(0)
                        if i == BH + 8:
                            project(0)
                    finish(1)
                    pe.wait_ge(added, g * B + 2)
                    project(1)

            @block.vector
            def _(dve):
                dve.sem_inc(added, 1)
                with dve.Fori(0, CH) as g:
                    for b in range(B):
                        nc.vector.tensor_copy(qc[b][:], q[:, :, bass.ds(g * P + b * T, P)]).then_inc(q_in, 1)

                    def finish(b):
                        dve.wait_ge(exped, g * N + (b + 1) * BH)
                        nc.vector.reciprocal(rs[:, b], rs[:, b]).then_inc(recip, 1)
                        dve.wait_ge(recip, g * B + b + 1)
                        dve.wait_ge(out_made, g * N + (b + 1) * BH)
                        r = rs[:, b].unsqueeze(2).broadcast_to([P, BH, BD])
                        nc.vector.tensor_tensor(on[b][:].rearrange("p (h n) -> p h n", n=BD),
                                                k.bank[4 + b][:, 0:D].rearrange("p (h n) -> p h n", n=BD), r, ALU.mult).then_inc(normed, 1)

                    def add(b):
                        dve.wait_ge(c_in, 160)
                        dve.wait_ge(done, g * B + b + 1)
                        x = k.x[:, bass.ds(g + b * CH, 1), :].rearrange("p t n -> p (t n)")
                        nc.vector.tensor_tensor(on[b][:], k.bank[7][:, 0:D], bout[:], ALU.add).then_inc(sums_added, 1)
                        dve.wait_ge(c_in, 160)
                        dve.wait_ge(sums_added, g * B + b + 1)
                        nc.vector.tensor_tensor(x, x, on[b][:], ALU.add).then_inc(added, 1)

                    for i in range(N):
                        dve.wait_ge(made, g * N + i + 1)
                        if i >= 2:
                            dve.wait_ge(exped, g * N + i - 1)
                        nc.vector.tensor_reduce(nmax[:, i % 2:i % 2 + 1], k.bank[i % 2][:], AX.X, ALU.max, negate=True).then_inc(nm_made, 1)
                        dve.wait_ge(nm_made, g * N + i + 1)
                        nc.vector.tensor_scalar(nmax[:, i % 2:i % 2 + 1], nmax[:, i % 2:i % 2 + 1], B_SCALE, None, ALU.mult).then_inc(maxed, 1)
                        if i == BH + 2:
                            finish(0)
                        if i == BH + 10:
                            add(0)
                    finish(1)
                    add(1)

            @block.scalar
            def _(act):
                with act.Fori(0, CH) as g:
                    def keep(i):
                        act.wait_ge(pturned, g * N + i + 1)
                        if i >= 2:
                            act.wait_ge(out_made, g * N + i - 1)
                        nc.scalar.activation(pT[i % 2][:].rearrange("p t n -> p (t n)"), k.bank[2 + i % 2][:], ACT.Copy).then_inc(pkept, 1)

                    def finish(b):
                        act.wait_ge(oturned, g * B + b + 1)
                        nc.scalar.activation(oT[b][:].rearrange("p c n -> p (c n)"), k.bank[6][:, 0:D], ACT.Copy).then_inc(okept, 1)

                    act.wait_ge(added, g * B + 1)
                    for i in range(N + 1):
                        if i < N:
                            b, h = i // BH, i % BH
                            act.wait_ge(maxed, g * N + i + 1)
                            if i >= 2:
                                act.wait_ge(pturned, g * N + i - 1)
                            nc.scalar.activation(pr[i % 2][:], k.bank[i % 2][:], ACT.Exp, bias=nmax[:, i % 2:i % 2 + 1], scale=B_SCALE,
                                                 accum_out=rs[:, b, h:h + 1]).then_inc(exped, 1)
                        if i >= 1:
                            keep(i - 1)
                        if i == BH + 5:
                            finish(0)
                    finish(1)


def build(nc, d, out, layers="ABCD"):
    with ExitStack() as ctx:
        k = Core(nc, ctx, d)
        stored = k.sem("stored")
        with nc.Block() as block:
            @block.sync
            def _(sp):
                x_in = d["hidden_states"].rearrange("b (c p) n -> p (b c) n", p=P)
                sp.dma_start(k.x[:], x_in).then_inc(k.io_in, 16)
                sp.dma_start(k.eye[:], d["c_eye"]).then_inc(k.io_in, 16)
                sp.wait_ge(k.io_in, 32)
        if "A" in layers:
            slot_attention(k)
        if "B" in layers:
            expert_block(k, 0)
        if "C" in layers:
            full_attention(k)
        if "D" in layers:
            expert_block(k, 1)
        with nc.Block() as block:
            @block.sync
            def _(sp):
                sp.dma_start(out.rearrange("b (c p) n -> p (b c) n", p=P), k.x[:]).then_inc(stored, 16)
                sp.wait_ge(stored, 16)


def kernel(**inputs):
    import concourse.bacc as _bacc
    from concourse.bass_utils import run_bass_kernel_spmd as _run

    names = {}
    for name, a in inputs.items():
        for long, short in (("L0_attn_a_", ""), ("L0_attn_b_", "b_"), ("L0_ffn_", "f_")):
            if name.startswith(long):
                names[short + name[len(long):]] = np.ascontiguousarray(np.asarray(a))
    held = {**lay_out(names), **constants()}
    nc = _bacc.Bacc("TRN2", target_bir_lowering=False, num_devices=1)
    d = {n: nc.dram_tensor(f"in_{n}_dram", a.shape, mybir.dt.from_np(a.dtype), kind="ExternalInput").ap() for n, a in held.items()}
    out = nc.dram_tensor("out_0_dram", (B, T, D), F32, kind="ExternalOutput").ap()
    build(nc, d, out)
    r = _run(nc, [{f"in_{n}_dram": a for n, a in held.items()}], core_ids=[0])
    return r.results[0]["out_0_dram"]
```

```python
from contextlib import ExitStack

import numpy as np

import concourse.bass as bass
from concourse import mybir

F32 = mybir.dt.float32
U32 = mybir.dt.uint32
BF16 = mybir.dt.bfloat16
ALU = mybir.AluOpType
ACT = mybir.ActivationFunctionType
AX = mybir.AxisListType

P = 128
B, T, D = 2, 512, 256
NT = B * T // P
CH = T // P
DC = D // P
EPS = 1e-5

H = 16
HG = 4
NG = H // HG
LEVELS = 7
SLOT_SCALE = float(P) ** -0.5

FH = 16
E, I, TOPK = 4, 256, 2
BH, BD = 16, 16
BT = 4
B_SCALE = float(BD) ** -0.5


def rope(heads_dim, length):
    inv = (1.0 / np.float32(10000.0) ** (np.arange(0, heads_dim, 2, dtype=np.float32) / np.float32(heads_dim))).astype(np.float32)
    freqs = np.arange(length, dtype=np.float32)[:, None] * inv[None, :]
    emb = np.concatenate([freqs, freqs], axis=-1)
    return np.cos(emb).astype(np.float32).T, np.sin(emb).astype(np.float32).T


def constants():
    eye = np.eye(P, dtype=np.float32)
    i, t = np.arange(P)[:, None], np.arange(P)[None, :]
    masks = []
    for l in range(LEVELS):
        right = [c for c in range(P) if (c >> l) & 1]
        masks.append(((i >> l) + 1 == (t >> l)).astype(np.float32)[:, right])
    cos, sin = rope(P, T)
    swap = np.concatenate([sin[P // 2:], -sin[:P // 2]])
    scale = np.float32(P ** -0.5)
    fold = np.stack([cos * scale, swap * scale, cos, swap])
    bcos, bsin = rope(BD, T)
    pcos, psin = np.zeros((P, T), np.float32), np.zeros((P, T), np.float32)
    turn = np.zeros((P, P), np.float32)
    for g in range(4):
        pcos[32 * g:32 * g + BD], psin[32 * g:32 * g + BD] = bcos, bsin
        for d in range(BD // 2):
            turn[32 * g + d + BD // 2, 32 * g + d] = -1.0
            turn[32 * g + d, 32 * g + d + BD // 2] = 1.0
    causal = np.where(t <= i, 0.0, -3.3e38).astype(np.float32)
    return {
        "c_eye": eye,
        "c_masks": np.ascontiguousarray(np.concatenate(masks, axis=1)),
        "c_rope": np.ascontiguousarray(fold.transpose(1, 0, 2)),
        "c_brope": np.ascontiguousarray(np.stack([pcos, psin], axis=1)),
        "c_turn": turn,
        "c_causal": causal,
    }


class Chain:

    def __init__(self, eng, sem, at, total):
        self.eng, self.sem, self.base, self.total, self.n = eng, sem, at * total, total, 0

    def then(self, ins):
        self.n += 1
        ins.then_inc(self.sem, 1)
        self.eng.wait_ge(self.sem, self.base + self.n)

    def end(self):
        assert self.n == self.total, f"{self.sem.name}: {self.n} signals, {self.total} stated"


class Core:

    def __init__(self, nc, ctx, d):
        self.nc, self.ctx, self.d = nc, ctx, d
        self.sems = []
        self.bank = [ctx.enter_context(nc.psum_tensor(f"bank{n}", [P, 512], F32)) for n in range(8)]
        self.x = self.sb("x", [P, NT, D])
        self.xT = self.sb("xT", [P, DC, B * T])
        self.eye = self.sb("eye", [P, P])
        self.io_in = self.sem("io_in")
        self.stats = self.sb("stats", [P, NT, 6])
        self.mean_var = self.sb("mean_var", [P, NT, 2])
        self.rstd = self.sb("rstd", [P, NT])
        self.norm_chain = self.sem("norm_chain")
        self.norm_var = self.sem("norm_var")
        self.norm_root = self.sem("norm_root")
        self.norm_tile = self.sem("norm_tile")
        self.norm_turned = self.sem("norm_turned")
        self.norm_stored = self.sem("norm_stored")
        self.norms = 0
        self.norms_turned = 0
        self.norm_chains = 0

    def sb(self, name, shape, dt=F32, ctx=None):
        return (ctx or self.ctx).enter_context(self.nc.sbuf_tensor(name, shape, dt))

    def sem(self, name):
        self.sems.append(self.nc.alloc_semaphore(name))
        return self.sems[-1]

    def free_sems(self, kept):
        self.nc.all_engine_barrier()
        self.nc.clear_and_free_semaphores(self.sems[kept:])
        self.nc.all_engine_barrier()
        del self.sems[kept:]


def layer_norm(k, src, dst, turned, weight=None, bias=None, ready=None, loads=None):
    nc = k.nc
    n = k.norms
    k.norms += 1
    before = k.norms_turned
    k.norms_turned += 2 * DC if turned else 0
    with nc.Block() as block:
        if loads:
            @block.sync
            def _(sp):
                loads(sp)

        @block.vector
        def _(dve):
            chain = [k.norm_chains]

            def then(ins):
                chain[0] += 1
                ins.then_inc(k.norm_chain, 1)
                dve.wait_ge(k.norm_chain, chain[0])

            for t in range(NT):
                last = nc.vector.bn_stats(k.stats[:, t, :], src[:, t, :])
            then(last)
            for t in range(NT):
                last = nc.vector.bn_aggr(k.mean_var[:, t, :], k.stats[:, t, :])
            then(last)
            nc.vector.tensor_scalar(k.rstd[:], k.mean_var[:, :, 1], EPS, None, ALU.add).then_inc(k.norm_var, 1)
            dve.wait_ge(k.norm_root, n + 1)
            then(nc.vector.reciprocal(k.rstd[:], k.rstd[:]))
            for t in range(NT):
                nc.vector.tensor_scalar(dst[:, t, :], src[:, t, :], k.mean_var[:, t, 0:1], k.rstd[:, t:t + 1],
                                        ALU.subtract, ALU.mult).then_inc(k.norm_tile, 1)
            k.norm_chains = chain[0]

        @block.scalar
        def _(act):
            act.wait_ge(k.norm_var, n + 1)
            nc.scalar.activation(k.rstd[:], k.rstd[:], ACT.Sqrt).then_inc(k.norm_root, 1)
            if weight is not None:
                act.wait_ge(*ready)
            if turned:
                for g in range(2 * DC):
                    c, half = g % DC, g // DC
                    act.wait_ge(k.norm_turned, before + g + 1)
                    out = k.xT[:, c, half * 512:half * 512 + 512]
                    if weight is None:
                        ins = nc.scalar.activation(out, k.bank[g][:], ACT.Copy)
                    else:
                        ins = nc.scalar.activation(out, k.bank[g][:], ACT.Identity, bias=bias[:, c:c + 1],
                                                   scale=weight[:, c:c + 1])
                    ins.then_inc(k.norm_stored, 1)

        if turned:
            @block.tensor
            def _(pe):
                for g in range(2 * DC):
                    c, half = g % DC, g // DC
                    pe.wait_ge(k.norm_tile, n * NT + 4 * half + 4)
                    for t in range(4):
                        last = nc.tensor.transpose(k.bank[g][:, t * P:(t + 1) * P],
                                                   dst[:, 4 * half + t, c * P:(c + 1) * P], k.eye[:])
                    last.then_inc(k.norm_turned, 1)


def lay_out(a):
    a = dict(a)
    wide = np.zeros((D, BT, 4, 32), np.float32)
    for name in ("b_q_w", "b_k_w"):
        w = wide.copy()
        w[:, :, :, :BD] = np.asarray(a[name]).T.reshape(D, BT, 4, BD)
        a[name] = np.ascontiguousarray(w.reshape(D, BT * P))
    for name in ("b_q_b", "b_k_b"):
        w = np.zeros((BT, 4, 32), np.float32)
        w[:, :, :BD] = np.asarray(a[name]).reshape(BT, 4, BD)
        a[name] = w.reshape(-1)
    a["b_v_w"] = np.ascontiguousarray(np.asarray(a["b_v_w"]).T)
    w = np.zeros((BH, 32, D), np.float32)
    w[:, :BD] = np.asarray(a["b_out_w"]).T.reshape(BH, BD, D)
    a["b_out_w"] = w.reshape(BT * P, D)
    return a


KINDS = ("w", "k", "v", "q")
UNITS = [(kind, b, h) for kind in KINDS for b in range(B) for h in range(HG)]
NU, NTURN = len(UNITS), 3 * B * HG

TURNS = [(c, what) for c in range(CH)
         for what in [("decayed", l) for l in range(1, LEVELS)] + [("decayed", LEVELS)] * (c < CH - 1)
         + ["scores", "slots"] + ["keys"] * (c < CH - 1)]
PRODUCTS = [(c, what) for c in range(CH)
            for what in ["own score"] + [("score", l) for l in range(LEVELS)] + ["state score"] * (c > 0)
            + ["own pair"] + [("pair", l) for l in range(LEVELS)]
            + ["state 0", "state 1"] * (c < CH - 1)]
CHAIN_W = [(c, l) for c in range(CH) for l in range(LEVELS - (c == CH - 1))]
CHAIN_V = [(c, step) for c in range(CH) for step in [0, "slots"] + list(range(1, LEVELS - 1))]
CHAIN_S = [(c, y, l) for c in range(CH) for y in range(2)
           for l in range(LEVELS - (c == 0))]

SLOTS, STEPS = B * CH + 1, 14


def own_registers(eng, g):
    other = eng.alloc_register(f"group_of_{eng.engine.name}")
    eng.reg_add(other, g, 0)
    return g, eng.snap(other, min_val=0, max_val=NG - 1)


def order(events, at, c, *what):
    key = (c, *what)
    return at * len(events) + events.index(key) + 1


def halves(ap, l):
    return ap.rearrange("p h (b s n) -> p h b s n", s=2, n=1 << l)


def packed(ap, l):
    return ap.rearrange("p h (b n) -> p h b n", n=1 << l)


def slot_attention(k):
    nc, d = k.nc, k.d
    with ExitStack() as ctx:
        def sb(name, shape, dt=F32):
            return k.sb(name, shape, dt, ctx)

        sem = k.sem
        masks = sb("masks", [P, LEVELS * 64])
        low_f, low_g = sb("low_f", [P, B * T]), sb("low_g", [P, B * T])
        beta = sb("beta", [P, NT, H])
        taps = sb("taps", [P, 3, H, 4])
        beta_g, taps_g = sb("beta_g", [P, NT, HG]), sb("taps_g", [P, 3, HG, 4])
        nw = sb("nw", [P, 1])
        wring = [sb(f"wring{n}", [P, DC, HG * P]) for n in range(2)]
        wf2, wg2 = sb("wf2", [P, HG * P]), sb("wg2", [P, HG * P])
        bg2 = sb("bg2", [P, HG * P])
        wo = sb("wo_a", [P, HG, D])
        qT, kT, wT, gT = (sb(n, [P, B, HG, T]) for n in ("qT", "kT", "wT", "gT"))
        kv = sb("kv", [P, B, CH, HG, 2 * P])
        bw = sb("bw", [P, B, CH, HG, P])
        ss_w, rt_w = sb("ss_w", [P, NT, HG]), sb("rt_w", [P, NT, HG])
        ss_o, rt_o = sb("ss_o", [P, NT, HG]), sb("rt_o", [P, NT, HG])
        sums, nmax = sb("sums", [P, B, HG]), sb("nmax", [P, B, HG])

        work = sb("work", [P, WORK_WORDS])
        a_const = sem("a_const")
        low_made, low_kept = sem("low_made"), sem("low_kept")
        layer_norm(k, k.x, qT[:, 0].rearrange("p h t -> p (h t)").rearrange("p (t n) -> p t n", n=D), True)
        wlow = work[:, 0:2 * DC * P].rearrange("p (m c n) -> p m c n", m=2, c=DC)
        wb = work[:, 2 * DC * P:2 * DC * P + DC * H].rearrange("p (c n) -> p c n", c=DC)
        with nc.Block() as block:
            @block.sync
            def _(sp):
                sp.dma_start(wlow[:, 0], d["Wf1"].rearrange("(c p) n -> p c n", p=P)).then_inc(a_const, 16)
                sp.dma_start(wlow[:, 1], d["Wg1"].rearrange("(c p) n -> p c n", p=P)).then_inc(a_const, 16)
                sp.dma_start(wb, d["Wb"].rearrange("(c p) n -> p c n", p=P)).then_inc(a_const, 16)
                sp.dma_start(masks[:], d["c_masks"]).then_inc(a_const, 16)
                for n, name in enumerate(("cq", "ck", "cv")):
                    sp.dma_start(taps[:, n], d[name].rearrange("(h p) j -> p h j", p=P)).then_inc(a_const, 16)
                sp.dma_start(nw[:], d["norm_w"].rearrange("(p a) -> p a", a=1)).then_inc(a_const, 16)

            @block.tensor
            def _(pe):
                pe.wait_ge(a_const, 8 * 16)
                for m in range(2):
                    for half in range(2):
                        for c in range(DC):
                            last = nc.tensor.matmul(k.bank[2 * m + half][:], wlow[:, m, c, :],
                                                    k.xT[:, c, half * 512:half * 512 + 512],
                                                    start=(c == 0), stop=(c == DC - 1))
                        last.then_inc(low_made, 1)
                for t in range(NT):
                    for c in range(DC):
                        last = nc.tensor.matmul(k.bank[4][:, t * H:(t + 1) * H], k.xT[:, c, t * P:(t + 1) * P],
                                                wb[:, c, :], start=(c == 0), stop=(c == DC - 1))
                last.then_inc(low_made, 1)

            @block.scalar
            def _(act):
                for m, low in enumerate((low_f, low_g)):
                    for half in range(2):
                        act.wait_ge(low_made, 2 * m + half + 1)
                        nc.scalar.activation(low[:, half * 512:half * 512 + 512], k.bank[2 * m + half][:],
                                             ACT.Copy).then_inc(low_kept, 1)
                act.wait_ge(low_made, 5)
                nc.scalar.activation(beta[:].rearrange("p t h -> p (t h)"), k.bank[4][:, 0:NT * H],
                                     ACT.Sigmoid).then_inc(low_kept, 1)

        w_in = [sem(f"w_in{n}") for n in range(2)]
        rest_in = sem("rest_in")
        taps_ready = sem("taps_ready")
        projected, tapped, conved, silued = sem("projected"), sem("tapped"), sem("conved"), sem("silued")
        conv_chain = sem("conv_chain")
        turned1, kept1 = sem("turned1"), sem("kept1")
        gated = sem("gated")
        squared, w_sums, w_root, w_scale, w_scaled = (sem(n) for n in ("squared", "w_sums", "w_root", "w_scale", "w_scaled"))
        turned = [sem(f"turned_{b}") for b in range(B)]
        kept = [sem(f"kept_{b}") for b in range(B)]
        made = [sem(f"made_{b}") for b in range(B)]
        used = [sem(f"used_{b}") for b in range(B)]
        paired = [sem(f"paired_{b}") for b in range(B)]
        masked = [sem(f"masked_{b}") for b in range(B)]
        out_kept = [sem(f"out_kept_{b}") for b in range(B)]
        chain_w = [sem(f"chain_w_{b}") for b in range(B)]
        chain_v = [sem(f"chain_v_{b}") for b in range(B)]
        chain_s = [sem(f"chain_s_{b}") for b in range(B)]
        chain_e = sem("chain_e")
        scored = [sem(f"scored_{b}") for b in range(B)]
        maxed = [sem(f"maxed_{b}") for b in range(B)]
        normed = [sem(f"normed_{b}") for b in range(B)]
        dve_chain = sem("dve_chain")
        out_copied = sem("out_copied")
        o_var, o_root, o_rstd = sem("o_var"), sem("o_root"), sem("o_rstd")
        gate_made, gate_biased, gate_done = sem("gate_made"), sem("gate_biased"), sem("gate_done")
        y_ready, y_turned, y_kept, y_out, x_added = (sem(n) for n in ("y_ready", "y_turned", "y_kept", "y_out", "x_added"))

        at = [0]

        def part(words):
            at[0] += words
            assert at[0] <= WORK_WORDS
            return work[:, at[0] - words:at[0]]

        hv = "p (h n) -> p h n"
        at[0] = 0
        cbuf = [part(512) for _ in range(4)]
        vtmp = [part(512) for _ in range(2)]
        sq = part(CH * HG * P).rearrange("p (c h n) -> p c h n", c=CH, h=HG)
        at[0] = 0
        U = [part(512).rearrange(hv, h=HG) for _ in range(B)]
        UT = [[part(512).rearrange(hv, h=HG) for _ in range(2)] for _ in range(B)]
        S = [part(512).rearrange(hv, h=HG) for _ in range(B)]
        acc = [part(512).rearrange(hv, h=HG) for _ in range(B)]
        EE = [part(512).rearrange(hv, h=HG) for _ in range(B)]
        PT = [part(512).rearrange(hv, h=HG) for _ in range(B)]
        AM = [[part(256).rearrange(hv, h=HG) for _ in range(2)] for _ in range(B)]
        KV = [part(1024).rearrange(hv, h=HG) for _ in range(B)]
        SK = [part(512).rearrange(hv, h=HG) for _ in range(B)]
        tmp = part(512).rearrange(hv, h=HG)
        at[0] = 0
        gt = [part(512) for _ in range(2)]
        y = [part(512).rearrange(hv, h=HG) for _ in range(2)]
        yT = [part(512).rearrange(hv, h=HG) for _ in range(2)]

        def blocks(b, l, c):
            if l == 0:
                return gT[:, b, :, c * P:(c + 1) * P]
            o = P - (P >> (l - 1))
            return EE[b][:, :, o:o + (P >> l)]

        def decay(b, l, c, half):
            e = blocks(b, l, c).rearrange("p h (b s) -> p h b s", s=2)[:, :, :, half:half + 1]
            return e.broadcast_to([P, HG, 64 >> l, 1 << l])

        def chunk(ap, b, c):
            return ap[:, b, :, c * P:(c + 1) * P]

        def rbank(b, c, *what):
            return k.bank[4 * b + 1 + PRODUCTS.index((c, *what)) % 2]

        b3 = lambda n: n[:].rearrange("p (h n) -> p h n", h=HG)

        def mask(l):
            m = masks[:, 64 * l:64 * l + 64].rearrange("p (b n) -> p b n", n=1 << l)
            return m.unsqueeze(1).broadcast_to([P, HG, 64 >> l, 1 << l])

        eyes = k.eye[:].unsqueeze(1).broadcast_to([P, HG, P])

        with nc.Block() as block:
            @block.sync
            def _(sp):
                src = {"w": "Ww", "k": "Wk", "v": "Wv", "q": "Wq"}

                def load(kind, g):
                    n = KINDS.index(kind) % 2
                    w = d[src[kind]].rearrange("(c p) (g n) -> g p c n", p=P, n=HG * P)
                    sp.dma_start(wring[n][:], w[bass.ds(g, 1)].rearrange("g p c n -> (g p) c n")).then_inc(w_in[n], 16)

                def rest(g):
                    sp.dma_start(wf2[:], d["Wf2"].rearrange("p (g n) -> p g n", n=HG * P)[:, bass.ds(g, 1)]
                                 .rearrange("p g n -> p (g n)")).then_inc(rest_in, 16)
                    sp.dma_start(wg2[:], d["Wg2"].rearrange("p (g n) -> p g n", n=HG * P)[:, bass.ds(g, 1)]
                                 .rearrange("p g n -> p (g n)")).then_inc(rest_in, 16)
                    sp.dma_start(bg2[:], d["bg2"].rearrange("(g n) -> g n", n=HG * P)[bass.ds(g, 1)]
                                 .broadcast_to([P, HG * P])).then_inc(rest_in, 16)
                    sp.dma_start(wo[:], d["Wo"].rearrange("(g h p) n -> g p h n", p=P, h=HG)[bass.ds(g, 1)]
                                 .rearrange("g p h n -> (g p) h n")).then_inc(rest_in, 16)

                def group(g, last):
                    sp.wait_ge(x_added, g * NT + 1)
                    rest(g)
                    for n, kind in enumerate(("v", "q")):
                        sp.wait_ge(projected, g * (NU + 8) + 8 * n + 8)
                        load(kind, g)
                    if not last:
                        for n, kind in enumerate(("w", "k")):
                            sp.wait_ge(projected, g * (NU + 8) + 8 * n + 24)
                            load(kind, g + 1)

                load("w", 0)
                load("k", 0)
                with sp.Fori(0, NG - 1) as g:
                    group(g, False)
                group(NG - 1, True)

            @block.tensor
            def _(pe):
                with pe.Fori(0, NG) as g:
                    pe.wait_ge(x_added, g * NT + 1)

                    def turn_unit(i):
                        kind, b, h = UNITS[i]
                        src = {"w": wT[:, b, h], "k": kT[:, b, h], "v": vtmp[i % 2]}[kind]
                        pe.wait_ge(silued, g * NU + i + 1)
                        if i >= 2:
                            pe.wait_ge(kept1, g * 32 + i - 1)
                        for c in range(CH):
                            last = nc.tensor.transpose(k.bank[4 + i % 2][:, c * P:(c + 1) * P],
                                                       src[:, c * P:(c + 1) * P], k.eye[:])
                        last.then_inc(turned1, 1)

                    for i, (kind, b, h) in enumerate(UNITS):
                        n = KINDS.index(kind)
                        if i % 8 == 0:
                            pe.wait_ge(w_in[n % 2], g * 32 + 16 * (n // 2) + 16)
                        if i >= 4:
                            pe.wait_ge(conved, g * NU + i - 3)
                        for c in range(DC):
                            last = nc.tensor.matmul(k.bank[i % 4][:], wring[n % 2][:, c, h * P:(h + 1) * P],
                                                    k.xT[:, c, b * T:(b + 1) * T], start=(c == 0), stop=(c == DC - 1))
                        last.then_inc(projected, 1)
                        if 2 <= i < NTURN + 2:
                            turn_unit(i - 2)
                    pe.wait_ge(rest_in, g * 64 + 64)
                    for i in range(8):
                        b, h = i // HG, i % HG
                        if i < 4:
                            pe.wait_ge(conved, g * NU + NU - 3 + i)
                        else:
                            pe.wait_ge(gated, g * 8 + i - 3)
                        nc.tensor.matmul(k.bank[i % 4][:], wf2[:, h * P:(h + 1) * P], low_f[:, b * T:(b + 1) * T],
                                         start=True, stop=True).then_inc(projected, 1)
                    for i in range(8):
                        b, h = i // HG, i % HG
                        if i % HG == 0:
                            pe.wait_ge(w_scaled, g * 2 + b + 1)
                        pe.wait_ge(kept1, g * 32 + NTURN + i - 1)
                        for c in range(CH):
                            last = nc.tensor.transpose(k.bank[4 + i % 2][:, c * P:(c + 1) * P], bw[:, b, c, h, :], k.eye[:])
                        last.then_inc(turned1, 1)

                    pe.wait_ge(kept1, g * 32 + 32)
                    pe.wait_ge(gated, g * 8 + 8)

                    at = own_registers(pe, g)
                    def product(b, c, what, pairs):
                        g = at[b]
                        i = PRODUCTS.index((c, what))
                        if i >= 2:
                            pe.wait_ge(used[b], g * len(PRODUCTS) + i - 1)
                        out = b3(rbank(b, c, what))
                        for h in range(HG):
                            lhsT, rhs = pairs(h)
                            last = nc.tensor.matmul(out[:, h], lhsT, rhs, start=True, stop=True)
                        last.then_inc(made[b], 1)

                    def turn(b, c, what, src):
                        g = at[b]
                        i = TURNS.index((c, what))
                        if i >= 1:
                            pe.wait_ge(kept[b], g * len(TURNS) + i)
                        for h in range(HG):
                            last = nc.tensor.transpose(k.bank[4 * b][:, h * P:(h + 1) * P], src(h), k.eye[:])
                        last.then_inc(turned[b], 1)

                    def scores_step(n, b, c):
                        g = at[b]
                        if n == 0:
                            if c:
                                pe.wait_ge(out_kept[b], g * CH + c)
                            for h in range(HG):
                                last = nc.tensor.matmul(b3(k.bank[4 * b + 3])[:, h], chunk(kT, b, c)[:, h], chunk(qT, b, c)[:, h],
                                                        start=True, stop=True)
                            last.then_inc(paired[b], 1)
                            if c:
                                pe.wait_ge(used[b], order(PRODUCTS, g, c - 1, "state 1"))
                                turn(b, c - 1, "keys", lambda h: KV[b][:, h, 0:P])
                        if n == 1:
                            pe.wait_ge(masked[b], g * CH * 8 + c * 8 + 1)
                            product(b, c, "own score", lambda h: (bw[:, b, c, h], PT[b][:, h]))
                        if 2 <= n < LEVELS + 2:
                            l = n - 2
                            pe.wait_ge(masked[b], g * CH * 8 + c * 8 + 2 + l)
                            if l:
                                pe.wait_ge(kept[b], order(TURNS, g, c, ("decayed", l)))
                            product(b, c, ("score", l),
                                    lambda h: (UT[b][l % 2][:, h] if l else bw[:, b, c, h],
                                               AM[b][l % 2][:, h].unsqueeze(1).broadcast_to([P, 2, 64])))
                        if (c, ("decayed", n)) in TURNS:
                            pe.wait_ge(chain_w[b], order(CHAIN_W, g, c, n - 1))
                            turn(b, c, ("decayed", n), lambda h: U[b][:, h])
                        if n == LEVELS + 2 and c:
                            pe.wait_ge(kept[b], order(TURNS, g, c - 1, "keys"))
                            product(b, c, "state score", lambda h: (SK[b][:, h], chunk(qT, b, c)[:, h]))
                        if n == LEVELS + 4:
                            pe.wait_ge(scored[b], g * CH + c + 1)
                            turn(b, c, "scores", lambda h: acc[b][:, h])

                    def outputs_step(n, b, c):
                        g = at[b]
                        if n == 2:
                            pe.wait_ge(normed[b], g * CH + c + 1)
                            turn(b, c, "slots", lambda h: acc[b][:, h])
                        if n == 3:
                            pe.wait_ge(kept[b], order(TURNS, g, c, "slots"))
                            product(b, c, "own pair", lambda h: (chunk(wT, b, c)[:, h], S[b][:, h]))
                        if 4 <= n < LEVELS + 4:
                            l = n - 4
                            if l:
                                pe.wait_ge(chain_s[b], order(CHAIN_S, g, c, 1, l - 1))
                            pe.wait_ge(chain_v[b], order(CHAIN_V, g, c, l - 1 if l > 1 else "slots"))
                            product(b, c, ("pair", l),
                                    lambda h: (U[b][:, h] if l else chunk(wT, b, c)[:, h],
                                               S[b][:, h]))
                        if n == LEVELS + 5:
                            pe.wait_ge(used[b], order(PRODUCTS, g, c, ("pair", LEVELS - 1)))
                            if c:
                                pe.wait_ge(chain_s[b], order(CHAIN_S, g, c, 1, LEVELS - 1))
                            for h in range(HG):
                                out = b3(k.bank[4 * b + 3])[:, h]
                                if c:
                                    nc.tensor.matmul(out, S[b][:, h], KV[b][:, h, P:], start=True, stop=False)
                                last = nc.tensor.matmul(out, PT[b][:, h], kv[:, b, c, h, P:], start=(c == 0), stop=True)
                            last.then_inc(paired[b], 1)
                        if n == LEVELS + 6 and c < CH - 1:
                            for half in range(2):
                                what = f"state {half}"
                                i = PRODUCTS.index((c, what))
                                pe.wait_ge(used[b], g * len(PRODUCTS) + i - 1)
                                for h in (2 * half, 2 * half + 1):
                                    last = nc.tensor.matmul(rbank(b, c, what)[:, (h % 2) * 256:(h % 2) * 256 + 256],
                                                            UT[b][LEVELS % 2][:, h], kv[:, b, c, h, :], start=True, stop=True)
                                last.then_inc(made[b], 1)

                    for s in range(SLOTS):
                        for n in range(STEPS):
                            if s < B * CH:
                                scores_step(n, s % B, s // B)
                            if s:
                                outputs_step(n, (s - 1) % B, (s - 1) // B)

                    def gate(t):
                        if t >= 2:
                            pe.wait_ge(gate_biased, g * NT + t - 1)
                        nc.tensor.matmul(k.bank[t % 2][:], low_g[:, t * P:(t + 1) * P], wg2[:], start=True, stop=True)\
                            .then_inc(gate_made, 1)

                    for b in range(B):
                        pe.wait_ge(out_kept[b], g * CH + CH)
                    gate(0)
                    for t in range(NT):
                        if t + 1 < NT:
                            gate(t + 1)
                        pe.wait_ge(y_ready, g * NT + t + 1)
                        if t >= 2:
                            pe.wait_ge(y_kept, g * NT + t - 1)
                        for h in range(HG):
                            last = nc.tensor.transpose(k.bank[2 + t % 2][:, h * P:(h + 1) * P], y[t % 2][:, h], k.eye[:])
                        last.then_inc(y_turned, 1)
                        pe.wait_ge(y_kept, g * NT + t + 1)
                        if t >= 2:
                            pe.wait_ge(x_added, g * NT + t)
                        for h in range(HG):
                            last = nc.tensor.matmul(k.bank[4 + t % 2][:, 0:D], yT[t % 2][:, h], wo[:, h], start=(h == 0), stop=(h == HG - 1))
                        last.then_inc(y_out, 1)

            @block.scalar
            def _(act):
                with act.Fori(0, NG) as g:
                    dest = {"w": wT, "k": kT, "q": qT}

                    def keep_turned(i):
                        kind, b, h = UNITS[i]
                        act.wait_ge(turned1, g * 32 + i + 1)
                        out = {"w": bw[:, b, :, h, :], "k": kv[:, b, :, h, 0:P], "v": kv[:, b, :, h, P:]}[kind]
                        nc.scalar.activation(out, k.bank[4 + i % 2][:].rearrange("p (c n) -> p c n", c=CH), ACT.Copy).then_inc(kept1, 1)

                    act.wait_ge(taps_ready, g + 1)
                    for i in range(NU + 2):
                        if i < NU:
                            kind, b, h = UNITS[i]
                            act.wait_ge(projected, g * (NU + 8) + i + 1)
                            if i >= 4:
                                act.wait_ge(silued, g * NU + i - 3)
                            nc.scalar.activation(cbuf[i % 4], k.bank[i % 4][:], ACT.Copy,
                                                 scale=taps_g[:, {"q": 0, "k": 1}.get(kind, 2), h, 3:4]).then_inc(tapped, 1)
                        if 1 <= i <= NU:
                            kind, b, h = UNITS[i - 1]
                            act.wait_ge(conved, g * NU + i)
                            if kind == "v" and i - 1 >= 18:
                                act.wait_ge(turned1, g * 32 + i - 2)
                            out = vtmp[(i - 1) % 2] if kind == "v" else dest[kind][:, b, h]
                            nc.scalar.activation(out, cbuf[(i - 1) % 4], ACT.Silu).then_inc(silued, 1)
                        if 3 <= i < NTURN + 3:
                            keep_turned(i - 3)
                    act.wait_ge(w_sums, g * 3 + 3)
                    nc.scalar.activation(rt_w[:], ss_w[:], ACT.Sqrt).then_inc(w_root, 1)
                    for i in range(8):
                        act.wait_ge(projected, g * (NU + 8) + NU + i + 1)
                        nc.scalar.activation(gT[:, i // HG, i % HG], k.bank[i % 4][:], ACT.Sigmoid).then_inc(gated, 1)
                    for i in range(8):
                        act.wait_ge(turned1, g * 32 + NTURN + i + 1)
                        nc.scalar.activation(wT[:, i // HG, i % HG], k.bank[4 + i % 2][:], ACT.Copy).then_inc(kept1, 1)

                    at = own_registers(act, g)
                    def keep(b, c, what, out):
                        g = at[b]
                        act.wait_ge(turned[b], order(TURNS, g, c, what))
                        nc.scalar.activation(out, b3(k.bank[4 * b]), ACT.Copy).then_inc(kept[b], 1)

                    def scores_step(n, b, c):
                        g = at[b]
                        if n == 0 and c:
                            keep(b, c - 1, "keys", SK[b])
                        if (c, ("decayed", n)) in TURNS:
                            keep(b, c, ("decayed", n), UT[b][n % 2])
                        if n == LEVELS + 5:
                            act.wait_ge(turned[b], order(TURNS, g, c, "scores"))
                            act.wait_ge(maxed[b], g * CH + c + 1)
                            for h in range(HG):
                                last = nc.scalar.activation(acc[b][:, h], b3(k.bank[4 * b])[:, h], ACT.Exp, bias=nmax[:, b, h:h + 1],
                                                            scale=SLOT_SCALE, accum_out=sums[:, b, h:h + 1])
                            last.then_inc(kept[b], 1)

                    def outputs_step(n, b, c):
                        g = at[b]
                        if n == 2:
                            keep(b, c, "slots", S[b])
                        if n == LEVELS + 5:
                            act.wait_ge(paired[b], g * 2 * CH + 2 * c + 2)
                            out = b3(k.bank[4 * b + 3])
                            nc.scalar.activation(chunk(qT, b, c), out, ACT.Copy).then_inc(out_copied, 1)
                            act.wait_ge(out_copied, g * CH * B + c * B + b + 1)
                            for h in range(HG):
                                last = nc.scalar.activation(out[:, h], out[:, h], ACT.Square, accum_out=ss_o[:, b * CH + c, h:h + 1])
                            last.then_inc(out_kept[b], 1)

                    for s in range(SLOTS):
                        for n in range(STEPS):
                            if s < B * CH:
                                scores_step(n, s % B, s // B)
                            if s:
                                outputs_step(n, (s - 1) % B, (s - 1) // B)

                    act.wait_ge(o_var, g + 1)
                    nc.scalar.activation(rt_o[:], rt_o[:], ACT.Sqrt).then_inc(o_root, 1)

                    def gate(t):
                        act.wait_ge(gate_biased, g * NT + t + 1)
                        nc.scalar.activation(gt[t % 2], gt[t % 2], ACT.Sigmoid).then_inc(gate_done, 1)

                    gate(0)
                    for t in range(NT):
                        if t + 1 < NT:
                            gate(t + 1)
                        act.wait_ge(y_turned, g * NT + t + 1)
                        if t >= 2:
                            act.wait_ge(y_out, g * NT + t - 1)
                        nc.scalar.activation(yT[t % 2], b3(k.bank[2 + t % 2]), ACT.Copy, scale=nw[:]).then_inc(y_kept, 1)

            @block.gpsimd
            def _(pool):
                with pool.Fori(0, NG) as g:
                    pool.wait_ge(kept1, g * 32 + 8)
                    for b in range(B):
                        if b:
                            pool.wait_ge(w_sums, g * 3 + 1)
                        nc.gpsimd.tensor_tensor(sq, bw[:, b], bw[:, b], ALU.mult).then_inc(squared, 1)
                    pool.wait_ge(gated, g * 8 + 8)
                    pool.wait_ge(kept1, g * 32 + 32)
                    e = Chain(pool, chain_e, g, B * CH * LEVELS)
                    at = own_registers(pool, g)

                    def scores_step(n, b, c):
                        g = at[b]
                        if n < LEVELS:
                            l = n
                            if l == 0 and c:
                                pool.wait_ge(paired[b], g * 2 * CH + 2 * c)
                            if l == LEVELS - 1 and c:
                                pool.wait_ge(used[b], order(PRODUCTS, g, c - 1, "state 1"))
                            eb = blocks(b, l, c).rearrange("p h (b s) -> p h b s", s=2)
                            ins = nc.gpsimd.tensor_tensor(blocks(b, l + 1, c), eb[:, :, :, 0], eb[:, :, :, 1], ALU.mult)
                            if l == 0:
                                nc.gpsimd.tensor_copy(halves(U[b], 0)[:, :, :, 1], halves(chunk(wT, b, c), 0)[:, :, :, 1])
                                nc.gpsimd.tensor_copy(halves(S[b], 0)[:, :, :, 0], halves(chunk(gT, b, c), 0)[:, :, :, 0])
                            e.then(ins)
                            if (c, l) in CHAIN_W:
                                src = U[b] if l else chunk(wT, b, c)
                                if l:
                                    pool.wait_ge(turned[b], order(TURNS, g, c, ("decayed", l)))
                                nc.gpsimd.tensor_tensor(halves(U[b], l)[:, :, :, 0], halves(src, l)[:, :, :, 0], decay(b, l, c, 1), ALU.mult)\
                                    .then_inc(chain_w[b], 1)
                                pool.wait_ge(chain_w[b], order(CHAIN_W, g, c, l))
                        if (c, 0, n - 3) in CHAIN_S:
                            l = n - 3
                            if l:
                                pool.wait_ge(used[b], order(PRODUCTS, g, c, ("score", l)))
                            src = S[b] if l else chunk(gT, b, c)
                            nc.gpsimd.tensor_tensor(halves(S[b], l)[:, :, :, 1], halves(src, l)[:, :, :, 1], decay(b, l, c, 0), ALU.mult)\
                                .then_inc(chain_s[b], 1)
                            pool.wait_ge(chain_s[b], order(CHAIN_S, g, c, 0, l))

                    def outputs_step(n, b, c):
                        g = at[b]
                        l = n - 5
                        if l == 0:
                            pool.wait_ge(chain_v[b], order(CHAIN_V, g, c, "slots"))
                        if l >= 0 and (c, 1, l) in CHAIN_S:
                            pool.wait_ge(made[b], order(PRODUCTS, g, c, ("pair", l)))
                            nc.gpsimd.tensor_tensor(halves(S[b], l)[:, :, :, 1], halves(S[b], l)[:, :, :, 1], decay(b, l, c, 0), ALU.mult)\
                                .then_inc(chain_s[b], 1)
                            pool.wait_ge(chain_s[b], order(CHAIN_S, g, c, 1, l))

                    for s in range(SLOTS):
                        for n in range(STEPS):
                            if s:
                                outputs_step(n, (s - 1) % B, (s - 1) // B)
                            if s < B * CH:
                                scores_step(n, s % B, s // B)
                    e.end()

            @block.vector
            def _(dve):
                dve.sem_inc(x_added, 1)
                with dve.Fori(0, NG) as g:
                    nc.vector.tensor_copy(beta_g[:], beta[:, :, bass.ds(g * HG, HG)])
                    nc.vector.tensor_copy(taps_g[:], taps[:, :, bass.ds(g * HG, HG), :]).then_inc(taps_ready, 1)
                    ch = Chain(dve, conv_chain, g, 2 * NU)
                    for i, (kind, b, h) in enumerate(UNITS):
                        dve.wait_ge(tapped, g * NU + i + 1)
                        for j in (2, 1, 0):
                            s = 3 - j
                            ins = nc.vector.scalar_tensor_tensor(out=cbuf[i % 4][:, s:], in0=k.bank[i % 4][:, 0:T - s],
                                                                 scalar=taps_g[:, {"q": 0, "k": 1}.get(kind, 2), h, j:j + 1],
                                                                 in1=cbuf[i % 4][:, s:], op0=ALU.mult, op1=ALU.add)
                            if j:
                                ch.then(ins)
                            else:
                                ins.then_inc(conved, 1)
                        if i == 20 or i == 26:
                            b = (i - 20) // 6
                            dve.wait_ge(squared, g * 2 + b + 1)
                            nc.vector.tensor_reduce(ss_w[:, b * CH:(b + 1) * CH], sq, AX.X, ALU.add).then_inc(w_sums, 1)
                    ch.end()
                    dve.wait_ge(w_sums, g * 3 + 2)
                    nc.vector.tensor_scalar(ss_w[:], ss_w[:], 1e-6, None, ALU.add).then_inc(w_sums, 1)
                    dve.wait_ge(w_root, g + 1)
                    nc.vector.reciprocal(rt_w[:], rt_w[:]).then_inc(w_scale, 1)
                    dve.wait_ge(w_scale, g * 2 + 1)
                    nc.vector.tensor_tensor(rt_w[:], rt_w[:], beta_g[:], ALU.mult).then_inc(w_scale, 1)
                    dve.wait_ge(w_scale, g * 2 + 2)
                    for b in range(B):
                        sc = rt_w[:, b * CH:(b + 1) * CH].unsqueeze(3).broadcast_to([P, CH, HG, P])
                        nc.vector.tensor_tensor(bw[:, b], bw[:, b], sc, ALU.mult).then_inc(w_scaled, 1)

                    ch = Chain(dve, dve_chain, g, DVE_CHAIN)
                    at = own_registers(dve, g)
                    def mask_level(b, c, l):
                        g = at[b]
                        if l >= 2:
                            dve.wait_ge(made[b], order(PRODUCTS, g, c, ("score", l - 2)))
                        src = halves(b3(k.bank[4 * b + 3]), l)[:, :, :, 1]
                        nc.vector.tensor_tensor(packed(AM[b][l % 2], l), src, mask(l), ALU.mult).then_inc(masked[b], 1)

                    def take(b, c, what):
                        g = at[b]
                        dve.wait_ge(made[b], order(PRODUCTS, g, c, what))
                        return b3(rbank(b, c, what))

                    def scores_step(n, b, c):
                        g = at[b]
                        if n == 0:
                            dve.wait_ge(paired[b], g * 2 * CH + 2 * c + 1)
                            nc.vector.tensor_tensor(PT[b], b3(k.bank[4 * b + 3]), eyes, ALU.mult).then_inc(masked[b], 1)
                            mask_level(b, c, 0)
                        if n == 1:
                            mask_level(b, c, 1)
                        if n == 2:
                            nc.vector.tensor_copy(acc[b], take(b, c, "own score")).then_inc(used[b], 1)
                            dve.wait_ge(used[b], order(PRODUCTS, g, c, "own score"))
                        if 3 <= n < LEVELS + 3:
                            l = n - 3
                            if l + 2 < LEVELS:
                                mask_level(b, c, l + 2)
                            src = packed(take(b, c, ("score", l))[:, :, 0:64], l)
                            if l:
                                dve.wait_ge(chain_s[b], order(CHAIN_S, g, c, 0, l - 1))
                            reach = S[b] if l else chunk(gT, b, c)
                            if l == 0:
                                dve.wait_ge(gated, g * 8 + 8)
                            nc.vector.tensor_tensor(packed(tmp[:, :, 0:64], l), src, halves(reach, l)[:, :, :, 1], ALU.mult).then_inc(used[b], 1)
                            dve.wait_ge(used[b], order(PRODUCTS, g, c, ("score", l)))
                            a = halves(acc[b], l)[:, :, :, 1]
                            ins = nc.vector.tensor_tensor(a, a, packed(tmp[:, :, 0:64], l), ALU.add)
                            if l == LEVELS - 1 and c == 0:
                                ins.then_inc(scored[b], 1)
                                dve.wait_ge(scored[b], g * CH + c + 1)
                            else:
                                ch.then(ins)
                        if n == LEVELS + 3 and c:
                            src = take(b, c, "state score")
                            dve.wait_ge(chain_s[b], order(CHAIN_S, g, c, 0, LEVELS - 1))
                            nc.vector.tensor_tensor(tmp, src, S[b], ALU.mult).then_inc(used[b], 1)
                            dve.wait_ge(used[b], order(PRODUCTS, g, c, "state score"))
                            nc.vector.tensor_tensor(acc[b], acc[b], tmp, ALU.add).then_inc(scored[b], 1)
                            dve.wait_ge(scored[b], g * CH + c + 1)
                        if n == LEVELS + 5:
                            dve.wait_ge(turned[b], order(TURNS, g, c, "scores"))
                            ch.then(nc.vector.tensor_reduce(nmax[:, b], b3(k.bank[4 * b]), AX.X, ALU.max, negate=True))
                            nc.vector.tensor_scalar(nmax[:, b], nmax[:, b], SLOT_SCALE, None, ALU.mult).then_inc(maxed[b], 1)

                    def outputs_step(n, b, c):
                        g = at[b]
                        if n == 0:
                            dve.wait_ge(kept[b], order(TURNS, g, c, "scores"))
                            ch.then(nc.vector.reciprocal(sums[:, b], sums[:, b]))
                            r = sums[:, b].unsqueeze(2).broadcast_to([P, HG, P])
                            nc.vector.tensor_tensor(acc[b], acc[b], r, ALU.mult).then_inc(normed[b], 1)
                        if n == 3:
                            last_turn = ("decayed", LEVELS if c < CH - 1 else LEVELS - 1)
                            dve.wait_ge(turned[b], order(TURNS, g, c, last_turn))
                            src = chunk(wT, b, c)
                            nc.vector.tensor_copy(halves(U[b], 0)[:, :, :, 1], halves(src, 0)[:, :, :, 1])
                            nc.vector.tensor_tensor(halves(U[b], 0)[:, :, :, 0], halves(src, 0)[:, :, :, 0], decay(b, 0, c, 1), ALU.mult)\
                                .then_inc(chain_v[b], 1)
                        if n == 4:
                            src = take(b, c, "own pair")
                            nc.vector.tensor_tensor(S[b], S[b], chunk(gT, b, c), ALU.mult).then_inc(chain_v[b], 1)
                            nc.vector.tensor_tensor(PT[b], src, eyes, ALU.mult).then_inc(used[b], 1)
                        l = n - 5
                        if l >= 1 and (c, l) in CHAIN_V:
                            dve.wait_ge(chain_v[b], order(CHAIN_V, g, c, l - 1 if l > 1 else "slots"))
                            dve.wait_ge(made[b], order(PRODUCTS, g, c, ("pair", l)))
                            left = halves(U[b], l)[:, :, :, 0]
                            nc.vector.tensor_tensor(left, left, decay(b, l, c, 1), ALU.mult).then_inc(chain_v[b], 1)
                        if 0 <= l < LEVELS:
                            there = dve.to_reg(order(PRODUCTS, g, c, ("pair", l)))
                            before = dve.to_reg(g * len(PRODUCTS) + PRODUCTS.index((c, ("pair", l))))
                            dve.wait_ge(a_const, 8 * 16)
                            dve.wait_ge(made[b], there)
                            dve.wait_ge(used[b], before)
                            src = halves(b3(rbank(b, c, ("pair", l))), l)[:, :, :, 1]
                            nc.vector.copy_predicated(halves(PT[b], l)[:, :, :, 1], mask(l).bitcast(U32), src).then_inc(used[b], 1)
                        if n == LEVELS + 6 and c < CH - 1:
                            dve.wait_ge(paired[b], g * 2 * CH + 2 * c + 2)
                            for half in range(2):
                                dve.wait_ge(made[b], order(PRODUCTS, g, c, f"state {half}"))
                                src = rbank(b, c, f"state {half}")[:].rearrange("p (h n) -> p h n", h=2)
                                for h in (2 * half, 2 * half + 1):
                                    if c:
                                        ins = nc.vector.scalar_tensor_tensor(out=KV[b][:, h], in0=KV[b][:, h], scalar=blocks(b, LEVELS, c)[:, h],
                                                                             in1=src[:, h % 2], op0=ALU.mult, op1=ALU.add)
                                    else:
                                        ins = nc.vector.tensor_copy(KV[b][:, h], src[:, h % 2])
                                ins.then_inc(used[b], 1)

                    for s in range(SLOTS):
                        if s < B * CH:
                            scores_step(0, s % B, s // B)
                        for n in range(STEPS):
                            if s:
                                outputs_step(n, (s - 1) % B, (s - 1) // B)
                            if s < B * CH and n:
                                scores_step(n, s % B, s // B)
                    ch.end()

                    for b in range(B):
                        dve.wait_ge(out_kept[b], g * CH + CH)
                    nc.vector.tensor_scalar(rt_o[:], ss_o[:], 1.0 / P, EPS, ALU.mult, ALU.add).then_inc(o_var, 1)
                    dve.wait_ge(o_root, g + 1)
                    nc.vector.reciprocal(rt_o[:], rt_o[:]).then_inc(o_rstd, 1)
                    dve.wait_ge(o_rstd, g + 1)

                    def bias(t):
                        dve.wait_ge(gate_made, g * NT + t + 1)
                        if t == 0:
                            dve.wait_ge(rest_in, g * 64 + 64)
                        nc.vector.tensor_tensor(gt[t % 2], k.bank[t % 2][:], bg2[:], ALU.add).then_inc(gate_biased, 1)

                    def add(t):
                        dve.wait_ge(y_out, g * NT + t + 1)
                        nc.vector.tensor_tensor(k.x[:, t], k.x[:, t], k.bank[4 + t % 2][:, 0:D], ALU.add).then_inc(x_added, 1)

                    bias(0)
                    for t in range(NT):
                        dve.wait_ge(gate_done, g * NT + t + 1)
                        if t >= 2:
                            dve.wait_ge(y_turned, g * NT + t - 1)
                        for h in range(HG):
                            o = qT[:, t // CH, h, (t % CH) * P:(t % CH + 1) * P]
                            last = nc.vector.scalar_tensor_tensor(out=y[t % 2][:, h], in0=o, scalar=rt_o[:, t, h:h + 1],
                                                                  in1=gt[t % 2][:, h * P:(h + 1) * P], op0=ALU.mult, op1=ALU.mult)
                        last.then_inc(y_ready, 1)
                        if t + 1 < NT:
                            bias(t + 1)
                        if t:
                            add(t - 1)
                    add(NT - 1)


WORK_WORDS = 11776
DVE_CHAIN = B * (CH * LEVELS - 1) + 2 * B * CH


def expert_block(k, rep):
    nc, d = k.nc, k.d
    r = f"_{rep}"
    with ExitStack() as ctx:
        def sb(name, shape, dt=F32):
            return k.sb(name + r, shape, dt, ctx)

        def sem(name):
            return k.sem(name + r)

        HEADS = 4
        BODY = HEADS * B
        hid = sb("hid", [P, NT, D])
        nrm = sb("nrm", [P, NT, D])
        ln = sb("ln", [P, 4, DC])
        ropes = sb("ropes", [P, 4, T])
        causal = sb("causal", [P, P])
        bqkv = sb("bqkv", [P, 3, FH + 1])
        bo = sb("bo", [P, D])
        wqkv = [sb(f"wqkv{n}", [P, 3, DC, P]) for n in range(HEADS)]
        wo = sb("wo", [P, FH, D])
        oT = sb("oT", [P, FH, B * T])

        we1, we2 = sb("we1", [P, E, DC, I]), sb("we2", [P, E, I // P, D])
        wg, be1, be2 = sb("wg", [P, DC, E]), sb("be1", [P, E, I // P]), sb("be2", [E, D])
        f_const, wo_in, m_in = sem("f_const"), sem("wo_in"), sem("m_in")

        def constants_and_weights(sp):
            for n, name in enumerate(("ln1_w", "ln1_b", "ln2_w", "ln2_b")):
                sp.dma_start(ln[:, n], d["f_" + name].rearrange("(c p) -> p c", p=P),
                             allow_slow_non_contiguous=True).then_inc(f_const, 16)
            sp.dma_start(ropes[:], d["c_rope"]).then_inc(f_const, 16)
            sp.dma_start(causal[:], d["c_causal"]).then_inc(f_const, 16)
            for n, name in enumerate(("bq", "bk", "bv")):
                sp.dma_start(bqkv[:, n, 0:FH], d["f_" + name].rearrange("(h p) -> p h", p=P),
                             allow_slow_non_contiguous=True).then_inc(f_const, 16)
            sp.dma_start(bo[:], d["f_bo"].rearrange("(a n) -> a n", a=1).broadcast_to([P, D])).then_inc(f_const, 16)
            sp.dma_start(wo[:], d["f_wo"].rearrange("(h p) n -> p h n", p=P)).then_inc(wo_in, 16)
            sp.dma_start(wg[:], d["f_w_gate"].rearrange("(c p) e -> p c e", p=P)).then_inc(m_in, 16)
            sp.dma_start(we1[:], d["f_we1"].rearrange("e (c p) n -> p e c n", p=P)).then_inc(m_in, 16)
            sp.dma_start(be1[:], d["f_be1"].rearrange("e (c p) -> p e c", p=P), allow_slow_non_contiguous=True).then_inc(m_in, 16)
            sp.dma_start(be2[:], d["f_be2"]).then_inc(m_in, 16)
            sp.dma_start(we2[:], d["f_we2"].rearrange("e (c p) n -> p e c n", p=P)).then_inc(m_in, 16)

        layer_norm(k, k.x, hid, False, loads=constants_and_weights)
        layer_norm(k, hid, nrm, True, ln[:, 0], ln[:, 1], (f_const, 160))

        q_in = [sem(f"q_in{n}") for n in range(HEADS)]
        q_made, q_flat, k_made = sem("q_made"), sem("q_flat"), sem("k_made")
        q_roped, k_roped = sem("q_roped"), sem("k_roped")
        halves_done = [sem(f"halves_done{m}") for m in range(2)]
        v_made, v_kept = sem("v_made"), sem("v_kept")
        s_made, s_max, s_exp = sem("s_made"), sem("s_max"), sem("s_exp")
        s_recip, p_ready = sem("s_recip"), sem("p_ready")
        p_turned, p_kept = sem("p_turned"), sem("p_kept")
        o_made, o_kept = sem("o_made"), sem("o_kept")
        masks_in = sem("masks_in")
        with ExitStack() as inner:
            def tb(name, shape):
                return k.sb(name + r, shape, F32, inner)

            rot = [[tb(f"rot{n}_{m}", [P, T]) for m in range(2)] for n in range(2)]
            part = [tb(f"rpart{n}", [P, T]) for n in range(2)]
            flat = tb("q_plain", [P, T])
            vv = [tb(f"vv{n}", [P, CH, P]) for n in range(2)]
            pr = [tb(f"pr{n}", [P, T]) for n in range(2)]
            pT = [tb(f"pT{n}", [P, CH, T]) for n in range(2)]
            nmax = tb("nmaxf", [P, 2])
            rs = tb("rs", [P, 2])
            eye_b = k.sb("eye_b" + r, [P, P], BF16, inner)
            causal_b = k.sb("causal_b" + r, [P, P], BF16, inner)

            def keep_o(act, u, g):
                n, b = u // B, u % B
                act.wait_ge(f_const, 160)
                act.wait_ge(o_made, g * BODY + u + 1)
                out = oT[:, bass.ds(g * HEADS + n, 1), b * T:(b + 1) * T].rearrange("p h t -> p (h t)")
                nc.scalar.activation(out, k.bank[6][:], ACT.Identity, bias=bqkv[:, 2, bass.ds(g * HEADS + n, 1)]).then_inc(o_kept, 1)
            with nc.Block() as block:
                @block.sync
                def _(sp):
                    def load(head, n):
                        for m, name in enumerate(("f_wq", "f_wk", "f_wv")):
                            w = d[name].rearrange("(c p) (h n) -> h p c n", p=P, n=P)[bass.ds(head, 1)]
                            sp.dma_start(wqkv[n][:, m], w.rearrange("h p c n -> (h p) c n")).then_inc(q_in[n], 16)

                    for n in range(HEADS):
                        load(n, n)
                    with sp.Fori(0, FH // HEADS - 1) as g:
                        for n in range(HEADS):
                            sp.wait_ge(v_made, g * BODY + n * B + B)
                            load(g * HEADS + HEADS + n, n)
                    sp.wait_ge(v_made, FH * B - B)
                    load(0, 0)

                @block.tensor
                def _(pe):
                    def project(g, u, m):
                        n, b = u // B % HEADS, u % B
                        if m == 0 and b == 0:
                            pe.wait_ge(q_in[n], (g + u // BODY) * 48 + 48)
                        if u:
                            pe.wait_ge((q_flat, k_roped)[m], g * BODY + u)
                        for c in range(DC):
                            last = nc.tensor.matmul(k.bank[(0, 7)[m]][:], wqkv[n][:, m, c, :], k.xT[:, c, b * T:(b + 1) * T],
                                                    start=(c == 0), stop=(c == DC - 1))
                        last.then_inc((q_made, k_made)[m], 1)

                    def values(g, u):
                        n, b = u // B % HEADS, u % B
                        if u:
                            pe.wait_ge(v_kept, g * BODY + u)
                        for t in range(CH):
                            for c in range(DC):
                                last = nc.tensor.matmul(k.bank[1][:, t * P:(t + 1) * P], k.xT[:, c, b * T + t * P:b * T + (t + 1) * P],
                                                        wqkv[n][:, 2, c, :], start=(c == 0), stop=(c == DC - 1))
                        last.then_inc(v_made, 1)

                    pe.wait_ge(masks_in, 2)
                    project(0, 0, 0)
                    project(0, 0, 1)
                    values(0, 0)
                    with pe.Fori(0, FH // HEADS) as g:
                        def scores(u, n):
                            i, qt = u * CH + n, CH - 1 - n
                            if n == 0:
                                pe.wait_ge(q_roped, g * BODY + u + 1)
                                pe.wait_ge(k_roped, g * BODY + u + 1)
                            q, kk = rot[u % 2]
                            if i >= 2:
                                pe.wait_ge(s_exp, g * BODY * CH + i - 1)
                            nc.tensor.matmul(k.bank[2 + i % 2][:, 0:(qt + 1) * P], q[:, qt * P:(qt + 1) * P],
                                             kk[:, 0:(qt + 1) * P], start=True, stop=False)
                            nc.tensor.matmul(k.bank[2 + i % 2][:, qt * P:(qt + 1) * P], eye_b[:], causal_b[:],
                                             start=False, stop=True).then_inc(s_made, 1)

                        def turn(u, n):
                            i, qt = u * CH + n, CH - 1 - n
                            pe.wait_ge(p_ready, g * BODY * CH + i + 1)
                            if i >= 2:
                                pe.wait_ge(p_kept, g * BODY * CH + i - 1)
                            for t in range(qt + 1):
                                last = nc.tensor.transpose(k.bank[4 + i % 2][:, t * P:(t + 1) * P],
                                                           pr[i % 2][:, t * P:(t + 1) * P], k.eye[:])
                            last.then_inc(p_turned, 1)

                        def outputs(u):
                            pe.wait_ge(p_kept, (g * BODY + u + 1) * CH)
                            pe.wait_ge(v_kept, g * BODY + u + 1)
                            if u >= 1:
                                pe.wait_ge(o_kept, g * BODY + u + 1)
                            for t in range(CH):
                                last = nc.tensor.matmul(k.bank[6][:, t * P:], vv[u % 2][:, t, :], pT[u % 2][:, t, t * P:],
                                                        start=(t == 0), stop=(t == CH - 1))
                            last.then_inc(o_made, 1)

                        pe.wait_ge(o_kept, g * BODY + 1)
                        for u in range(BODY):
                            scores(u, 0)
                            scores(u, 1)
                            project(g, u + 1, 0)
                            project(g, u + 1, 1)
                            if u:
                                outputs(u - 1)
                            turn(u, 0)
                            scores(u, 2)
                            turn(u, 1)
                            scores(u, 3)
                            values(g, u + 1)
                            turn(u, 2)
                            turn(u, 3)
                        outputs(BODY - 1)

                @block.vector
                def _(dve):
                    def rope_k(g, u):
                        n = u // B
                        dve.wait_ge(k_made, g * BODY + u + 1)
                        src, out, half = k.bank[7], rot[u % 2][1], P // 2
                        bias = bqkv[:, 1, bass.ds(g * HEADS + n, 1)]
                        nc.vector.scalar_tensor_tensor(out=out[:], in0=src[:], scalar=bias, in1=ropes[:, 2],
                                                       op0=ALU.add, op1=ALU.mult)
                        for lo in (0, half):
                            last = nc.vector.scalar_tensor_tensor(
                                out=part[1][half - lo:P - lo, :], in0=src[lo:lo + half, :],
                                scalar=bqkv[lo:lo + half, 1, bass.ds(g * HEADS + n, 1)],
                                in1=ropes[lo:lo + half, 3], op0=ALU.add, op1=ALU.mult)
                        last.then_inc(halves_done[1], 1)
                        dve.wait_ge(halves_done[1], g * BODY + u + 1)
                        nc.vector.tensor_tensor(out[:], out[:], part[1][:], ALU.add).then_inc(k_roped, 1)
                        dve.wait_ge(k_roped, g * BODY + u + 1)

                    nc.vector.tensor_copy(eye_b[:], k.eye[:]).then_inc(masks_in, 1)
                    nc.vector.tensor_copy(causal_b[:], causal[:]).then_inc(masks_in, 1)
                    nc.vector.memset(bqkv[:, :, FH:FH + 1], 0.0).then_inc(masks_in, 1)
                    dve.wait_ge(f_const, 160)
                    dve.wait_ge(masks_in, 3)

                    rope_k(0, 0)
                    with dve.Fori(0, FH // HEADS) as g:
                        def maximum(u, n):
                            i, qt = u * CH + n, CH - 1 - n
                            dve.wait_ge(s_made, g * BODY * CH + i + 1)
                            if i >= 2:
                                dve.wait_ge(s_exp, g * BODY * CH + i - 1)
                            nc.vector.tensor_reduce(nmax[:, i % 2:i % 2 + 1], k.bank[2 + i % 2][:, 0:(qt + 1) * P], AX.X, ALU.max,
                                                    negate=True).then_inc(s_max, 1)

                        def normalise(u, n):
                            i, qt = u * CH + n, CH - 1 - n
                            dve.wait_ge(s_exp, g * BODY * CH + i + 1)
                            nc.vector.reciprocal(rs[:, i % 2:i % 2 + 1], rs[:, i % 2:i % 2 + 1]).then_inc(s_recip, 1)
                            dve.wait_ge(s_recip, g * BODY * CH + i + 1)
                            nc.vector.tensor_scalar(pr[i % 2][:, 0:(qt + 1) * P], pr[i % 2][:, 0:(qt + 1) * P], rs[:, i % 2:i % 2 + 1],
                                                    None, ALU.mult).then_inc(p_ready, 1)

                        for u in range(BODY):
                            maximum(u, 0)
                            maximum(u, 1)
                            normalise(u, 0)
                            normalise(u, 1)
                            rope_k(g, u + 1)
                            maximum(u, 2)
                            normalise(u, 2)
                            maximum(u, 3)
                            normalise(u, 3)

                @block.gpsimd
                def _(pool):
                    def rope_q(g, u):
                        pool.wait_ge(q_flat, g * BODY + u + 1)
                        out, half = rot[u % 2][0], P // 2
                        nc.gpsimd.tensor_tensor(out[:], flat[:], ropes[:, 0], ALU.mult).then_inc(halves_done[0], 1)
                        for i, lo in enumerate((0, half)):
                            pool.wait_ge(halves_done[0], (g * BODY + u) * 3 + i + 1)
                            nc.gpsimd.tensor_tensor(part[0][half - lo:P - lo, :], flat[lo:lo + half, :],
                                                    ropes[lo:lo + half, 1], ALU.mult).then_inc(halves_done[0], 1)
                        pool.wait_ge(halves_done[0], (g * BODY + u) * 3 + 3)
                        nc.gpsimd.tensor_tensor(out[:], out[:], part[0][:], ALU.add).then_inc(q_roped, 1)
                        pool.wait_ge(q_roped, g * BODY + u + 1)

                    pool.wait_ge(f_const, 160)
                    rope_q(0, 0)
                    with pool.Fori(0, FH // HEADS) as g:
                        for u in range(BODY):
                            rope_q(g, u + 1)

                @block.scalar
                def _(act):
                    def keep_q(g, u):
                        made = act.to_reg(g * BODY + u + 1)
                        act.wait_ge(f_const, 160)
                        act.wait_ge(masks_in, 3)
                        act.wait_ge(q_made, made)
                        nc.scalar.activation(flat[:], k.bank[0][:], ACT.Identity, bias=bqkv[:, 0, bass.ds(g * HEADS + u // B, 1)]).then_inc(q_flat, 1)

                    def keep_v(g, u):
                        act.wait_ge(v_made, g * BODY + u + 1)
                        if u >= 2:
                            act.wait_ge(o_made, g * BODY + u - 1)
                        nc.scalar.activation(vv[u % 2][:].rearrange("p t n -> p (t n)"), k.bank[1][:], ACT.Copy).then_inc(v_kept, 1)

                    act.sem_inc(o_kept, 1)
                    act.wait_ge(masks_in, 3)
                    keep_q(0, 0)
                    keep_v(0, 0)
                    with act.Fori(0, FH // HEADS) as g:
                        def exps(u, n):
                            i, qt = u * CH + n, CH - 1 - n
                            act.wait_ge(s_max, g * BODY * CH + i + 1)
                            if i >= 2:
                                act.wait_ge(p_turned, g * BODY * CH + i - 1)
                            nc.scalar.activation(pr[i % 2][:, 0:(qt + 1) * P], k.bank[2 + i % 2][:, 0:(qt + 1) * P], ACT.Exp,
                                                 bias=nmax[:, i % 2:i % 2 + 1], accum_out=rs[:, i % 2:i % 2 + 1]).then_inc(s_exp, 1)

                        def keep_p(u, n):
                            i, qt = u * CH + n, CH - 1 - n
                            act.wait_ge(p_turned, g * BODY * CH + i + 1)
                            nc.scalar.activation(pT[u % 2][:, 0:qt + 1, qt * P:(qt + 1) * P],
                                                 k.bank[4 + i % 2][:, 0:(qt + 1) * P].rearrange("p (t n) -> p t n", n=P),
                                                 ACT.Copy).then_inc(p_kept, 1)

                        for u in range(BODY):
                            exps(u, 0)
                            exps(u, 1)
                            keep_q(g, u + 1)
                            if u:
                                keep_o(act, u - 1, g)
                            keep_p(u, 0)
                            exps(u, 2)
                            keep_p(u, 1)
                            exps(u, 3)
                            keep_v(g, u + 1)
                            keep_p(u, 2)
                            keep_p(u, 3)
                        keep_o(act, BODY - 1, g)

        out_made, h_added = sem("out_made"), sem("h_added")
        hid_biased = sem("hid_biased")
        with nc.Block() as block:
            @block.tensor
            def _(pe):
                pe.wait_ge(wo_in, 16)
                for t in range(NT):
                    if t >= 4:
                        pe.wait_ge(h_added, t - 3)
                    for h in range(FH):
                        last = nc.tensor.matmul(k.bank[t % 4][:, 0:D], oT[:, h, t * P:(t + 1) * P], wo[:, h, :],
                                                start=(h == 0), stop=(h == FH - 1))
                    last.then_inc(out_made, 1)

            @block.vector
            def _(dve):
                nc.vector.tensor_tensor(hid[:], hid[:], bo[:].unsqueeze(1).broadcast_to([P, NT, D]), ALU.add).then_inc(hid_biased, 1)
                dve.wait_ge(hid_biased, 1)
                for t in range(NT):
                    dve.wait_ge(out_made, t + 1)
                    nc.vector.tensor_tensor(hid[:, t], hid[:, t], k.bank[t % 4][:, 0:D], ALU.add).then_inc(h_added, 1)
                dve.wait_ge(h_added, NT)
                nc.vector.tensor_tensor(k.x[:], k.x[:], hid[:], ALU.add)

        layer_norm(k, hid, nrm, True, ln[:, 2], ln[:, 3], (f_const, 160))
        with ExitStack() as inner:
            def tb(name, shape):
                return k.sb(name + r, shape, F32, inner)

            raw, gap, comb = tb("raw", [P, NT, E]), tb("gap", [P, NT, E]), tb("comb", [P, NT, E])
            gap2 = tb("gap2", [P, NT, E])
            top, tot = tb("top", [P, NT]), tb("tot", [P, NT])
            beat = tb("beat", [P, NT, E, E])
            combT = tb("combT", [E, B * T])
            hm = [tb(f"hm{n}", [P, I // P, B * T]) for n in range(2)]
            logits, chain_m, exped, combed, comb_turned, comb_kept = (sem(n) for n in ("logits", "chain_m", "exped", "combed", "comb_turned", "comb_kept"))
            h_made, h_kept, y_made, y_used = (sem(n) for n in ("h_made", "h_kept", "y_made", "y_used"))
            IC = I // P
            with nc.Block() as block:
                @block.tensor
                def _(pe):
                    pe.wait_ge(m_in, 80)
                    for t in range(NT):
                        for c in range(DC):
                            last = nc.tensor.matmul(k.bank[0][:, t * E:(t + 1) * E], k.xT[:, c, t * P:(t + 1) * P], wg[:, c, :],
                                                    start=(c == 0), stop=(c == DC - 1))
                    last.then_inc(logits, 1)

                    def hidden(e):
                        for i in range(2 * IC):
                            ic, half = i // 2, i % 2
                            n = e * 2 * IC + i
                            if n >= 2:
                                pe.wait_ge(h_kept, n - 1)
                            for c in range(DC):
                                last = nc.tensor.matmul(k.bank[4 + n % 2][:], we1[:, e, c, ic * P:(ic + 1) * P],
                                                        k.xT[:, c, half * 512:half * 512 + 512], start=(c == 0), stop=(c == DC - 1))
                            last.then_inc(h_made, 1)

                    def result(n, pairs):
                        if n >= 2:
                            pe.wait_ge(y_used, n - 1)
                        for i, (lhsT, rhs) in enumerate(pairs):
                            last = nc.tensor.matmul(k.bank[6 + n % 2][:, 0:D], lhsT, rhs, start=(i == 0), stop=(i == len(pairs) - 1))
                        last.then_inc(y_made, 1)

                    hidden(0)
                    hidden(1)
                    pe.wait_ge(combed, 1)
                    for t in range(NT):
                        last = nc.tensor.transpose(k.bank[1 + t // 4][0:E, (t % 4) * P:(t % 4 + 1) * P], comb[:, t, :], k.eye[:])
                    last.then_inc(comb_turned, 1)
                    pe.wait_ge(comb_kept, 1)
                    for t in range(NT):
                        result(t, [(combT[:, t * P:(t + 1) * P], be2[:])])
                    for e in range(E):
                        pe.wait_ge(h_kept, (e + 1) * 2 * IC)
                        for t in range(NT):
                            result((e + 1) * NT + t, [(hm[e % 2][:, ic, t * P:(t + 1) * P], we2[:, e, ic, :]) for ic in range(IC)])
                        if e + 2 < E:
                            hidden(e + 2)

                @block.scalar
                def _(act):
                    act.wait_ge(exped, 1)
                    nc.scalar.activation(raw[:], gap[:], ACT.Exp).then_inc(exped, 1)
                    act.wait_ge(exped, 3)
                    nc.scalar.activation(comb[:], gap[:], ACT.Exp).then_inc(exped, 1)
                    for e in range(E):
                        if e == 2:
                            act.wait_ge(comb_turned, 1)
                            for n in range(2):
                                last = nc.scalar.activation(combT[:, n * 512:n * 512 + 512], k.bank[1 + n][0:E, :], ACT.Copy)
                            last.then_inc(comb_kept, 1)
                        for i in range(2 * IC):
                            ic, half = i // 2, i % 2
                            n = e * 2 * IC + i
                            act.wait_ge(h_made, n + 1)
                            if e >= 2:
                                act.wait_ge(y_made, e * NT)
                            nc.scalar.activation(hm[e % 2][:, ic, half * 512:half * 512 + 512], k.bank[4 + n % 2][:], ACT.Gelu,
                                                 bias=be1[:, e, ic:ic + 1]).then_inc(h_kept, 1)

                @block.vector
                def _(dve):
                    count = [0]

                    def then(ins):
                        count[0] += 1
                        ins.then_inc(chain_m, 1)
                        dve.wait_ge(chain_m, count[0])

                    def wide(ap):
                        return ap.unsqueeze(2).broadcast_to([P, NT, E])

                    dve.wait_ge(logits, 1)
                    lg = k.bank[0][:, 0:NT * E].rearrange("p (t e) -> p t e", e=E)
                    then(nc.vector.tensor_reduce(top[:], lg, AX.X, ALU.max))
                    nc.vector.tensor_tensor(gap[:], lg, wide(top[:]), ALU.subtract).then_inc(exped, 1)
                    dve.wait_ge(exped, 2)
                    then(nc.vector.tensor_reduce(tot[:], raw[:], AX.X, ALU.add))
                    then(nc.vector.reciprocal(tot[:], tot[:]))
                    then(nc.vector.tensor_tensor(raw[:], raw[:], wide(tot[:]), ALU.mult))
                    then(nc.vector.tensor_reduce(top[:], raw[:], AX.X, ALU.max))
                    nc.vector.tensor_tensor(gap[:], raw[:], wide(top[:]), ALU.subtract).then_inc(exped, 1)
                    then(nc.vector.memset(beat[:], 0.0))
                    for e in range(E):
                        if e:
                            last = nc.vector.tensor_tensor(beat[:, :, e, 0:e], raw[:, :, 0:e], raw[:, :, e:e + 1].broadcast_to([P, NT, e]), ALU.is_ge)
                        if e < E - 1:
                            last = nc.vector.tensor_tensor(beat[:, :, e, e + 1:E], raw[:, :, e + 1:E], raw[:, :, e:e + 1].broadcast_to([P, NT, E - 1 - e]), ALU.is_gt)
                    then(last)
                    then(nc.vector.tensor_reduce(gap2[:], beat[:], AX.X, ALU.add))
                    then(nc.vector.tensor_scalar(gap2[:], gap2[:], TOPK - 0.5, None, ALU.is_lt))
                    dve.wait_ge(exped, 4)
                    then(nc.vector.tensor_tensor(comb[:], comb[:], gap2[:], ALU.mult))
                    then(nc.vector.tensor_reduce(tot[:], comb[:], AX.X, ALU.add))
                    then(nc.vector.reciprocal(tot[:], tot[:]))
                    nc.vector.tensor_tensor(comb[:], comb[:], wide(tot[:]), ALU.mult).then_inc(combed, 1)
                    dve.wait_ge(combed, 1)
                    for n in range((E + 1) * NT):
                        t = n % NT
                        dve.wait_ge(y_made, n + 1)
                        if n >= NT:
                            dve.wait_ge(y_used, n - NT + 1)
                            nc.vector.scalar_tensor_tensor(out=k.x[:, t], in0=k.bank[6 + n % 2][:, 0:D], scalar=comb[:, t, n // NT - 1:n // NT],
                                                           in1=k.x[:, t], op0=ALU.mult, op1=ALU.add).then_inc(y_used, 1)
                        else:
                            nc.vector.tensor_tensor(k.x[:, t], k.x[:, t], k.bank[6 + n % 2][:, 0:D], ALU.add).then_inc(y_used, 1)


HEAD_ROWS = 32
QUERY_PARTS, KEY_PARTS = (0, 0, 0, 1, 1, 2), (0, 1, 2, 0, 1, 0)
ROWS = len(QUERY_PARTS) * BD
BATCH_UNITS, HEAD_UNITS = CH, B * CH
CU = 4 * HEAD_UNITS
AHEAD = 3


def full_attention(k):
    nc, d = k.nc, k.d
    with ExitStack() as ctx:
        def sb(name, shape, dt=F32):
            return k.sb(name, shape, dt, ctx)

        sem = k.sem
        nrm = sb("c_nrm", [P, NT, D])
        brope, turn_m = sb("brope", [P, 2, T]), sb("turn_m", [P, P])
        wqk = [sb(f"c_w{n}", [P, DC, BT * P]) for n in "qk"]
        wv, wout = sb("c_wv", [P, DC, D]), sb("c_wout", [P, BT, D])
        bqk = sb("c_bqk", [P, 2, BT])
        bv, bout = sb("c_bv", [P, D]), sb("c_bout", [P, D])
        split = [[sb(f"c_split{m}{n}", [P, BT, B * T], BF16) for n in range(3)] for m in range(2)]
        v = sb("c_v", [P, NT, BH, HEAD_ROWS])
        oT = sb("c_oT", [P, BT, B * T])
        placed = [[sb(f"c_placed{m}{h}", [ROWS, B * T], BF16) for h in range(4)] for m in range(2)]
        vj = [sb(f"c_vj{b}", [P, CH, P]) for b in range(B)]
        c_in = sem("c_in")

        def constants_and_weights(sp):
            for dst, src in ((wqk[0], "b_q_w"), (wqk[1], "b_k_w"), (wv, "b_v_w"), (wout, "b_out_w")):
                sp.dma_start(dst[:], d[src].rearrange("(c p) n -> p c n", p=P)).then_inc(c_in, 16)
            for n, name in enumerate(("b_q_b", "b_k_b")):
                sp.dma_start(bqk[:, n], d[name].rearrange("(j p) -> p j", p=P), allow_slow_non_contiguous=True).then_inc(c_in, 16)
            for dst, name in ((bv, "b_v_b"), (bout, "b_out_b")):
                sp.dma_start(dst[:], d[name].rearrange("(a n) -> a n", a=1).broadcast_to([P, D])).then_inc(c_in, 16)
            sp.dma_start(brope[:], d["c_brope"]).then_inc(c_in, 16)
            sp.dma_start(turn_m[:], d["c_turn"]).then_inc(c_in, 16)

        layer_norm(k, k.x, nrm, True, loads=constants_and_weights)

        flat = [sb(f"c_flat{n}", [P, T]) for n in range(3)]
        cs, sn = ([sb(f"c_{a}{n}", [P, T]) for n in range(2)] for a in ("cs", "sn"))
        full, rest = ([sb(f"c_{a}{n}", [P, T]) for n in range(4)] for a in ("full", "rest"))
        pr = [sb(f"c_pr{n}", [P, T]) for n in range(4)]
        pT = [sb(f"c_pT{n}", [P, CH, T]) for n in range(2)]
        nmax, rs = sb("c_nmax", [P, 4]), sb("c_rs", [P, 4])
        c_proj, biased, c_turned, c_cos, c_sin, c_roped = (sem(f"c_{n}") for n in ("proj", "biased", "turned", "cos", "sin", "roped"))
        part_sem = [sem(f"c_part{n}") for n in range(3)]
        c_rest, v_zero, c_vmade, c_vkept, x_biased = (sem(f"c_{n}") for n in ("rest", "v_zero", "vmade", "vkept", "x_biased"))
        parts = [(j, m, b) for j in range(BT) for m in range(2) for b in range(B)]
        NPART = len(parts)
        head_in = [sem(f"c_head_in{h}") for h in range(4)]
        v_in = [sem(f"c_v_in{b}") for b in range(B)]
        made, maxed, exped, recip, pturned, weighed, o_kept, done, added = (
            sem(f"c_{n}") for n in ("made", "maxed", "exped", "recip", "pturned", "weighed", "o_kept", "done", "added"))
        normed = [sem(f"c_normed{n}") for n in range(2)]
        pkept = [sem(f"c_pkept{n}") for n in range(2)]
        LOADS = 2 * len(QUERY_PARTS)
        with nc.Block() as block:
            @block.sync
            def _(sp):
                def load_head(j, h):
                    for m, which in enumerate((QUERY_PARTS, KEY_PARTS)):
                        for r, part in enumerate(which):
                            src = split[m][part][h * HEAD_ROWS:h * HEAD_ROWS + BD, bass.ds(j, 1), :]
                            sp.dma_start(placed[m][h][r * BD:(r + 1) * BD, :], src.rearrange("p j n -> p (j n)")).then_inc(head_in[h], 16)

                def load_values(j, b):
                    src = v[:, b * CH:(b + 1) * CH].rearrange("p t h n -> p t (h n)")[:, :, bass.ds(j * P, P)]
                    sp.dma_start(vj[b][:], src).then_inc(v_in[b], 16)

                for n in range(3):
                    sp.wait_ge(part_sem[n], 2 * B)
                for h in range(4):
                    load_head(0, h)
                sp.wait_ge(c_vkept, NT)
                for b in range(B):
                    load_values(0, b)
                for n in range(3):
                    sp.wait_ge(part_sem[n], NPART)
                with sp.Fori(0, BT - 1) as g:
                    for h in range(4):
                        sp.wait_ge(made, g * CU + (h + 1) * HEAD_UNITS)
                        load_head(g + 1, h)
                    for b in range(B):
                        sp.wait_ge(weighed, g * 4 * B + 3 * B + b + 1)
                        load_values(g + 1, b)

            @block.tensor
            def _(pe):
                pe.wait_ge(c_in, 160)

                def project(i):
                    j, m, b = parts[i]
                    if i >= 2:
                        pe.wait_ge(biased, i - 1)
                    for c in range(DC):
                        last = nc.tensor.matmul(k.bank[i % 2][:], wqk[m][:, c, j * P:(j + 1) * P], k.xT[:, c, b * T:(b + 1) * T],
                                                start=(c == 0), stop=(c == DC - 1))
                    last.then_inc(c_proj, 1)

                project(0)
                for i in range(NPART):
                    if i + 1 < NPART:
                        project(i + 1)
                    pe.wait_ge(biased, i + 1)
                    if i >= 2:
                        pe.wait_ge(c_sin, i - 1)
                    nc.tensor.matmul(k.bank[2 + i % 2][:], turn_m[:], flat[i % 3][:], start=True, stop=True).then_inc(c_turned, 1)
                for t in range(NT):
                    if t >= 2:
                        pe.wait_ge(c_vkept, t - 1)
                    for c in range(DC):
                        last = nc.tensor.matmul(k.bank[4 + t % 2][:, 0:D], k.xT[:, c, t * P:(t + 1) * P], wv[:, c, :],
                                                start=(c == 0), stop=(c == DC - 1))
                    last.then_inc(c_vmade, 1)
                pe.wait_ge(c_vkept, NT)
                pe.wait_ge(c_sin, NPART)

                with pe.Fori(0, BT) as g:
                    def scores(u):
                        h, b, t = u // HEAD_UNITS, u // CH % B, u % CH
                        if u % HEAD_UNITS == 0:
                            pe.wait_ge(head_in[h], g * LOADS * 16 + LOADS * 16)
                        if u >= 3:
                            pe.wait_ge(exped, g * CU + u - 2)
                        q = placed[0][h][:, b * T + t * P:b * T + (t + 1) * P]
                        nc.tensor.matmul(k.bank[u % 3][:], q, placed[1][h][:, b * T:(b + 1) * T], start=True, stop=True).then_inc(made, 1)

                    def turn(u):
                        pe.wait_ge(normed[u % 2], g * (CU // 2) + u // 2 + 1)
                        if u >= 3:
                            w = u - 3
                            if w % 4 == 3:
                                pe.wait_ge(pkept[1], g * (CU // 4) + w // 4 + 1)
                            else:
                                pe.wait_ge(pkept[0], g * (CU // 4 * 3) + w // 4 * 3 + w % 4 + 1)
                        for c in range(CH):
                            last = nc.tensor.transpose(k.bank[3 + u % 3][:, c * P:(c + 1) * P], pr[u % 4][:, c * P:(c + 1) * P], k.eye[:])
                        last.then_inc(pturned, 1)

                    def outputs(m):
                        h, b = m // B, m % B
                        pe.wait_ge(pkept[0], g * (CU // 4 * 3) + 3 * m + 3)
                        pe.wait_ge(pkept[1], g * (CU // 4) + m + 1)
                        if h == 0:
                            pe.wait_ge(v_in[b], g * 16 + 16)
                            pe.wait_ge(o_kept, g * 2 + b + 1)
                        rows = slice(h * HEAD_ROWS, (h + 1) * HEAD_ROWS)
                        for c in range(CH):
                            last = nc.tensor.matmul(k.bank[6 + b][rows, :], vj[b][:, c, rows], pT[m % 2][:, c, :],
                                                    start=(c == 0), stop=(c == CH - 1))
                        last.then_inc(weighed, 1)

                    for n in range(CU + AHEAD + 1):
                        if n < CU:
                            scores(n)
                        if AHEAD <= n < CU + AHEAD:
                            turn(n - AHEAD)
                        m = (n - AHEAD - 1) // CH - 1
                        if m >= 0 and (n - AHEAD - 1) % CH == 0:
                            outputs(m)
                    outputs(4 * B - 1)

                pe.wait_ge(o_kept, 2 * BT + 2)
                for t in range(NT):
                    if t >= 4:
                        pe.wait_ge(added, t - 3)
                    for j in range(BT):
                        last = nc.tensor.matmul(k.bank[t % 4][:, 0:D], oT[:, j, t * P:(t + 1) * P], wout[:, j, :], start=(j == 0), stop=(j == BT - 1))
                    last.then_inc(done, 1)

            @block.scalar
            def _(act):
                act.wait_ge(c_in, 160)
                for n in range(NPART + 2):
                    if n < NPART:
                        j, m, b = parts[n]
                        act.wait_ge(c_proj, n + 1)
                        if n >= 3:
                            act.wait_ge(c_turned, n - 2)
                            act.wait_ge(c_cos, n - 2)
                        nc.scalar.activation(flat[n % 3][:], k.bank[n % 2][:], ACT.Identity, bias=bqk[:, m, j:j + 1]).then_inc(biased, 1)
                    if 1 <= n <= NPART:
                        j, m, b = parts[n - 1]
                        act.wait_ge(c_roped, n)
                        nc.scalar.activation(split[m][0][:, j, b * T:(b + 1) * T], full[(n - 1) % 4][:], ACT.Copy,
                                             scale=(B_SCALE, 1.0)[m]).then_inc(part_sem[0], 1)
                    if n >= 2:
                        j, m, b = parts[n - 2]
                        act.wait_ge(c_rest, n - 1)
                        nc.scalar.activation(split[m][1][:, j, b * T:(b + 1) * T], rest[(n - 2) % 4][:], ACT.Copy).then_inc(part_sem[1], 1)

                with act.Fori(0, BT) as g:
                    def keep(u):
                        m, t = u // CH, u % CH
                        act.wait_ge(pturned, g * CU + u + 1)
                        if m >= 2:
                            act.wait_ge(weighed, g * 4 * B + m - 1)
                        nc.scalar.activation(pT[m % 2][:, :, t * P:(t + 1) * P], k.bank[3 + u % 3][:].rearrange("p (c n) -> p c n", c=CH),
                                             ACT.Copy).then_inc(pkept[0], 1)

                    for n in range(CU + AHEAD + 1):
                        if n < CU:
                            act.wait_ge(maxed, g * CU + n + 1)
                            if n >= 4:
                                act.wait_ge(pturned, g * CU + n - 3)
                            nc.scalar.activation(pr[n % 4][:], k.bank[n % 3][:], ACT.Exp, bias=nmax[:, n % 4:n % 4 + 1],
                                                 accum_out=rs[:, n % 4:n % 4 + 1]).then_inc(exped, 1)
                        u = n - AHEAD - 1
                        if u >= 0 and u % 4 != 3:
                            keep(u)

            @block.gpsimd
            def _(pool):
                nc.gpsimd.memset(v[:], 0.0).then_inc(v_zero, 1)
                pool.wait_ge(c_in, 160)
                for n in range(NPART + 2):
                    if n < NPART:
                        pool.wait_ge(biased, n + 1)
                        if n >= 2:
                            pool.wait_ge(c_roped, n - 1)
                        nc.gpsimd.tensor_tensor(cs[n % 2][:], flat[n % 3][:], brope[:, 0], ALU.mult).then_inc(c_cos, 1)
                    if n >= 2:
                        j, m, b = parts[n - 2]
                        pool.wait_ge(part_sem[1], n - 1)
                        nc.gpsimd.tensor_tensor(split[m][2][:, j, b * T:(b + 1) * T], rest[(n - 2) % 4][:],
                                                split[m][1][:, j, b * T:(b + 1) * T], ALU.subtract).then_inc(part_sem[2], 1)
                for t in range(NT):
                    nc.gpsimd.tensor_tensor(k.x[:, t], k.x[:, t], bout[:], ALU.add).then_inc(x_biased, 1)
                with pool.Fori(0, BT) as g:
                    for u in range(0, CU, 2):
                        pool.wait_ge(recip, g * CU + u + 1)
                        nc.gpsimd.tensor_tensor(pr[u % 4][:], pr[u % 4][:], rs[:, u % 4:u % 4 + 1].broadcast_to([P, T]), ALU.mult)\
                            .then_inc(normed[0], 1)

            @block.vector
            def _(dve):
                dve.sem_inc(o_kept, 2)
                dve.wait_ge(c_in, 160)
                for n in range(NPART + 1):
                    if n < NPART:
                        dve.wait_ge(c_turned, n + 1)
                        if n >= 2:
                            dve.wait_ge(c_roped, n - 1)
                        nc.vector.tensor_tensor(sn[n % 2][:], k.bank[2 + n % 2][:], brope[:, 1], ALU.mult).then_inc(c_sin, 1)
                        dve.wait_ge(c_sin, n + 1)
                        dve.wait_ge(c_cos, n + 1)
                        if n >= 4:
                            dve.wait_ge(c_rest, n - 3)
                        nc.vector.tensor_tensor(full[n % 4][:], cs[n % 2][:], sn[n % 2][:], ALU.add).then_inc(c_roped, 1)
                    if n >= 1:
                        i = n - 1
                        j, m, b = parts[i]
                        dve.wait_ge(part_sem[0], i + 1)
                        dve.wait_ge(c_roped, i + 1)
                        if i >= 4:
                            dve.wait_ge(part_sem[2], i - 3)
                        nc.vector.scalar_tensor_tensor(out=rest[i % 4][:], in0=full[i % 4][:], scalar=(B_SCALE, 1.0)[m],
                                                       in1=split[m][0][:, j, b * T:(b + 1) * T], op0=ALU.mult, op1=ALU.subtract).then_inc(c_rest, 1)
                dve.wait_ge(v_zero, 1)
                for t in range(NT):
                    dve.wait_ge(c_vmade, t + 1)
                    nc.vector.tensor_tensor(v[:, t, :, 0:BD], k.bank[4 + t % 2][:, 0:D].rearrange("p (h n) -> p h n", n=BD),
                                            bv[:].rearrange("p (h n) -> p h n", n=BD), ALU.add).then_inc(c_vkept, 1)

                with dve.Fori(0, BT) as g:
                    def keep(u):
                        m, t = u // CH, u % CH
                        dve.wait_ge(pturned, g * CU + u + 1)
                        if m >= 2:
                            dve.wait_ge(weighed, g * 4 * B + m - 1)
                        nc.vector.tensor_copy(pT[m % 2][:, :, t * P:(t + 1) * P], k.bank[3 + u % 3][:].rearrange("p (c n) -> p c n", c=CH))\
                            .then_inc(pkept[1], 1)

                    for n in range(CU + AHEAD + 1):
                        if n < CU:
                            dve.wait_ge(made, g * CU + n + 1)
                            nc.vector.tensor_reduce(nmax[:, n % 4:n % 4 + 1], k.bank[n % 3][:], AX.X, ALU.max, negate=True).then_inc(maxed, 1)
                        if 1 <= n <= CU:
                            i = (n - 1) % 4
                            dve.wait_ge(exped, g * CU + n)
                            nc.vector.reciprocal(rs[:, i:i + 1], rs[:, i:i + 1]).then_inc(recip, 1)
                            if i % 2:
                                dve.wait_ge(recip, g * CU + n)
                                nc.vector.tensor_scalar(pr[i][:], pr[i][:], rs[:, i:i + 1], None, ALU.mult).then_inc(normed[1], 1)
                        u = n - AHEAD - 1
                        if u >= 0 and u % 4 == 3:
                            keep(u)
                    for b in range(B):
                        dve.wait_ge(weighed, g * 4 * B + 3 * B + b + 1)
                        out = oT[:, bass.ds(g, 1), b * T:(b + 1) * T].rearrange("p j n -> p (j n)")
                        nc.vector.tensor_scalar(out, k.bank[6 + b][:], 1.0, None, ALU.mult).then_inc(o_kept, 1)

                dve.wait_ge(x_biased, NT)
                for t in range(NT):
                    dve.wait_ge(done, t + 1)
                    nc.vector.tensor_tensor(k.x[:, t], k.x[:, t], k.bank[t % 4][:, 0:D], ALU.add).then_inc(added, 1)


def build(nc, d, out, layers="ABCD"):
    with ExitStack() as ctx:
        k = Core(nc, ctx, d)
        stored = k.sem("stored")
        with nc.Block() as block:
            @block.sync
            def _(sp):
                x_in = d["hidden_states"].rearrange("b (c p) n -> p (b c) n", p=P)
                sp.dma_start(k.x[:], x_in).then_inc(k.io_in, 16)
                sp.dma_start(k.eye[:], d["c_eye"]).then_inc(k.io_in, 16)
                sp.wait_ge(k.io_in, 32)
        if "A" in layers:
            kept = len(k.sems)
            slot_attention(k)
            k.free_sems(kept)
        if "B" in layers:
            expert_block(k, 0)
        if "C" in layers:
            full_attention(k)
        if "D" in layers:
            expert_block(k, 1)
        with nc.Block() as block:
            @block.sync
            def _(sp):
                sp.dma_start(out.rearrange("b (c p) n -> p (b c) n", p=P), k.x[:]).then_inc(stored, 16)
                sp.wait_ge(stored, 16)


def kernel(**inputs):
    import concourse.bacc as _bacc
    from concourse.bass_utils import run_bass_kernel_spmd as _run

    names = {}
    for name, a in inputs.items():
        for long, short in (("L0_attn_a_", ""), ("L0_attn_b_", "b_"), ("L0_ffn_", "f_")):
            if name.startswith(long):
                names[short + name[len(long):]] = np.ascontiguousarray(np.asarray(a))
    held = {**lay_out(names), **constants()}
    nc = _bacc.Bacc("TRN2", target_bir_lowering=False, num_devices=1)
    d = {n: nc.dram_tensor(f"in_{n}_dram", a.shape, mybir.dt.from_np(a.dtype), kind="ExternalInput").ap() for n, a in held.items()}
    out = nc.dram_tensor("out_0_dram", (B, T, D), F32, kind="ExternalOutput").ap()
    build(nc, d, out)
    r = _run(nc, [{f"in_{n}_dram": a for n, a in held.items()}], core_ids=[0])
    return r.results[0]["out_0_dram"]
```
